# Optimizing a Trainium2 kernel written in Bass

```python
import numpy as np
import jax
import jax.numpy as jnp

def _softmax(x, axis=-1):
    return jax.nn.softmax(x, axis=axis)
def _gelu(x):
    return jax.nn.gelu(x, approximate=True)
def _silu(x):
    return jax.nn.silu(x)
def _sigmoid(x):
    return jax.nn.sigmoid(x)
def _layernorm(x, axis=-1, eps=1e-5):
    m = jnp.mean(x, axis=axis, keepdims=True)
    v = jnp.var(x, axis=axis, keepdims=True)
    return (x - m) / jnp.sqrt(v + eps)
def _scatter_add(tgt, idx, src, axis=0):
    return tgt.at[idx].add(src)
def _segment_sum(src, seg, n):
    return jax.ops.segment_sum(src, seg, n)

kernel_name = 'mk_conv_seq_d4_conv_nhwc256_ffa9a0'

def setup_inputs(seed: int = 0):
    np.random.seed(seed)
    _w = jnp.asarray
    def _rec_inputs():
        import jax
        import jax.numpy as jnp
        _gk = jax.random.key(seed)
        x = -0.0005207 + 1.001 * jax.random.normal(jax.random.fold_in(_gk, 1), (2, 64, 64, 256), jnp.float32)
        return x
    x = _rec_inputs()
    def _L0_conv_setup():
        import jax, jax.numpy as jnp
        import numpy as np
        EPS = 1e-05

        def _layer_norm(x, g, b):
            m = jnp.mean(x, axis=-1, keepdims=True)
            v = jnp.var(x, axis=-1, keepdims=True)
            return (x - m) * jax.lax.rsqrt(v + EPS) * g + b
        key = jax.random.key(seed)
        ks = jax.random.split(key, 16)
        B, N, E, H = (2, 64, 256, 8)
        F = 2 * E
        s = 1.0 / np.sqrt(E)
        return {'x_in': jax.random.normal(ks[0], (B, N, N, E), jnp.float32), 'Wq': jax.random.normal(ks[1], (E, E), jnp.float32) * s, 'Wk': jax.random.normal(ks[2], (E, E), jnp.float32) * s, 'Wv1': jax.random.normal(ks[3], (E, E), jnp.float32) * s, 'Wv2': jax.random.normal(ks[4], (E, E), jnp.float32) * s, 'Wo': jax.random.normal(ks[5], (E, E), jnp.float32) * s, 'ln_agg_g': jnp.ones((E,), jnp.float32), 'ln_agg_b': jnp.zeros((E,), jnp.float32), 'W1': jax.random.normal(ks[6], (E, F), jnp.float32) * s, 'b1': jnp.zeros((F,), jnp.float32), 'W2': jax.random.normal(ks[7], (F, E), jnp.float32) * (1.0 / np.sqrt(F)), 'b2': jnp.zeros((E,), jnp.float32), 'ln_out_g': jnp.ones((E,), jnp.float32), 'ln_out_b': jnp.zeros((E,), jnp.float32)}
    _L0_conv_all = _L0_conv_setup()
    _L0_conv_in = {k: v for k, v in _L0_conv_all.items() if k in ('Wq', 'Wk', 'Wv1', 'Wv2', 'Wo', 'ln_agg_g', 'ln_agg_b', 'W1', 'b1', 'W2', 'b2', 'ln_out_g', 'ln_out_b', )}
    del _L0_conv_all

    def _L1_conv_setup():
        import jax, jax.numpy as jnp
        import numpy as np
        LN_EPS = 0.001
        key = jax.random.key(seed)
        ks = jax.random.split(key, 6)
        B, H, W, C = (8, 64, 64, 256)
        s = 1.0 / np.sqrt(C)
        return {'x': jax.random.normal(ks[0], (B, H, W, C), dtype=jnp.float32), 'ln_gamma': jnp.ones((C,), jnp.float32), 'ln_beta': jnp.zeros((C,), jnp.float32), 'w_q': jax.random.normal(ks[1], (C, C), jnp.float32) * s, 'b_q': jnp.zeros((C,), jnp.float32), 'w_k': jax.random.normal(ks[2], (C, C), jnp.float32) * s, 'b_k': jnp.zeros((C,), jnp.float32), 'w_v': jax.random.normal(ks[3], (C, C), jnp.float32) * s, 'b_v': jnp.zeros((C,), jnp.float32), 'w_p': jax.random.normal(ks[4], (C, C), jnp.float32) * s, 'b_p': jnp.zeros((C,), jnp.float32)}
    _L1_conv_all = _L1_conv_setup()
    _L1_conv_in = {k: v for k, v in _L1_conv_all.items() if k in ('ln_gamma', 'ln_beta', 'w_q', 'b_q', 'w_k', 'b_k', 'w_v', 'b_v', 'w_p', 'b_p', )}
    del _L1_conv_all

    def _L2_conv_setup():
        import jax, jax.numpy as jnp
        import numpy as np
        EPS = 1e-05

        def _layer_norm(x, g, b):
            m = jnp.mean(x, axis=-1, keepdims=True)
            v = jnp.var(x, axis=-1, keepdims=True)
            return (x - m) * jax.lax.rsqrt(v + EPS) * g + b
        key = jax.random.key(seed)
        ks = jax.random.split(key, 16)
        B, N, E, H = (2, 64, 256, 8)
        F = 2 * E
        s = 1.0 / np.sqrt(E)
        return {'x_in': jax.random.normal(ks[0], (B, N, N, E), jnp.float32), 'Wq': jax.random.normal(ks[1], (E, E), jnp.float32) * s, 'Wk': jax.random.normal(ks[2], (E, E), jnp.float32) * s, 'Wv1': jax.random.normal(ks[3], (E, E), jnp.float32) * s, 'Wv2': jax.random.normal(ks[4], (E, E), jnp.float32) * s, 'Wo': jax.random.normal(ks[5], (E, E), jnp.float32) * s, 'ln_agg_g': jnp.ones((E,), jnp.float32), 'ln_agg_b': jnp.zeros((E,), jnp.float32), 'W1': jax.random.normal(ks[6], (E, F), jnp.float32) * s, 'b1': jnp.zeros((F,), jnp.float32), 'W2': jax.random.normal(ks[7], (F, E), jnp.float32) * (1.0 / np.sqrt(F)), 'b2': jnp.zeros((E,), jnp.float32), 'ln_out_g': jnp.ones((E,), jnp.float32), 'ln_out_b': jnp.zeros((E,), jnp.float32)}
    _L2_conv_all = _L2_conv_setup()
    _L2_conv_in = {k: v for k, v in _L2_conv_all.items() if k in ('Wq', 'Wk', 'Wv1', 'Wv2', 'Wo', 'ln_agg_g', 'ln_agg_b', 'W1', 'b1', 'W2', 'b2', 'ln_out_g', 'ln_out_b', )}
    del _L2_conv_all

    def _L3_conv_setup():
        import jax, jax.numpy as jnp
        import numpy as np
        N = 3
        B, R, C, CH = (32, 56, 56, 256)
        key = jax.random.key(seed)
        k1, k2 = jax.random.split(key)
        x = jax.random.normal(k1, (B, R, C, CH), dtype=jnp.float32)
        kernel = jax.random.normal(k2, (N, N, CH), dtype=jnp.float32) * 0.1
        return {'x': x, 'kernel': kernel}
    _L3_conv_all = _L3_conv_setup()
    _L3_conv_in = {k: v for k, v in _L3_conv_all.items() if k in ('kernel', )}
    del _L3_conv_all

    return {
        "x": x,
        "L0_conv_Wq": _L0_conv_in["Wq"],
        "L0_conv_Wk": _L0_conv_in["Wk"],
        "L0_conv_Wv1": _L0_conv_in["Wv1"],
        "L0_conv_Wv2": _L0_conv_in["Wv2"],
        "L0_conv_Wo": _L0_conv_in["Wo"],
        "L0_conv_ln_agg_g": _L0_conv_in["ln_agg_g"],
        "L0_conv_ln_agg_b": _L0_conv_in["ln_agg_b"],
        "L0_conv_W1": _L0_conv_in["W1"],
        "L0_conv_b1": _L0_conv_in["b1"],
        "L0_conv_W2": _L0_conv_in["W2"],
        "L0_conv_b2": _L0_conv_in["b2"],
        "L0_conv_ln_out_g": _L0_conv_in["ln_out_g"],
        "L0_conv_ln_out_b": _L0_conv_in["ln_out_b"],
        "L1_conv_ln_gamma": _L1_conv_in["ln_gamma"],
        "L1_conv_ln_beta": _L1_conv_in["ln_beta"],
        "L1_conv_w_q": _L1_conv_in["w_q"],
        "L1_conv_b_q": _L1_conv_in["b_q"],
        "L1_conv_w_k": _L1_conv_in["w_k"],
        "L1_conv_b_k": _L1_conv_in["b_k"],
        "L1_conv_w_v": _L1_conv_in["w_v"],
        "L1_conv_b_v": _L1_conv_in["b_v"],
        "L1_conv_w_p": _L1_conv_in["w_p"],
        "L1_conv_b_p": _L1_conv_in["b_p"],
        "L2_conv_Wq": _L2_conv_in["Wq"],
        "L2_conv_Wk": _L2_conv_in["Wk"],
        "L2_conv_Wv1": _L2_conv_in["Wv1"],
        "L2_conv_Wv2": _L2_conv_in["Wv2"],
        "L2_conv_Wo": _L2_conv_in["Wo"],
        "L2_conv_ln_agg_g": _L2_conv_in["ln_agg_g"],
        "L2_conv_ln_agg_b": _L2_conv_in["ln_agg_b"],
        "L2_conv_W1": _L2_conv_in["W1"],
        "L2_conv_b1": _L2_conv_in["b1"],
        "L2_conv_W2": _L2_conv_in["W2"],
        "L2_conv_b2": _L2_conv_in["b2"],
        "L2_conv_ln_out_g": _L2_conv_in["ln_out_g"],
        "L2_conv_ln_out_b": _L2_conv_in["ln_out_b"],
        "L3_conv_kernel": _L3_conv_in["kernel"],
    }

def reference(x, L0_conv_Wq, L0_conv_Wk, L0_conv_Wv1, L0_conv_Wv2, L0_conv_Wo, L0_conv_ln_agg_g, L0_conv_ln_agg_b, L0_conv_W1, L0_conv_b1, L0_conv_W2, L0_conv_b2, L0_conv_ln_out_g, L0_conv_ln_out_b, L1_conv_ln_gamma, L1_conv_ln_beta, L1_conv_w_q, L1_conv_b_q, L1_conv_w_k, L1_conv_b_k, L1_conv_w_v, L1_conv_b_v, L1_conv_w_p, L1_conv_b_p, L2_conv_Wq, L2_conv_Wk, L2_conv_Wv1, L2_conv_Wv2, L2_conv_Wo, L2_conv_ln_agg_g, L2_conv_ln_agg_b, L2_conv_W1, L2_conv_b1, L2_conv_W2, L2_conv_b2, L2_conv_ln_out_g, L2_conv_ln_out_b, L3_conv_kernel):
    import jax
    import jax.numpy as jnp
    def _L0_conv_ref(x_in, Wq, Wk, Wv1, Wv2, Wo, ln_agg_g, ln_agg_b, W1, b1, W2, b2, ln_out_g, ln_out_b):
        import jax, jax.numpy as jnp
        import numpy as np
        EPS = 1e-05

        def _layer_norm(x, g, b):
            m = jnp.mean(x, axis=-1, keepdims=True)
            v = jnp.var(x, axis=-1, keepdims=True)
            return (x - m) * jax.lax.rsqrt(v + EPS) * g + b
        B, N, _, E = x_in.shape
        H = 8
        d_k = E // H
        q = (x_in @ Wq).reshape(B, N, N, H, d_k)
        k = (x_in @ Wk).reshape(B, N, N, H, d_k)
        v1 = (x_in @ Wv1).reshape(B, N, N, H, d_k)
        v2 = (x_in @ Wv2).reshape(B, N, N, H, d_k)
        scores = jnp.einsum('bilhd,bljhd->biljh', q, k) / np.sqrt(d_k)
        att = jax.nn.softmax(scores, axis=2)
        out = jnp.einsum('biljh,bilhd,bljhd->bijhd', att, v1, v2)
        attn_out = out.reshape(B, N, N, E) @ Wo
        h = x_in + attn_out
        h = _layer_norm(h, ln_agg_g, ln_agg_b)
        mlp = jax.nn.relu(h @ W1 + b1) @ W2 + b2
        h = mlp + h
        return _layer_norm(h, ln_out_g, ln_out_b)

    def _L1_conv_ref(x, ln_gamma, ln_beta, w_q, b_q, w_k, b_k, w_v, b_v, w_p, b_p):
        import jax, jax.numpy as jnp
        import numpy as np
        LN_EPS = 0.001
        B, H, W, C = x.shape
        units = w_q.shape[1]
        scale = jnp.asarray(units, x.dtype) ** (-0.5)
        mean = jnp.mean(x, axis=-1, keepdims=True)
        var = jnp.mean(jnp.square(x - mean), axis=-1, keepdims=True)
        xn = (x - mean) * jax.lax.rsqrt(var + LN_EPS) * ln_gamma + ln_beta
        xf = xn.reshape(B, H * W, C)
        q = xf @ w_q + b_q
        k = xf @ w_k + b_k
        v = xf @ w_v + b_v
        scores = jnp.einsum('bnc,bmc->bnm', q, k) * scale
        attn = jax.nn.softmax(scores, axis=-1)
        out = jnp.einsum('bnm,bmc->bnc', attn, v)
        proj = (out @ w_p + b_p).reshape(B, H, W, units)
        return xn + proj

    def _L2_conv_ref(x_in, Wq, Wk, Wv1, Wv2, Wo, ln_agg_g, ln_agg_b, W1, b1, W2, b2, ln_out_g, ln_out_b):
        import jax, jax.numpy as jnp
        import numpy as np
        EPS = 1e-05

        def _layer_norm(x, g, b):
            m = jnp.mean(x, axis=-1, keepdims=True)
            v = jnp.var(x, axis=-1, keepdims=True)
            return (x - m) * jax.lax.rsqrt(v + EPS) * g + b
        B, N, _, E = x_in.shape
        H = 8
        d_k = E // H
        q = (x_in @ Wq).reshape(B, N, N, H, d_k)
        k = (x_in @ Wk).reshape(B, N, N, H, d_k)
        v1 = (x_in @ Wv1).reshape(B, N, N, H, d_k)
        v2 = (x_in @ Wv2).reshape(B, N, N, H, d_k)
        scores = jnp.einsum('bilhd,bljhd->biljh', q, k) / np.sqrt(d_k)
        att = jax.nn.softmax(scores, axis=2)
        out = jnp.einsum('biljh,bilhd,bljhd->bijhd', att, v1, v2)
        attn_out = out.reshape(B, N, N, E) @ Wo
        h = x_in + attn_out
        h = _layer_norm(h, ln_agg_g, ln_agg_b)
        mlp = jax.nn.relu(h @ W1 + b1) @ W2 + b2
        h = mlp + h
        return _layer_norm(h, ln_out_g, ln_out_b)

    def _L3_conv_ref(x, kernel):
        import jax, jax.numpy as jnp
        import numpy as np
        N = 3
        B, R, C, CH = (32, 56, 56, 256)
        n = kernel.shape[0]
        ch = kernel.shape[2]
        mask = jnp.ones((n, n, 1), dtype=kernel.dtype).at[n // 2, n // 2, 0].set(0.0)
        k = kernel * mask
        k_hwio = k[:, :, None, :]
        out = jax.lax.conv_general_dilated(x, k_hwio, window_strides=(1, 1), padding='SAME', dimension_numbers=('NHWC', 'HWIO', 'NHWC'), feature_group_count=ch)
        return out + x

    def _gn(v, G=32, eps=1e-5):
        B_, H_, W_, C_ = v.shape
        g = v.reshape(B_, H_, W_, G, C_ // G)
        m = jnp.mean(g, axis=(1, 2, 4), keepdims=True)
        s = jnp.var(g, axis=(1, 2, 4), keepdims=True)
        return ((g - m) / jnp.sqrt(s + eps)).reshape(v.shape)

    def _ln_c(v, eps=1e-6):
        m = jnp.mean(v, axis=-1, keepdims=True)
        s = jnp.var(v, axis=-1, keepdims=True)
        return (v - m) / jnp.sqrt(s + eps)

    def _ln_t(v, eps=1e-5):
        m = jnp.mean(v, axis=-1, keepdims=True)
        s = jnp.var(v, axis=-1, keepdims=True)
        return (v - m) / jnp.sqrt(s + eps)

    def _to_tokens(v):
        B_, H_, W_, C_ = v.shape
        return v.reshape(B_, H_ * W_, C_)
    def _from_tokens(t, like):
        return t.reshape(like.shape)

    x = _L0_conv_ref(x, L0_conv_Wq, L0_conv_Wk, L0_conv_Wv1, L0_conv_Wv2, L0_conv_Wo, L0_conv_ln_agg_g, L0_conv_ln_agg_b, L0_conv_W1, L0_conv_b1, L0_conv_W2, L0_conv_b2, L0_conv_ln_out_g, L0_conv_ln_out_b)
    x = _L1_conv_ref(x, L1_conv_ln_gamma, L1_conv_ln_beta, L1_conv_w_q, L1_conv_b_q, L1_conv_w_k, L1_conv_b_k, L1_conv_w_v, L1_conv_b_v, L1_conv_w_p, L1_conv_b_p)
    x = _L2_conv_ref(x, L2_conv_Wq, L2_conv_Wk, L2_conv_Wv1, L2_conv_Wv2, L2_conv_Wo, L2_conv_ln_agg_g, L2_conv_ln_agg_b, L2_conv_W1, L2_conv_b1, L2_conv_W2, L2_conv_b2, L2_conv_ln_out_g, L2_conv_ln_out_b)
    x = _L3_conv_ref(x, L3_conv_kernel)
    return x


_drawn_inputs = setup_inputs


def setup_inputs(seed=0):
    import zlib

    import numpy as np

    out = dict(_drawn_inputs(seed))
    spreads = {'L0_conv_ln_agg_g': (1.0, 0.2),
     'L0_conv_ln_agg_b': (0.0, 0.1),
     'L0_conv_b1': (0.0, 0.1),
     'L0_conv_b2': (0.0, 0.1),
     'L0_conv_ln_out_g': (1.0, 0.2),
     'L0_conv_ln_out_b': (0.0, 0.1),
     'L1_conv_ln_gamma': (1.0, 0.2),
     'L1_conv_ln_beta': (0.0, 0.1),
     'L1_conv_b_q': (0.0, 0.8),
     'L1_conv_b_k': (0.0, 0.8),
     'L1_conv_b_v': (0.0, 0.1),
     'L1_conv_b_p': (0.0, 0.1),
     'L2_conv_ln_agg_g': (1.0, 0.2),
     'L2_conv_ln_agg_b': (0.0, 0.1),
     'L2_conv_b1': (0.0, 0.1),
     'L2_conv_b2': (0.0, 0.1),
     'L2_conv_ln_out_g': (1.0, 0.2),
     'L2_conv_ln_out_b': (0.0, 0.1)}
    factors = {}
    for name, (base, spread) in spreads.items():
        noise = np.random.default_rng([zlib.crc32(name.encode()), seed]).standard_normal(out[name].shape)
        drawn = base * np.exp(spread * noise) if base else spread * noise
        out[name] = jnp.asarray(drawn.astype(out[name].dtype))
    for name, factor in factors.items():
        out[name] = (out[name] * factor).astype(out[name].dtype)
    return out
```

```python
from contextlib import ExitStack

import numpy as np

import concourse.bass as bass
from concourse import mybir

F32 = mybir.dt.float32
ALU = mybir.AluOpType
ACT = mybir.ActivationFunctionType
AX_X = mybir.AxisListType.X

P = 128
B, N, E, H = 2, 64, 256, 8
D = E // H
KC = E // P
F = 2 * E
FC = F // P
R = P // D
BANK = 512
PAIRS = N // 2
GROUPS = N // 4
EPS_TRI = 1e-5
EPS_GLOBAL = 1e-3
TOK = N * N
KT = TOK // P
CHUNK = TOK // BANK


class Step:

    def __init__(self, half, odd):
        self.half, self.odd = half, odd

    def __add__(self, k):
        return Step(self.half, self.odd + k)

    def __sub__(self, k):
        return self + -k

    @property
    def slot(self):
        return self.odd % 2

    @property
    def pair(self):
        return self.half + self.odd // 2

    @property
    def number(self):
        return self.half * 2 + self.odd


CREDIT = 32


def after(step, per=1, nth=None):
    return step.number * per + (per if nth is None else nth) + CREDIT


def slot_after(step, dmas=1):
    return (step.pair + 1) * (16 * dmas) + CREDIT


def credit(nc, sems):
    with nc.Block() as block:
        @block.gpsimd
        def _(pool):
            for sem in sems:
                pool.sem_inc(sem, CREDIT)


def clear(nc, sems):
    with nc.Block() as block:
        @block.gpsimd
        def _(pool):
            for sem in sems:
                pool.sem_clear(sem)


def settle(eng, sem):
    eng.sem_inc(sem, 1)


def inverse_root(eng, lib, variance, root, to, tmp, sem, step):
    lib.reciprocal(to, root).then_inc(sem, 1)
    eng.wait_ge(sem, after(step, 5, 1))
    lib.tensor_tensor(tmp, to, to, ALU.mult).then_inc(sem, 1)
    eng.wait_ge(sem, after(step, 5, 2))
    lib.tensor_tensor(tmp, tmp, variance, ALU.mult).then_inc(sem, 1)
    eng.wait_ge(sem, after(step, 5, 3))
    lib.tensor_scalar(tmp, tmp, -0.5, 1.5, ALU.mult, ALU.add).then_inc(sem, 1)
    eng.wait_ge(sem, after(step, 5, 4))
    lib.tensor_tensor(to, to, tmp, ALU.mult).then_inc(sem, 1)
    eng.wait_ge(sem, after(step, 5))


def triangle_layer(nc, consts, x, w, out, name):
    with ExitStack() as ctx:
        def sb(what, shape):
            return ctx.enter_context(nc.sbuf_tensor(f"{name}_{what}", shape, F32))

        def sem(what):
            return ctx.enter_context(nc.semaphore(f"{name}_{what}"))

        psum = ctx.enter_context(nc.psum_tensor(f"{name}_psum", [P, 8, BANK], F32))
        ident, pick, ones_row = consts["ident"], consts["pick"], consts["ones_row"]
        eye = ident[:, P:2 * P]

        wq, wk, wv1, wv2, wo = (sb(k, [P, KC, E]) for k in ("wq", "wk", "wv1", "wv2", "wo"))
        w1, w2 = sb("w1", [P, KC, F]), sb("w2", [P, FC, E])
        agg_g, agg_b, b1 = sb("agg_g", [P, KC]), sb("agg_b", [P, KC]), sb("b1", [P, FC])
        out_g, out_b, b2 = sb("out_g", [P, E]), sb("out_b", [P, E]), sb("b2", [1, E])
        v2 = sb("v2", [P, N, E])
        scores = sb("scores", [P, R * N, N])
        scores_i = scores[:, :, :].rearrange("p (r i) l -> p r i l", r=R)

        work = sb("work", [P, 14080])
        at = [0]

        def part(n):
            at[0] += n
            return work[:, at[0] - n:at[0]]

        x_row = [part(2 * E).rearrange("p (t c) -> p t c", t=2) for _ in range(2)]
        x_col = [part(2 * E).rearrange("p (t c) -> p t c", t=2) for _ in range(2)]
        rowT = part(KC * 2 * P).rearrange("p (k n) -> p k n", k=KC)
        colT = [part(KC * 4 * P).rearrange("p (k j n) -> p k j n", k=KC, j=4) for _ in range(2)]
        kT = [part(2 * 2 * P).rearrange("p (t n) -> p t n", t=2) for _ in range(2)]
        q_diag = [part(2 * 4 * R * N).rearrange("p (t l r i) -> p t l r i", t=2, l=4, r=R)
                  for _ in range(2)]
        q_diag_all = work[:, at[0] - 4 * 4 * R * N:at[0]]
        at[0] = 0
        prod_d = [part(8 * E) for _ in range(2)]
        prod_p = [part(8 * E) for _ in range(2)]
        probs = part(2 * R * N)
        a_sb = [part(BANK) for _ in range(2)]
        v1_sb = [part(E) for _ in range(2)]
        x_pair = [part(E) for _ in range(2)]
        x_res = [part(E) for _ in range(2)]
        x_pairT, o_sb, oT, h0, hn, hT, on = (part(E) for _ in range(7))
        reluT = part(F)
        o_out = [part(E) for _ in range(2)]
        small = sb("small", [P, 64])
        neg_max = [small[:, 8 * k:8 * k + 8] for k in range(2)]
        sums = [small[:, 16 + 8 * k:24 + 8 * k] for k in range(2)]
        row_max, inv = small[:, 32:40], small[:, 40:48]
        stats, mv1, mv2 = small[:, 48:54], small[:, 54:56], small[:, 56:58]
        rstd, root, tmp = small[:, 58:59], small[:, 59:60], small[:, 60:61]
        variance = small[:, 61:62]

        x_toks = x.rearrange("b (s i) j c -> b s (i j) c", i=2)
        x_cols = x.rearrange("b r (s j) c -> b s j r c", j=2)
        x_grid = x.rearrange("b (s i) (t g) c -> b s g t i c", i=2, g=4)
        out_grid = out.rearrange("b (s i) (t g) c -> b s g t i c", i=2, g=4)

        weights_in = sem("weights_in")
        with nc.Block() as block:
            @block.sync
            def _(sp):
                n = 0
                for dst, src in ((wq, w["Wq"]), (wk, w["Wk"]), (wv1, w["Wv1"]), (wv2, w["Wv2"]),
                                 (wo, w["Wo"]), (w1, w["W1"]), (w2, w["W2"])):
                    sp.dma_start(dst[:, :, :], src.rearrange("(k p) n -> p k n", p=P)).then_inc(weights_in, 16)
                    n += 1
                for dst, src in ((agg_g, w["ln_agg_g"]), (agg_b, w["ln_agg_b"]), (b1, w["b1"])):
                    sp.dma_start(dst[:, :], src.rearrange("(k p) -> p k", p=P), allow_slow_non_contiguous=True).then_inc(weights_in, 16)
                    n += 1
                for dst, src in ((out_g, w["ln_out_g"]), (out_b, w["ln_out_b"])):
                    sp.dma_start(dst[:, :], src.rearrange("(a n) -> a n", a=1).to_broadcast([P, E])).then_inc(weights_in, 16)
                    n += 1
                sp.dma_start(b2[:, :], w["b2"].rearrange("(a n) -> a n", a=1)).then_inc(weights_in, 16)
                sp.wait_ge(weights_in, 16 * (n + 1))

        names = ("rows_in0", "rows_in1", "cols_in0", "cols_in1", "diag_zero", "xT_mm", "rowT_copy",
                 "colT_copy", "v2_mm", "v2_copy", "qk_mm", "kT_copy", "q0_copy", "q1_copy",
                 "scores_mm", "scores_copy",
                 "pair_in0", "pair_in1", "res_in0", "res_in1", "pairT_mm", "pairT_copy", "v1_mm",
                 "v1_copy", "max_raw", "max_ready", "exp_ready", "inv_ready", "probs_ready", "a_mm",
                 "a_copy", "d_first", "d_ready", "p_first", "p_ready", "unit_mm", "o_copy", "oT_mm",
                 "oT_copy", "wo_mm", "h0_ready", "stats1", "mean1", "var1", "root1", "rstd1", "hn_ready",
                 "hT_mm", "hT_copy", "w1_mm", "relu_ready", "w2_mm", "stats2", "mean2", "var2",
                 "root2", "rstd2", "on_ready", "scaled", "out_ready", "out_stored0", "out_stored1",
                 "settled", "sp_settled")
        s = {k: sem(k) for k in names}
        credit(nc, s.values())
        rows_in, cols_in = (s["rows_in0"], s["rows_in1"]), (s["cols_in0"], s["cols_in1"])
        pair_in, res_in = (s["pair_in0"], s["pair_in1"]), (s["res_in0"], s["res_in1"])
        out_stored = (s["out_stored0"], s["out_stored1"])

        with nc.Fori(0, B) as b:
            def group_steps(eng, body):
                half = b * (GROUPS // 2)
                body(Step(half, -1), None)
                with eng.Fori(0, GROUPS // 2 - 1) as i:
                    for u in range(2):
                        body(Step(half + i, u), (i, u))
                for g in (GROUPS - 2, GROUPS - 1):
                    body(Step(half, g), (0, g))

            with nc.Block() as block:
                t_bank, qk_bank = (0, 1), (2, 3)
                v2_psum = psum[:, 4:6, :].rearrange("p a n -> p (a n)")
                s_psum = psum[:, 6:8, :].rearrange("p a n -> p (a n)")

                @block.sync
                def _(sp):
                    def load(g, i):
                        sp.wait_ge(s["xT_mm"], after(g - 2))
                        for t in range(2):
                            sp.dma_start(x_row[g.slot][:, t, :],
                                         x_toks[bass.ds(b, 1), bass.ds(i * 2 + t, 1)].rearrange("a s p c -> p (a s c)")
                                         ).then_inc(rows_in[g.slot], 16)
                            for j in range(2):
                                sp.dma_start(x_col[g.slot][N * j:N * j + N, t, :],
                                             x_cols[bass.ds(b, 1), bass.ds(i * 2 + t, 1), j].rearrange("a s r c -> r (a s c)")
                                             ).then_inc(cols_in[g.slot], 16)

                    half = b * (GROUPS // 2)
                    for g in range(2):
                        load(Step(half, g), g)
                    with sp.Fori(0, GROUPS // 2 - 1) as i:
                        for u in range(2):
                            load(Step(half + i, 2 + u), i * 2 + 2 + u)

                @block.gpsimd
                def _(pool):
                    nc.gpsimd.memset(q_diag_all, 0.0).then_inc(s["diag_zero"], 1)

                @block.tensor
                def _(pe):
                    def body(g, where):
                        nxt = g + 1
                        if where is None or g.odd < GROUPS - 1:
                            pe.wait_ge(rows_in[nxt.slot], slot_after(nxt, 2))
                            pe.wait_ge(cols_in[nxt.slot], slot_after(nxt, 4))
                            pe.wait_ge(s["rowT_copy"], after(nxt - 1))
                            pe.wait_ge(s["colT_copy"], after(nxt - 1))
                            for bank, src in ((t_bank[0], x_row[nxt.slot]), (t_bank[1], x_col[nxt.slot])):
                                for k in range(KC):
                                    for t in range(2):
                                        c = (k * 2 + t) * P
                                        mm = nc.tensor.transpose(psum[:, bank, c:c + P], src[:, t, k * P:k * P + P], eye)
                            mm.then_inc(s["xT_mm"], 1)
                        if where is not None:
                            pe.wait_ge(s["v2_copy"], after(g - 1))
                            for j in range(4):
                                for k in range(KC):
                                    mm = nc.tensor.matmul(v2_psum[:, j * E:j * E + E], colT[g.slot][:, k, j, :],
                                                          wv2[:, k, :], start=(k == 0), stop=(k == KC - 1))
                            mm.then_inc(s["v2_mm"], 1)
                        if where is None or g.odd < GROUPS - 1:
                            pe.wait_ge(s["rowT_copy"], after(nxt))
                            pe.wait_ge(s["colT_copy"], after(nxt))
                            pe.wait_ge(s["kT_copy"], after(nxt - 1))
                            pe.wait_ge(s["q0_copy"], after(nxt - 1))
                            pe.wait_ge(s["q1_copy"], after(nxt - 1))
                            for bank, wt, src in ((qk_bank[0], wq, colT[nxt.slot][:, :, :, 0:N]),
                                                  (qk_bank[1], wk, rowT[:, :, :])):
                                for t in range(2):
                                    for k in range(KC):
                                        mm = nc.tensor.matmul(psum[:, bank, t * 2 * P:(t + 1) * 2 * P],
                                                              wt[:, k, t * P:t * P + P], src[:, k],
                                                              start=(k == 0), stop=(k == KC - 1))
                            mm.then_inc(s["qk_mm"], 1)
                        if where is not None:
                            pe.wait_ge(s["kT_copy"], after(g))
                            pe.wait_ge(s["q0_copy"], after(g))
                            pe.wait_ge(s["q1_copy"], after(g))
                            pe.wait_ge(s["scores_copy"], after(g - 1))
                            for l in range(4):
                                for t in range(2):
                                    mm = nc.tensor.matmul(s_psum[N * t:N * t + N, l * R * N:(l + 1) * R * N],
                                                          kT[g.slot][:, t, l * N:l * N + N],
                                                          q_diag[g.slot][:, t, l].rearrange("p r i -> p (r i)"),
                                                          start=True, stop=True)
                            mm.then_inc(s["scores_mm"], 1)

                    group_steps(pe, body)

                @block.scalar
                def _(act):
                    def body(g, where):
                        nxt = g + 1
                        if where is None or g.odd < GROUPS - 1:
                            act.wait_ge(s["xT_mm"], after(nxt))
                            act.wait_ge(s["qk_mm"], after(nxt - 1))
                            nc.scalar.activation(rowT[:, :, :], psum[:, t_bank[0], :].rearrange("p (k n) -> p k n", k=KC),
                                                 ACT.Copy).then_inc(s["rowT_copy"], 1)
                        if where is not None:
                            i, u = where
                            act.wait_ge(s["v2_mm"], after(g))
                            nc.scalar.activation(v2[:, bass.ds((i * 2 + u) * 4, 4), :].rearrange("p j n -> p (j n)"),
                                                 v2_psum, ACT.Copy).then_inc(s["v2_copy"], 1)
                        if where is None or g.odd < GROUPS - 1:
                            act.wait_ge(s["qk_mm"], after(nxt))
                            act.wait_ge(s["scores_mm"], after(nxt - 2))
                            nc.scalar.activation(kT[nxt.slot][:, :, :],
                                                 psum[:, qk_bank[1], :].rearrange("p (t n) -> p t n", t=2),
                                                 ACT.Copy).then_inc(s["kT_copy"], 1)
                            if where is None:
                                act.wait_ge(s["diag_zero"], b + 1 + CREDIT)
                            for r in range(2):
                                ins = q_copy(nc.scalar, nxt, r)
                            ins.then_inc(s["q0_copy"], 1)

                    def q_copy(eng, g, r):
                        rows = slice(D * r, D * r + D)
                        return eng.activation(q_diag[g.slot][rows, :, :, r, :],
                                              psum[rows, qk_bank[0], :].rearrange("p (t l i) -> p t l i", t=2, l=4),
                                              ACT.Copy)

                    group_steps(act, body)

                @block.vector
                def _(dve):
                    def body(g, where):
                        nxt = g + 1
                        if where is None or g.odd < GROUPS - 1:
                            dve.wait_ge(s["xT_mm"], after(nxt))
                            dve.wait_ge(s["v2_mm"], after(nxt - 2))
                            for k in range(KC):
                                src = psum[:, t_bank[1], k * 4 * N:(k + 1) * 4 * N].rearrange("p (j n) -> p j n", j=4)
                                ins = nc.vector.tensor_copy(colT[nxt.slot][:, k].rearrange("p j (a n) -> p j a n", a=2),
                                                            src.unsqueeze(2).to_broadcast([P, 4, 2, N]))
                            ins.then_inc(s["colT_copy"], 1)
                            dve.wait_ge(s["qk_mm"], after(nxt))
                            dve.wait_ge(s["kT_copy"], after(nxt))
                            if where is None:
                                dve.wait_ge(s["diag_zero"], b + 1 + CREDIT)
                            dve.wait_ge(s["q0_copy"], after(nxt))
                            for r in range(2, R):
                                rows = slice(D * r, D * r + D)
                                ins = nc.vector.tensor_copy(q_diag[nxt.slot][rows, :, :, r, :],
                                                            psum[rows, qk_bank[0], :].rearrange("p (t l i) -> p t l i", t=2, l=4))
                            ins.then_inc(s["q1_copy"], 1)
                        if where is not None:
                            i, u = where
                            dve.wait_ge(s["scores_mm"], after(g))
                            nc.vector.tensor_copy(scores[:, :, bass.ds((i * 2 + u) * 4, 4)],
                                                  s_psum.rearrange("p (l n) -> p n l", l=4)
                                                  ).then_inc(s["scores_copy"], 1)

                    group_steps(dve, body)

            UNITS = "DPDDPDDP"
            ND, NPL = UNITS.count("D"), UNITS.count("P")
            D_UNIT = [u for u, e in enumerate(UNITS) if e == "D"]
            P_UNIT = [u for u, e in enumerate(UNITS) if e == "P"]
            JU = N // len(UNITS)
            A, V1, O, X, Z = (0, 1), (2, 3), (4, 5), 6, 7
            HALF = PAIRS // 2

            def pair_steps(eng, body):
                half = b * HALF
                body(Step(half, -1), True, False, False, None)
                body(Step(half, 0), True, True, False, 0)
                with eng.Fori(0, HALF - 1) as i:
                    for u in range(2):
                        body(Step(half + i, 1 + u), True, True, True, i * 2 + 1 + u)
                body(Step(half, PAIRS - 1), False, True, True, PAIRS - 1)
                body(Step(half, PAIRS), False, False, True, PAIRS)

            with nc.Block() as block:
                @block.sync
                def _(sp):
                    def load_pair(m, i):
                        sp.wait_ge(s["pairT_mm"], after(m - 2))
                        sp.dma_start(x_pair[m.slot], x_toks[bass.ds(b, 1), bass.ds(i, 1)].rearrange("a s p c -> p (a s c)")
                                     ).then_inc(pair_in[m.slot], 16)

                    def load_res(m, i):
                        sp.wait_ge(s["h0_ready"], after(m - 2))
                        for g in range(4):
                            sp.dma_start(x_res[m.slot][32 * g:32 * g + 32],
                                         x_grid[bass.ds(b, 1), bass.ds(i, 1), g].rearrange("a s t i c -> t i (a s c)")
                                         ).then_inc(res_in[m.slot], 16)

                    def store(m, i):
                        sp.wait_ge(s["out_ready"], after(m))
                        for g in range(4):
                            sp.dma_start(out_grid[bass.ds(b, 1), bass.ds(i, 1), g].rearrange("a s t i c -> t i (a s c)"),
                                         o_out[m.slot][32 * g:32 * g + 32]).then_inc(out_stored[m.slot], 16)

                    half = b * HALF
                    load_pair(Step(half, 0), 0)
                    load_pair(Step(half, 1), 1)
                    load_res(Step(half, 0), 0)
                    load_res(Step(half, 1), 1)
                    load_pair(Step(half, 2), 2)
                    with sp.Fori(0, HALF - 2) as i:
                        for u in range(2):
                            load_pair(Step(half + i, 3 + u), i * 2 + 3 + u)
                            load_res(Step(half + i, 2 + u), i * 2 + 2 + u)
                            store(Step(half + i, u), i * 2 + u)
                    load_pair(Step(half, PAIRS - 1), PAIRS - 1)
                    for m in (PAIRS - 2, PAIRS - 1):
                        load_res(Step(half, m), m)
                        store(Step(half, m - 2), m - 2)
                    for m in (PAIRS - 2, PAIRS - 1):
                        store(Step(half, m), m)
                    for m in (PAIRS - 2, PAIRS - 1):
                        sp.wait_ge(out_stored[m % 2], slot_after(Step(half, m), 4))
                    settle(sp, s["sp_settled"])

                @block.tensor
                def _(pe):
                    def unit(n, u):
                        if u == 0:
                            pe.wait_ge(s["o_copy"], after(n - 2))
                        if UNITS[u] == "D":
                            k = D_UNIT.index(u)
                            pe.wait_ge(s["d_ready"], after(n, ND, k + 1))
                            src = prod_d[(n.odd * ND + k) % 2]
                        else:
                            k = P_UNIT.index(u)
                            pe.wait_ge(s["p_ready"], after(n, NPL, k + 1))
                            src = prod_p[(n.odd * NPL + k) % 2]
                        for jj in range(JU):
                            t, g = divmod(u * JU + jj, 4)
                            mm = nc.tensor.matmul(psum[32 * g:32 * g + 32, O[n.slot], 0:E],
                                                  pick[:, 30 - 2 * t:62 - 2 * t], src[:, jj * E:jj * E + E],
                                                  start=(t == 0), stop=(t == N // 4 - 1))
                        mm.then_inc(s["unit_mm"], 1)

                    def body(n, prep, units, dense, i):
                        nxt, prv = n + 1, n - 1
                        if prep:
                            pe.wait_ge(pair_in[nxt.slot], slot_after(nxt))
                            pe.wait_ge(s["relu_ready"], after(nxt - 3))
                            for k in range(KC):
                                mm = nc.tensor.transpose(psum[:, Z, k * P:k * P + P], x_pair[nxt.slot][:, k * P:k * P + P], eye)
                            mm.then_inc(s["pairT_mm"], 1)
                        if dense:
                            pe.wait_ge(s["o_copy"], after(prv))
                            pe.wait_ge(s["on_ready"], after(prv - 1))
                            for k in range(KC):
                                mm = nc.tensor.transpose(psum[:, X, k * P:k * P + P], o_sb[:, k * P:k * P + P], eye)
                            mm.then_inc(s["oT_mm"], 1)
                        if prep:
                            pe.wait_ge(s["pairT_copy"], after(nxt))
                            pe.wait_ge(s["d_ready"], after(nxt - 2, ND))
                            pe.wait_ge(s["v1_copy"], after(nxt - 2))
                            for k in range(KC):
                                mm = nc.tensor.matmul(psum[:, V1[nxt.slot], 0:E], x_pairT[:, k * P:k * P + P], wv1[:, k, :],
                                                      start=(k == 0), stop=(k == KC - 1))
                            mm.then_inc(s["v1_mm"], 1)
                        if units:
                            unit(n, 0)
                        if dense:
                            pe.wait_ge(s["oT_copy"], after(prv))
                            if prep:
                                pe.wait_ge(s["pairT_copy"], after(nxt))
                            else:
                                pe.wait_ge(s["relu_ready"], after(prv - 1))
                            for k in range(KC):
                                mm = nc.tensor.matmul(psum[:, Z, 0:E], oT[:, k * P:k * P + P], wo[:, k, :],
                                                      start=(k == 0), stop=(k == KC - 1))
                            mm.then_inc(s["wo_mm"], 1)
                        if units:
                            unit(n, 1)
                            unit(n, 2)
                        if dense:
                            pe.wait_ge(s["hn_ready"], after(prv))
                            for k in range(KC):
                                mm = nc.tensor.transpose(psum[:, X, k * P:k * P + P], hn[:, k * P:k * P + P], eye)
                            mm.then_inc(s["hT_mm"], 1)
                            pe.wait_ge(s["hT_copy"], after(prv))
                            for f in range(FC):
                                for k in range(KC):
                                    mm = nc.tensor.matmul(psum[:, Z, f * P:f * P + P], w1[:, k, f * P:f * P + P],
                                                          hT[:, k * P:k * P + P], start=(k == 0), stop=(k == KC - 1))
                            mm.then_inc(s["w1_mm"], 1)
                        if units:
                            unit(n, 3)
                            unit(n, 4)
                        if dense:
                            pe.wait_ge(s["relu_ready"], after(prv))
                            for f in range(FC):
                                nc.tensor.matmul(psum[:, X, 0:E], reluT[:, f * P:f * P + P], w2[:, f, :],
                                                 start=(f == 0), stop=False)
                            for k in range(KC):
                                nc.tensor.matmul(psum[:, X, 0:E], hT[:, k * P:k * P + P],
                                                 ident[:, P - k * P:P - k * P + E], start=False, stop=False)
                            nc.tensor.matmul(psum[:, X, 0:E], ones_row[:, :], b2[:, :], start=False, stop=True
                                             ).then_inc(s["w2_mm"], 1)
                        if prep:
                            pe.wait_ge(s["probs_ready"], after(nxt))
                            pe.wait_ge(s["d_ready"], after(nxt - 2, ND))
                            pe.wait_ge(s["a_copy"], after(nxt - 2))
                            a_bank = psum[:, A[nxt.slot], :].rearrange("p (t r j) -> p t r j", t=2, r=R)
                            for r in range(R):
                                mm = nc.tensor.transpose(a_bank[:, :, r, :], probs[:, r * P:r * P + P], eye)
                            mm.then_inc(s["a_mm"], 1)
                        if units:
                            unit(n, 5)
                            unit(n, 6)
                            unit(n, 7)

                    pair_steps(pe, body)

                @block.scalar
                def _(act):
                    def body(n, prep, units, dense, i):
                        nxt, prv = n + 1, n - 1
                        if dense:
                            act.wait_ge(s["unit_mm"], after(prv, len(UNITS)))
                            act.wait_ge(s["oT_mm"], after(prv - 1))
                            nc.scalar.activation(o_sb, psum[:, O[prv.slot], 0:E], ACT.Copy).then_inc(s["o_copy"], 1)
                        if prep:
                            act.wait_ge(s["pairT_mm"], after(nxt))
                            act.wait_ge(s["v1_mm"], after(nxt - 1))
                            nc.scalar.activation(x_pairT, psum[:, Z, 0:E], ACT.Copy).then_inc(s["pairT_copy"], 1)
                        if dense:
                            act.wait_ge(s["oT_mm"], after(prv))
                            act.wait_ge(s["wo_mm"], after(prv - 1))
                            nc.scalar.activation(oT, psum[:, X, 0:E], ACT.Copy).then_inc(s["oT_copy"], 1)
                        if prep:
                            act.wait_ge(s["v1_mm"], after(nxt))
                            act.wait_ge(s["p_ready"], after(nxt - 2, NPL))
                            nc.scalar.activation(v1_sb[nxt.slot], psum[:, V1[nxt.slot], 0:E], ACT.Copy).then_inc(s["v1_copy"], 1)
                            act.wait_ge(s["max_ready"], after(nxt))
                            act.wait_ge(s["a_mm"], after(nxt - 1))
                            for c in range(2 * R):
                                r, ii = divmod(c, 2)
                                ins = nc.scalar.activation(
                                    probs[:, c * N:c * N + N],
                                    scores_i[:, r, bass.ds((i + 1) * 2 + ii if i is not None else ii, 1), :].rearrange("p a l -> p (a l)"),
                                    ACT.Exp, bias=neg_max[nxt.slot][:, c:c + 1], scale=1.0 / float(np.sqrt(D)),
                                    accum_out=sums[nxt.slot][:, c:c + 1])
                            ins.then_inc(s["exp_ready"], 1)
                        if dense:
                            act.wait_ge(s["var1"], after(prv))
                            nc.scalar.activation(root, variance, ACT.Sqrt).then_inc(s["root1"], 1)
                            act.wait_ge(s["hT_mm"], after(prv))
                            act.wait_ge(s["w2_mm"], after(prv - 1))
                            for k in range(KC):
                                ins = nc.scalar.activation(hT[:, k * P:k * P + P], psum[:, X, k * P:k * P + P], ACT.Identity,
                                                           bias=agg_b[:, k:k + 1], scale=agg_g[:, k:k + 1])
                            ins.then_inc(s["hT_copy"], 1)
                            act.wait_ge(s["w1_mm"], after(prv))
                            for f in range(FC):
                                ins = nc.scalar.activation(reluT[:, f * P:f * P + P], psum[:, Z, f * P:f * P + P],
                                                           ACT.Relu, bias=b1[:, f:f + 1])
                            ins.then_inc(s["relu_ready"], 1)
                        if prep:
                            act.wait_ge(s["a_mm"], after(nxt))
                            act.wait_ge(s["p_ready"], after(nxt - 2, NPL))
                            nc.scalar.activation(a_sb[nxt.slot], psum[:, A[nxt.slot], :], ACT.Copy).then_inc(s["a_copy"], 1)
                        if dense:
                            act.wait_ge(s["var2"], after(prv))
                            nc.scalar.activation(root, variance, ACT.Sqrt).then_inc(s["root2"], 1)

                    pair_steps(act, body)

                def products(eng, lib, n, k, units, bufs, first, ready, v1, a):
                    count = len(units)
                    u = units[k]
                    buf = bufs[(n.odd * count + k) % 2]
                    if k >= 2:
                        eng.wait_ge(s["unit_mm"], after(n, len(UNITS), units[k - 2] + 1))
                    else:
                        eng.wait_ge(s["unit_mm"], after(n - 1, len(UNITS), units[count + k - 2] + 1))
                    lib.tensor_tensor(buf.rearrange("p (j n) -> p j n", j=JU), v2[:, u * JU:(u + 1) * JU, :],
                                      v1.unsqueeze(1).to_broadcast([P, JU, E]), ALU.mult).then_inc(s[first], 1)
                    eng.wait_ge(s[first], after(n, count, k + 1))
                    buf4 = buf.rearrange("p (j h d) -> p j h d", j=JU, h=H)
                    a4 = a.rearrange("p (h j) -> p j h", h=H)[:, u * JU:(u + 1) * JU, :]
                    lib.tensor_tensor(buf4, buf4, a4.unsqueeze(3).to_broadcast([P, JU, H, D]), ALU.mult
                                      ).then_inc(s[ready], 1)

                @block.vector
                def _(dve):
                    def body(n, prep, units, dense, i):
                        nxt, prv = n + 1, n - 1

                        def unit(k):
                            if k == 0:
                                dve.wait_ge(s["a_copy"], after(n))
                            products(dve, nc.vector, n, k, D_UNIT, prod_d, "d_first", "d_ready",
                                     psum[:, V1[n.slot], 0:E], psum[:, A[n.slot], :])

                        if prep:
                            nc.vector.tensor_reduce(row_max.rearrange("p (r i) -> p r i", r=R),
                                                    scores_i[:, :, bass.ds((i + 1) * 2 if i is not None else 0, 2), :],
                                                    AX_X, ALU.max).then_inc(s["max_raw"], 1)
                            dve.wait_ge(s["max_raw"], after(nxt))
                            nc.vector.tensor_scalar(neg_max[nxt.slot], row_max, -1.0 / float(np.sqrt(D)), None,
                                                    ALU.mult).then_inc(s["max_ready"], 1)
                        if units:
                            unit(0)
                        if dense:
                            dve.wait_ge(s["wo_mm"], after(prv))
                            dve.wait_ge(res_in[prv.slot], slot_after(prv, 4))
                            nc.vector.tensor_tensor(h0, psum[:, Z, 0:E], x_res[prv.slot], ALU.add).then_inc(s["h0_ready"], 1)
                            dve.wait_ge(s["h0_ready"], after(prv))
                            nc.vector.bn_stats(stats, h0).then_inc(s["stats1"], 1)
                            dve.wait_ge(s["stats1"], after(prv))
                            settle(dve, s["settled"])
                            nc.vector.bn_aggr(mv1, stats).then_inc(s["mean1"], 1)
                            dve.wait_ge(s["mean1"], after(prv))
                            nc.vector.tensor_scalar(variance, mv1[:, 1:2], EPS_TRI, None, ALU.add).then_inc(s["var1"], 1)
                        if units:
                            unit(1)
                        if prep:
                            dve.wait_ge(s["exp_ready"], after(nxt))
                            dve.wait_ge(s["probs_ready"], after(nxt - 1))
                            nc.vector.reciprocal(inv, sums[nxt.slot]).then_inc(s["inv_ready"], 1)
                            dve.wait_ge(s["inv_ready"], after(nxt))
                            nc.vector.tensor_tensor(probs.rearrange("p (c l) -> p c l", c=2 * R),
                                                    probs.rearrange("p (c l) -> p c l", c=2 * R),
                                                    inv.unsqueeze(2).to_broadcast([P, 2 * R, N]), ALU.mult
                                                    ).then_inc(s["probs_ready"], 1)
                        if dense:
                            dve.wait_ge(s["root1"], after(prv))
                            inverse_root(dve, nc.vector, variance, root, rstd, tmp, s["rstd1"], prv)
                            dve.wait_ge(s["hT_mm"], after(prv - 1))
                            nc.vector.tensor_scalar(hn, h0, mv1[:, 0:1], rstd, ALU.subtract, ALU.mult
                                                    ).then_inc(s["hn_ready"], 1)
                        if units:
                            unit(2)
                            unit(3)
                        if dense:
                            dve.wait_ge(s["w2_mm"], after(prv))
                            nc.vector.bn_stats(stats, psum[:, X, 0:E]).then_inc(s["stats2"], 1)
                            dve.wait_ge(s["stats2"], after(prv))
                            settle(dve, s["settled"])
                            nc.vector.bn_aggr(mv2, stats).then_inc(s["mean2"], 1)
                            dve.wait_ge(s["mean2"], after(prv))
                            nc.vector.tensor_scalar(variance, mv2[:, 1:2], EPS_TRI, None, ALU.add).then_inc(s["var2"], 1)
                        if units:
                            unit(4)
                        if dense:
                            dve.wait_ge(s["root2"], after(prv))
                            inverse_root(dve, nc.vector, variance, root, rstd, tmp, s["rstd2"], prv)
                            dve.wait_ge(s["scaled"], after(prv - 1))
                            nc.vector.tensor_scalar(on, psum[:, X, 0:E], mv2[:, 0:1], rstd, ALU.subtract, ALU.mult
                                                    ).then_inc(s["on_ready"], 1)

                    pair_steps(dve, body)

                @block.gpsimd
                def _(pool):
                    def body(n, prep, units, dense, i):
                        prv = n - 1

                        def unit(k):
                            if k == 0:
                                pool.wait_ge(s["a_copy"], after(n))
                            products(pool, nc.gpsimd, n, k, P_UNIT, prod_p, "p_first", "p_ready",
                                     v1_sb[n.slot], a_sb[n.slot])

                        if units:
                            unit(0)
                        if units:
                            unit(1)
                            unit(2)
                        if dense:
                            pool.wait_ge(s["on_ready"], after(prv))
                            pool.wait_ge(out_stored[(prv - 2).slot], slot_after(prv - 2, 4))
                            nc.gpsimd.tensor_tensor(o_out[prv.slot], on, out_g[:, :], ALU.mult).then_inc(s["scaled"], 1)
                            pool.wait_ge(s["scaled"], after(prv))
                            nc.gpsimd.tensor_tensor(o_out[prv.slot], o_out[prv.slot], out_b[:, :], ALU.add
                                                    ).then_inc(s["out_ready"], 1)

                    pair_steps(pool, body)

        clear(nc, [weights_in, *s.values()])


def global_layer(nc, consts, x, w, xn_dram, q_dram, out):
    G = TOK // BANK
    T4 = BANK // P
    scale = float(np.float32(E) ** np.float32(-0.5))
    with ExitStack() as ctx:
        def sb(what, shape):
            return ctx.enter_context(nc.sbuf_tensor(f"global_{what}", shape, F32))

        def sem(what):
            return ctx.enter_context(nc.semaphore(f"global_{what}"))

        psum = ctx.enter_context(nc.psum_tensor("global_psum", [P, 8, BANK], F32))
        eye = consts["ident"][:, P:2 * P]
        wq, wk, wv, wp = (sb(k, [P, KC, E]) for k in ("wq", "wk", "wv", "wp"))
        bq, bk = sb("bq", [P, KC]), sb("bk", [P, KC])
        gamma, beta, bv, bp = (sb(k, [P, E]) for k in ("gamma", "beta", "bv", "bp"))
        kT, v = sb("kT", [P, KC, TOK]), sb("v", [P, KT, E])
        work = sb("work", [P, 26112])
        at = [0]

        def part(n):
            at[0] += n
            return work[:, at[0] - n:at[0]]

        x_in = [part(T4 * E).rearrange("p (t c) -> p t c", t=T4) for _ in range(2)]
        centred = part(T4 * E).rearrange("p (t c) -> p t c", t=T4)
        xn = [part(T4 * E).rearrange("p (t c) -> p t c", t=T4) for _ in range(2)]
        xnT = part(KC * BANK).rearrange("p (k n) -> p k n", k=KC)
        qT_out = [part(KC * BANK).rearrange("p (k n) -> p k n", k=KC) for _ in range(2)]
        stats, mv = part(T4 * 6), part(T4 * 2)
        rstd, root, tmp, variance = (part(T4) for _ in range(4))
        at[0] = 0
        rows = [part(TOK) for _ in range(2)]
        probsT = part(TOK)
        qT = [part(KC * P).rearrange("p (k n) -> p k n", k=KC) for _ in range(2)]
        xn_in = [part(E) for _ in range(2)]
        xn_bp = [part(E) for _ in range(2)]
        o_sb, oT = part(E), part(E)
        y = [part(E) for _ in range(2)]
        maxima, row_max = part(CHUNK), part(1)
        neg_max = [part(1) for _ in range(2)]
        EXPS = 4
        sums, total = [part(EXPS) for _ in range(2)], part(1)
        inv = [part(1) for _ in range(2)]

        toks = x.rearrange("b (g i) j c -> b g (i j) c", g=G)
        xn_toks = xn_dram.rearrange("b (g i) j c -> b g (i j) c", g=G)
        xn_tiles = xn_dram.rearrange("b (s i) j c -> b s (i j) c", i=2)
        out_tiles = out.rearrange("b (s i) j c -> b s (i j) c", i=2)

        weights_in = sem("weights_in")
        with nc.Block() as block:
            @block.sync
            def _(sp):
                n = 0
                for dst, src in ((wq, w["w_q"]), (wk, w["w_k"]), (wv, w["w_v"]), (wp, w["w_p"])):
                    sp.dma_start(dst[:, :, :], src.rearrange("(k p) n -> p k n", p=P)).then_inc(weights_in, 16)
                    n += 1
                for dst, src in ((bq, w["b_q"]), (bk, w["b_k"])):
                    sp.dma_start(dst[:, :], src.rearrange("(k p) -> p k", p=P), allow_slow_non_contiguous=True).then_inc(weights_in, 16)
                    n += 1
                for dst, src in ((gamma, w["ln_gamma"]), (beta, w["ln_beta"]), (bv, w["b_v"]), (bp, w["b_p"])):
                    sp.dma_start(dst[:, :], src.rearrange("(a n) -> a n", a=1).to_broadcast([P, E])).then_inc(weights_in, 16)
                    n += 1
                sp.wait_ge(weights_in, 16 * n)

        names = ("x_in0", "x_in1", "xn_out0", "xn_out1", "q_out0", "q_out1", "stats", "mean", "variance", "root", "rstd",
                 "centred", "scaled", "xn_ready", "xT_mm", "xT_copy", "qk_mm", "v_mm", "q_copy", "k_copy", "v_copy",
                 "qT_in0", "qT_in1", "res_in0", "res_in1", "res_ready", "scores_mm", "scores_copy",
                 "chunk_max", "row_max", "neg_max", "exp_ready", "total", "inv_ready", "pT_mm", "pT_copy",
                 "pv_mm", "o_ready", "oT_mm", "oT_copy", "proj_mm", "y_ready", "y_out0", "y_out1",
                 "settled", "sp_settled")
        s = {k: sem(k) for k in names}
        credit(nc, s.values())
        x_loaded, xn_stored, q_stored = ((s[k + "0"], s[k + "1"]) for k in ("x_in", "xn_out", "q_out"))
        qT_loaded, res_loaded, y_stored = ((s[k + "0"], s[k + "1"]) for k in ("qT_in", "res_in", "y_out"))

        with nc.Fori(0, B) as b:
            def group_steps(eng, body):
                with eng.Fori(0, G // 2) as i:
                    for u in range(2):
                        body(Step(b * (G // 2) + i, u), i * 2 + u)

            with nc.Block() as block:
                @block.sync
                def _(sp):
                    def load(g, i):
                        sp.wait_ge(s["centred"], after(g - 2, T4))
                        sp.dma_start(x_in[g.slot], toks[bass.ds(b, 1), bass.ds(i, 1)].rearrange("a g (t p) c -> p (a g t) c", p=P)
                                     ).then_inc(x_loaded[g.slot], 16)

                    def store(g, i):
                        sp.wait_ge(s["xn_ready"], after(g))
                        sp.dma_start(xn_toks[bass.ds(b, 1), bass.ds(i, 1)].rearrange("a g (t p) c -> p (a g t) c", p=P),
                                     xn[g.slot]).then_inc(xn_stored[g.slot], 16)
                        sp.wait_ge(s["q_copy"], after(g, KC))
                        for k in range(KC):
                            sp.dma_start(q_dram[bass.ds(b, 1), k, :, bass.ds(i * BANK, BANK)].rearrange("a p n -> p (a n)"),
                                         qT_out[g.slot][:, k, :]).then_inc(q_stored[g.slot], 16)

                    half = b * (G // 2)
                    load(Step(half, 0), 0)
                    load(Step(half, 1), 1)
                    with sp.Fori(0, G // 2 - 1) as i:
                        for u in range(2):
                            store(Step(half + i, u), i * 2 + u)
                            load(Step(half + i, 2 + u), i * 2 + 2 + u)
                    for g in (G - 2, G - 1):
                        store(Step(half, g), g)
                    for g in (G - 2, G - 1):
                        sp.wait_ge(xn_stored[g % 2], slot_after(Step(half, g)))
                        settle(sp, s["sp_settled"])
                        sp.wait_ge(q_stored[g % 2], slot_after(Step(half, g), KC))
                    settle(sp, s["sp_settled"])

                @block.vector
                def _(dve):
                    def body(g, i):
                        dve.wait_ge(x_loaded[g.slot], slot_after(g))
                        dve.wait_ge(s["centred"], after(g - 1, T4))
                        for t in range(T4):
                            ins = nc.vector.bn_stats(stats[:, 6 * t:6 * t + 6], x_in[g.slot][:, t, :])
                        ins.then_inc(s["stats"], 1)
                        dve.wait_ge(s["stats"], after(g))
                        settle(dve, s["settled"])
                        for t in range(T4):
                            ins = nc.vector.bn_aggr(mv[:, 2 * t:2 * t + 2], stats[:, 6 * t:6 * t + 6])
                        ins.then_inc(s["mean"], 1)
                        dve.wait_ge(s["mean"], after(g))
                        nc.vector.tensor_scalar(variance, mv.rearrange("p (t a) -> p t a", a=2)[:, :, 1], EPS_GLOBAL, None,
                                                ALU.add).then_inc(s["variance"], 1)
                        dve.wait_ge(s["root"], after(g))
                        inverse_root(dve, nc.vector, variance, root, rstd, tmp, s["rstd"], g)
                        dve.wait_ge(s["scaled"], after(g - 1))
                        for t in range(T4):
                            nc.vector.tensor_scalar(centred[:, t, :], x_in[g.slot][:, t, :], mv[:, 2 * t:2 * t + 1],
                                                    rstd[:, t:t + 1], ALU.subtract, ALU.mult).then_inc(s["centred"], 1)
                        dve.wait_ge(s["qk_mm"], after(g))
                        for k in range(KC):
                            nc.vector.tensor_scalar(kT[:, k, bass.ds(i * BANK, BANK)], psum[:, 4 + k, :], bk[:, k:k + 1],
                                                    None, ALU.add).then_inc(s["k_copy"], 1)
                        dve.wait_ge(s["v_mm"], after(g))
                        nc.vector.tensor_tensor(v[:, bass.ds(i * T4, T4), :],
                                                psum[:, 6:8, :].rearrange("p a (t c) -> p (a t) c", c=E),
                                                bv[:, :].unsqueeze(1).to_broadcast([P, T4, E]), ALU.add
                                                ).then_inc(s["v_copy"], 1)

                    group_steps(dve, body)

                @block.gpsimd
                def _(pool):
                    def body(g, i):
                        pool.wait_ge(s["centred"], after(g, T4))
                        pool.wait_ge(xn_stored[(g - 2).slot], slot_after(g - 2))
                        pool.wait_ge(s["xT_mm"], after(g - 1))
                        nc.gpsimd.tensor_tensor(xn[g.slot], centred, gamma[:, :].unsqueeze(1).to_broadcast([P, T4, E]),
                                                ALU.mult).then_inc(s["scaled"], 1)
                        pool.wait_ge(s["scaled"], after(g))
                        nc.gpsimd.tensor_tensor(xn[g.slot], xn[g.slot], beta[:, :].unsqueeze(1).to_broadcast([P, T4, E]),
                                                ALU.add).then_inc(s["xn_ready"], 1)

                    group_steps(pool, body)

                @block.tensor
                def _(pe):
                    def body(g, i):
                        pe.wait_ge(s["xn_ready"], after(g))
                        pe.wait_ge(s["xT_copy"], after(g - 1, KC))
                        for k in range(KC):
                            for t in range(T4):
                                mm = nc.tensor.transpose(psum[:, k, t * P:t * P + P], xn[g.slot][:, t, k * P:k * P + P], eye)
                        mm.then_inc(s["xT_mm"], 1)
                        pe.wait_ge(s["xT_copy"], after(g, KC))
                        pe.wait_ge(s["q_copy"], after(g - 1, KC))
                        pe.wait_ge(s["k_copy"], after(g - 1, KC))
                        for wt, bank in ((wq, 2), (wk, 4)):
                            for m in range(KC):
                                for k in range(KC):
                                    mm = nc.tensor.matmul(psum[:, bank + m, :], wt[:, k, m * P:m * P + P], xnT[:, k, :],
                                                          start=(k == 0), stop=(k == KC - 1))
                        mm.then_inc(s["qk_mm"], 1)
                        pe.wait_ge(s["v_copy"], after(g - 1))
                        for t in range(T4):
                            for k in range(KC):
                                mm = nc.tensor.matmul(psum[:, 6 + t // 2, (t % 2) * E:(t % 2 + 1) * E],
                                                      xnT[:, k, t * P:t * P + P], wv[:, k, :],
                                                      start=(k == 0), stop=(k == KC - 1))
                        mm.then_inc(s["v_mm"], 1)

                    group_steps(pe, body)

                @block.scalar
                def _(act):
                    def body(g, i):
                        act.wait_ge(s["variance"], after(g))
                        nc.scalar.activation(root, variance, ACT.Sqrt).then_inc(s["root"], 1)
                        act.wait_ge(s["xT_mm"], after(g))
                        act.wait_ge(s["v_mm"], after(g - 1))
                        for k in range(KC):
                            nc.scalar.activation(xnT[:, k, :], psum[:, k, :], ACT.Copy).then_inc(s["xT_copy"], 1)
                        act.wait_ge(s["qk_mm"], after(g))
                        act.wait_ge(q_stored[(g - 2).slot], slot_after(g - 2, KC))
                        for k in range(KC):
                            nc.scalar.activation(qT_out[g.slot][:, k, :], psum[:, 2 + k, :], ACT.Identity,
                                                 bias=bq[:, k:k + 1]).then_inc(s["q_copy"], 1)

                    group_steps(act, body)

            SB, TB, O, X, Y = (0, 1), (2, 3), (4, 5), 6, 7
            ORDER = "S0 S1 T0 S2 T1 V0 S3 T2 V1 S4 T3 V2 S5 S6 T4 V3 S7 T5 V4 T6 V5 T7 V6 V7".split()
            HALF = KT // 2

            def tile_steps(eng, body):
                half = b * HALF
                body(Step(half, -1), True, False, False, -1)
                body(Step(half, 0), True, True, False, 0)
                with eng.Fori(0, HALF - 1) as i:
                    for u in range(2):
                        body(Step(half + i, 1 + u), True, True, True, i * 2 + 1 + u)
                body(Step(half, KT - 1), False, True, True, KT - 1)
                body(Step(half, KT), False, False, True, KT)

            with nc.Block() as block:
                @block.sync
                def _(sp):
                    def load(m, i):
                        sp.wait_ge(s["scores_mm"], after(m - 2, CHUNK))
                        sp.dma_start(qT[m.slot], q_dram[bass.ds(b, 1), :, :, bass.ds(i * P, P)].rearrange("a k p n -> p (a k) n")
                                     ).then_inc(qT_loaded[m.slot], 16)

                    def load_res(m, i):
                        sp.wait_ge(s["res_ready"], after(m - 2))
                        sp.dma_start(xn_in[m.slot], xn_tiles[bass.ds(b, 1), bass.ds(i, 1)].rearrange("a s p c -> p (a s c)")
                                     ).then_inc(res_loaded[m.slot], 16)

                    def store(m, i):
                        sp.wait_ge(s["y_ready"], after(m))
                        sp.dma_start(out_tiles[bass.ds(b, 1), bass.ds(i, 1)].rearrange("a s p c -> p (a s c)"),
                                     y[m.slot]).then_inc(y_stored[m.slot], 16)

                    half = b * HALF
                    for m in range(2):
                        load(Step(half, m), m)
                        load_res(Step(half, m), m)
                    with sp.Fori(0, HALF - 1) as i:
                        for u in range(2):
                            load(Step(half + i, 2 + u), i * 2 + 2 + u)
                            load_res(Step(half + i, 2 + u), i * 2 + 2 + u)
                            store(Step(half + i, u), i * 2 + u)
                    for m in (KT - 2, KT - 1):
                        store(Step(half, m), m)
                    for m in (KT - 2, KT - 1):
                        sp.wait_ge(y_stored[m % 2], slot_after(Step(half, m)))
                    settle(sp, s["sp_settled"])

                @block.tensor
                def _(pe):
                    def body(n, scores, probs, dense, i):
                        nxt, prv = n + 1, n - 1

                        def run(what, c):
                            if what == "S" and scores:
                                if c == 0:
                                    pe.wait_ge(qT_loaded[nxt.slot], slot_after(nxt))
                                if c >= 2:
                                    pe.wait_ge(s["scores_copy"], after(nxt, CHUNK, c - 1))
                                else:
                                    pe.wait_ge(s["scores_copy"], after(nxt - 1, CHUNK, CHUNK + c - 1))
                                for k in range(KC):
                                    mm = nc.tensor.matmul(psum[:, SB[c % 2], :], qT[nxt.slot][:, k, :],
                                                          kT[:, k, c * BANK:(c + 1) * BANK], start=(k == 0), stop=(k == KC - 1))
                                mm.then_inc(s["scores_mm"], 1)
                            if what == "T" and probs:
                                pe.wait_ge(s["exp_ready"], after(n, EXPS, c * EXPS // CHUNK + 1))
                                if c >= 2:
                                    pe.wait_ge(s["pT_copy"], after(n, CHUNK, c - 1))
                                else:
                                    pe.wait_ge(s["pT_copy"], after(n - 1, CHUNK, CHUNK + c - 1))
                                for t in range(T4):
                                    mm = nc.tensor.transpose(psum[:, TB[c % 2], t * P:t * P + P],
                                                             rows[n.slot][:, c * BANK + t * P:c * BANK + (t + 1) * P], eye)
                                mm.then_inc(s["pT_mm"], 1)
                            if what == "V" and probs:
                                if c == 0:
                                    pe.wait_ge(s["o_ready"], after(n - 2))
                                pe.wait_ge(s["pT_copy"], after(n, CHUNK, c + 1))
                                for t in range(T4):
                                    kt = c * T4 + t
                                    mm = nc.tensor.matmul(psum[:, O[n.slot], 0:E], probsT[:, kt * P:kt * P + P], v[:, kt, :],
                                                          start=(kt == 0), stop=(kt == KT - 1))
                                mm.then_inc(s["pv_mm"], 1)

                        for at_, op in enumerate(ORDER):
                            run(op[0], int(op[1:]))
                            if dense and op == "T1":
                                pe.wait_ge(s["o_ready"], after(prv))
                                pe.wait_ge(s["oT_copy"], after(prv - 1))
                                for k in range(KC):
                                    mm = nc.tensor.transpose(psum[:, X, k * P:k * P + P], o_sb[:, k * P:k * P + P], eye)
                                mm.then_inc(s["oT_mm"], 1)
                            if dense and op == "T3":
                                pe.wait_ge(s["oT_copy"], after(prv))
                                pe.wait_ge(s["y_ready"], after(prv - 1))
                                for k in range(KC):
                                    mm = nc.tensor.matmul(psum[:, Y, 0:E], oT[:, k * P:k * P + P], wp[:, k, :],
                                                          start=(k == 0), stop=(k == KC - 1))
                                mm.then_inc(s["proj_mm"], 1)

                    tile_steps(pe, body)

                @block.scalar
                def _(act):
                    def body(n, scores, probs, dense, i):
                        nxt, prv = n + 1, n - 1
                        for c in range(CHUNK):
                            if scores:
                                act.wait_ge(s["scores_mm"], after(nxt, CHUNK, c + 1))
                                if c == 0:
                                    act.wait_ge(s["pT_mm"], after(nxt - 2, CHUNK))
                                nc.scalar.activation(rows[nxt.slot][:, c * BANK:(c + 1) * BANK], psum[:, SB[c % 2], :],
                                                     ACT.Copy).then_inc(s["scores_copy"], 1)
                            if dense and c == 3:
                                act.wait_ge(s["oT_mm"], after(prv))
                                act.wait_ge(s["proj_mm"], after(prv - 1))
                                nc.scalar.activation(oT, psum[:, X, 0:E], ACT.Copy).then_inc(s["oT_copy"], 1)
                        if scores:
                            act.wait_ge(s["neg_max"], after(nxt))
                            for e in range(EXPS):
                                part_ = rows[nxt.slot][:, e * (TOK // EXPS):(e + 1) * (TOK // EXPS)]
                                nc.scalar.activation(part_, part_, ACT.Exp, bias=neg_max[nxt.slot], scale=scale,
                                                     accum_out=sums[nxt.slot][:, e:e + 1]).then_inc(s["exp_ready"], 1)

                    tile_steps(act, body)

                @block.vector
                def _(dve):
                    def body(n, scores, probs, dense, i):
                        nxt, prv = n + 1, n - 1
                        if dense:
                            dve.wait_ge(s["total"], after(prv))
                            dve.wait_ge(s["pv_mm"], after(prv, CHUNK))
                            dve.wait_ge(s["oT_mm"], after(prv - 1))
                            nc.vector.tensor_scalar(o_sb, psum[:, O[prv.slot], 0:E], inv[prv.slot], None, ALU.mult
                                                    ).then_inc(s["o_ready"], 1)
                        for at_, op in enumerate(ORDER):
                            what, c = op[0], int(op[1:])
                            if what == "S" and scores:
                                dve.wait_ge(s["scores_copy"], after(nxt, CHUNK, c + 1))
                                nc.vector.tensor_reduce(maxima[:, c:c + 1], rows[nxt.slot][:, c * BANK:(c + 1) * BANK],
                                                        AX_X, ALU.max).then_inc(s["chunk_max"], 1)
                                if c == CHUNK - 1:
                                    dve.wait_ge(s["chunk_max"], after(nxt, CHUNK))
                                    nc.vector.tensor_reduce(row_max, maxima, AX_X, ALU.max).then_inc(s["row_max"], 1)
                                    dve.wait_ge(s["row_max"], after(nxt))
                                    nc.vector.tensor_scalar(neg_max[nxt.slot], row_max, -scale, None, ALU.mult
                                                            ).then_inc(s["neg_max"], 1)
                            if what == "T" and probs:
                                dve.wait_ge(s["pT_mm"], after(n, CHUNK, c + 1))
                                dve.wait_ge(s["pv_mm"], after(n - 1, CHUNK, c + 1))
                                nc.vector.tensor_copy(probsT[:, c * BANK:(c + 1) * BANK], psum[:, TB[c % 2], :]
                                                      ).then_inc(s["pT_copy"], 1)
                            if dense and op == "T4":
                                dve.wait_ge(s["proj_mm"], after(prv))
                                dve.wait_ge(s["res_ready"], after(prv))
                                dve.wait_ge(y_stored[(prv - 2).slot], slot_after(prv - 2))
                                nc.vector.tensor_tensor(y[prv.slot], psum[:, Y, 0:E], xn_bp[prv.slot], ALU.add
                                                        ).then_inc(s["y_ready"], 1)
                        if probs:
                            dve.wait_ge(s["exp_ready"], after(n, EXPS))
                            nc.vector.tensor_reduce(total, sums[n.slot], AX_X, ALU.add).then_inc(s["inv_ready"], 1)
                            dve.wait_ge(s["inv_ready"], after(n))
                            nc.vector.reciprocal(inv[n.slot], total).then_inc(s["total"], 1)

                    tile_steps(dve, body)

                @block.gpsimd
                def _(pool):
                    with pool.Fori(0, HALF) as i:
                        for u in range(2):
                            m = Step(b * HALF + i, u)
                            pool.wait_ge(res_loaded[m.slot], slot_after(m))
                            pool.wait_ge(s["y_ready"], after(m - 1 - u))
                            nc.gpsimd.tensor_tensor(xn_bp[m.slot], xn_in[m.slot], bp[:, :], ALU.add
                                                    ).then_inc(s["res_ready"], 1)

        clear(nc, [weights_in, *s.values()])


def conv_layer(nc, consts, x, taps, out):
    G = N // 8
    NP = N + 2
    with ExitStack() as ctx:
        def sb(what, shape):
            return ctx.enter_context(nc.sbuf_tensor(f"conv_{what}", shape, F32))

        def sem(what):
            return ctx.enter_context(nc.semaphore(f"conv_{what}"))

        psum = ctx.enter_context(nc.psum_tensor("conv_psum", [P, 8, BANK], F32))
        eye = consts["ident"][:, P:2 * P]
        tap = sb("tap", [P, KC, 9])
        image = sb("image", [P, KC, NP * NP])
        x_in = [sb(f"x_in{k}", [P, 4, E]) for k in range(2)]
        acc = [sb(f"acc{k}", [P, KC, BANK]) for k in range(2)]
        tile = [sb(f"tile{k}", [P, 4, E]) for k in range(2)]
        img = image[:, :, :].rearrange("p k (r c) -> p k r c", c=NP)
        names = ("taps_in", "cleared", "x_in0", "x_in1", "xT_mm", "image_copy", "summed", "back_mm", "back_copy", "out0", "out1", "sp_settled")
        s = {k: sem(k) for k in names}
        credit(nc, s.values())
        x_loaded, stored = (s["x_in0"], s["x_in1"]), (s["out0"], s["out1"])
        toks = x.rearrange("b (g i) j c -> b g (i j) c", g=G)
        out_toks = out.rearrange("b (g i) j c -> b g (i j) c", g=G)
        with nc.Block() as block:
            @block.sync
            def _(sp):
                for k in range(KC):
                    sp.dma_start(tap[:, k, :], taps.rearrange("a b (k p) -> k p (a b)", p=P)[k], allow_slow_non_contiguous=True).then_inc(s["taps_in"], 16)
                sp.wait_ge(s["taps_in"], 16 * KC + CREDIT)

            @block.gpsimd
            def _(pool):
                nc.gpsimd.memset(image[:, :, :], 0.0).then_inc(s["cleared"], 1)
                pool.wait_ge(s["cleared"], 1 + CREDIT)

        with nc.Fori(0, B) as b:
            half = b * (G // 2)
            with nc.Block() as block:
                def steps(eng, body):
                    with eng.Fori(0, G // 2) as i:
                        for u in range(2):
                            body(Step(half + i, u), i * 2 + u)

                @block.sync
                def _(sp):
                    def body(g, i):
                        sp.wait_ge(s["xT_mm"], after(g - 1))
                        sp.dma_start(x_in[g.slot][:, :, :], toks[bass.ds(b, 1), bass.ds(i, 1)].rearrange("a g (t p) c -> p (a g t) c", p=P)
                                     ).then_inc(x_loaded[g.slot], 16)
                    steps(sp, body)

                @block.tensor
                def _(pe):
                    def body(g, i):
                        pe.wait_ge(x_loaded[g.slot], slot_after(g))
                        pe.wait_ge(s["image_copy"], after(g - 1, KC))
                        for k in range(KC):
                            for t in range(4):
                                mm = nc.tensor.transpose(psum[:, 2 * g.slot + k, t * P:t * P + P], x_in[g.slot][:, t, k * P:k * P + P], eye)
                        mm.then_inc(s["xT_mm"], 1)
                    steps(pe, body)

                @block.scalar
                def _(act):
                    def body(g, i):
                        act.wait_ge(s["xT_mm"], after(g))
                        for k in range(KC):
                            nc.scalar.activation(img[:, k, bass.ds(i * 8 + 1, 8), 1:N + 1],
                                                 psum[:, 2 * g.slot + k, :].rearrange("p (r c) -> p r c", c=N), ACT.Copy
                                                 ).then_inc(s["image_copy"], 1)
                    steps(act, body)

            with nc.Block() as block:
                def steps(eng, body):
                    with eng.Fori(0, G // 2) as i:
                        for u in range(2):
                            body(Step(half + i, u), i * 2 + u)

                TAPS = [(dy, dx) for dy in range(3) for dx in range(3) if (dy, dx) != (1, 1)]

                @block.vector
                def _(dve):
                    def body(g, i):
                        dve.wait_ge(s["back_mm"], after(g - 1))
                        for a, (dy, dx) in enumerate(TAPS):
                            for k in range(KC):
                                to = acc[g.slot][:, k, :].rearrange("p (r c) -> p r c", c=N)
                                plus = img[:, k, bass.ds(i * 8 + 1, 8), 1:N + 1] if a == 0 else to
                                if a:
                                    dve.wait_ge(s["summed"], after(g, 16, (a - 1) * KC + k + 1))
                                nc.vector.scalar_tensor_tensor(
                                    out=to, in0=img[:, k, bass.ds(i * 8 + dy, 8), dx:dx + N],
                                    scalar=tap[:, k, dy * 3 + dx:dy * 3 + dx + 1], in1=plus,
                                    op0=ALU.mult, op1=ALU.add).then_inc(s["summed"], 1)
                    steps(dve, body)

                @block.tensor
                def _(pe):
                    def body(g, i):
                        pe.wait_ge(s["summed"], after(g, 16))
                        pe.wait_ge(s["back_copy"], after(g - 1))
                        for t in range(4):
                            for k in range(KC):
                                mm = nc.tensor.transpose(psum[:, 4 + 2 * g.slot + t // 2, (t % 2) * E + k * P:(t % 2) * E + k * P + P],
                                                         acc[g.slot][:, k, t * P:t * P + P], eye)
                        mm.then_inc(s["back_mm"], 1)
                    steps(pe, body)

                @block.scalar
                def _(act):
                    def body(g, i):
                        act.wait_ge(s["back_mm"], after(g))
                        act.wait_ge(stored[(g - 2).slot], slot_after(g - 2))
                        nc.scalar.activation(tile[g.slot][:, :, :].rearrange("p t c -> p (t c)"),
                                             psum[:, 4 + 2 * g.slot:6 + 2 * g.slot, :].rearrange("p a n -> p (a n)"), ACT.Copy
                                             ).then_inc(s["back_copy"], 1)
                    steps(act, body)

                @block.sync
                def _(sp):
                    def body(g, i):
                        sp.wait_ge(s["back_copy"], after(g))
                        sp.dma_start(out_toks[bass.ds(b, 1), bass.ds(i, 1)].rearrange("a g (t p) c -> p (a g t) c", p=P),
                                     tile[g.slot][:, :, :]).then_inc(stored[g.slot], 16)
                    steps(sp, body)
                    for g in (G - 2, G - 1):
                        sp.wait_ge(stored[g % 2], slot_after(Step(half, g)))
                    settle(sp, s["sp_settled"])


def conv_seq_kernel(nc, x, l0, l1, l2, taps, ident, pick, out):
    x1, x2, x3, xn = (nc.dram_tensor(k, (B, N, N, E), F32).ap() for k in ("x1", "x2", "x3", "xn"))
    q_dram = nc.dram_tensor("qT", (B, KC, P, TOK), F32).ap()
    with ExitStack() as ctx:
        consts = {k: ctx.enter_context(nc.sbuf_tensor(k, shape, F32))
                  for k, shape in (("ident", [P, 3 * P]), ("pick", [P, 62]), ("ones_row", [1, P]))}
        consts_in = ctx.enter_context(nc.semaphore("consts_in"))
        with nc.Block() as block:
            @block.sync
            def _(sp):
                sp.dma_start(consts["ident"][:, :], ident).then_inc(consts_in, 16)
                sp.dma_start(consts["pick"][:, :], pick).then_inc(consts_in, 16)
                sp.wait_ge(consts_in, 32)

            @block.vector
            def _(dve):
                nc.vector.memset(consts["ones_row"][:, :], 1.0)

        triangle_layer(nc, consts, x, l0, x1, "tri0")
        global_layer(nc, consts, x1, l1, xn, q_dram, x2)
        triangle_layer(nc, consts, x2, l2, x3, "tri2")
        conv_layer(nc, consts, x3, taps, out)


_TRI = ("Wq", "Wk", "Wv1", "Wv2", "Wo", "ln_agg_g", "ln_agg_b", "W1", "b1", "W2", "b2", "ln_out_g", "ln_out_b")
_GLOBAL = ("ln_gamma", "ln_beta", "w_q", "b_q", "w_k", "b_k", "w_v", "b_v", "w_p", "b_p")


def kernel(**inputs):
    import concourse.bacc as bacc
    from concourse.bass_utils import run_bass_kernel_spmd

    nc = bacc.Bacc("TRN2", target_bir_lowering=False, num_devices=1)
    arrays = {f"in_{k}": np.ascontiguousarray(v) for k, v in inputs.items()}
    ident = np.zeros((P, 3 * P), np.float32)
    ident[:, P:2 * P] = np.eye(P, dtype=np.float32)
    pick = np.zeros((P, 62), np.float32)
    pick[:N, 30] = 1.0
    pick[N:, 31] = 1.0
    arrays["in_ident"], arrays["in_pick"] = ident, pick
    ap = {k: nc.dram_tensor(k, a.shape, mybir.dt.from_np(a.dtype), kind="ExternalInput").ap() for k, a in arrays.items()}
    out = nc.dram_tensor("out", (B, N, N, E), F32, kind="ExternalOutput").ap()
    conv_seq_kernel(nc, ap["in_x"], {k: ap[f"in_L0_conv_{k}"] for k in _TRI}, {k: ap[f"in_L1_conv_{k}"] for k in _GLOBAL},
                    {k: ap[f"in_L2_conv_{k}"] for k in _TRI}, ap["in_L3_conv_kernel"], ap["in_ident"], ap["in_pick"], out)
    return run_bass_kernel_spmd(nc, [arrays], core_ids=[0]).results[0]["out"]
```

```python
from contextlib import ExitStack

import numpy as np

import concourse.bass as bass
from concourse import mybir

F32 = mybir.dt.float32
ALU = mybir.AluOpType
ACT = mybir.ActivationFunctionType
AX_X = mybir.AxisListType.X

P = 128
B, N, E, H = 2, 64, 256, 8
D = E // H
KC = E // P
F = 2 * E
FC = F // P
R = P // D
BANK = 512
PAIRS = N // 2
GROUPS = N // 4
HW = 2
HP = H - HW
JU = 8
DU = 16
EPS_TRI = 1e-5
EPS_GLOBAL = 1e-3
TOK = N * N
KT = TOK // P
CHUNK = TOK // BANK


class Step:

    def __init__(self, half, odd):
        self.half, self.odd = half, odd

    def __add__(self, k):
        return Step(self.half, self.odd + k)

    def __sub__(self, k):
        return self + -k

    @property
    def slot(self):
        return self.odd % 2

    @property
    def pair(self):
        return self.half + self.odd // 2

    @property
    def number(self):
        return self.half * 2 + self.odd


CREDIT = 32


def after(step, per=1, nth=None):
    return step.number * per + (per if nth is None else nth) + CREDIT


def slot_after(step, dmas=1):
    return (step.pair + 1) * (16 * dmas) + CREDIT


def credit(nc, sems):
    with nc.Block() as block:
        @block.gpsimd
        def _(pool):
            for sem in sems:
                pool.sem_inc(sem, CREDIT)


def clear(nc, sems):
    with nc.Block() as block:
        @block.gpsimd
        def _(pool):
            for sem in sems:
                pool.sem_clear(sem)


def settle(eng, sem):
    eng.sem_inc(sem, 1)


def inverse_root(eng, lib, variance, root, to, tmp, sem, step):
    lib.reciprocal(to, root).then_inc(sem, 1)
    eng.wait_ge(sem, after(step, 5, 1))
    lib.tensor_tensor(tmp, to, to, ALU.mult).then_inc(sem, 1)
    eng.wait_ge(sem, after(step, 5, 2))
    lib.tensor_tensor(tmp, tmp, variance, ALU.mult).then_inc(sem, 1)
    eng.wait_ge(sem, after(step, 5, 3))
    lib.tensor_scalar(tmp, tmp, -0.5, 1.5, ALU.mult, ALU.add).then_inc(sem, 1)
    eng.wait_ge(sem, after(step, 5, 4))
    lib.tensor_tensor(to, to, tmp, ALU.mult).then_inc(sem, 1)
    eng.wait_ge(sem, after(step, 5))


def triangle_layer(nc, consts, x, w, out, name):
    with ExitStack() as ctx:
        def sb(what, shape):
            return ctx.enter_context(nc.sbuf_tensor(f"{name}_{what}", shape, F32))

        def sem(what):
            return ctx.enter_context(nc.semaphore(f"{name}_{what}"))

        psum = ctx.enter_context(nc.psum_tensor(f"{name}_psum", [P, 8, BANK], F32))
        ident, pick, ones_row = consts["ident"], consts["pick"], consts["ones_row"]
        eye = ident[:, P:2 * P]

        wv1, wo = (sb(k, [P, KC, E]) for k in ("wv1", "wo"))
        w1, w2 = sb("w1", [P, KC, F]), sb("w2", [P, FC, E])
        agg_g, agg_b, b1 = sb("agg_g", [P, KC]), sb("agg_b", [P, KC]), sb("b1", [P, FC])
        out_g, out_b, b2 = sb("out_g", [P, E]), sb("out_b", [P, E]), sb("b2", [1, E])
        v2 = sb("v2", [P, N, HP * D])
        v2_w = sb("v2_w", [P, HW * D, N])
        scores = sb("scores", [P, R * N, N])
        scores_i = scores[:, :, :].rearrange("p (r i) l -> p r i l", r=R)

        work = sb("work", [P, 15872])
        at = [0]

        def part(n):
            at[0] += n
            return work[:, at[0] - n:at[0]]

        x_row = [part(2 * E).rearrange("p (t c) -> p t c", t=2) for _ in range(2)]
        x_col = [part(2 * E).rearrange("p (t c) -> p t c", t=2) for _ in range(2)]
        rowT = part(KC * 2 * P).rearrange("p (k n) -> p k n", k=KC)
        colT = [part(KC * 4 * P).rearrange("p (k j n) -> p k j n", k=KC, j=4) for _ in range(2)]
        kT = [part(2 * 2 * P).rearrange("p (t n) -> p t n", t=2) for _ in range(2)]
        q_diag_all = part(2 * 2 * 4 * R * N)
        q_diag = [q_diag_all[:, k * 8 * R * N:(k + 1) * 8 * R * N].rearrange("p (t l r i) -> p t l r i", t=2, l=4, r=R)
                  for k in range(2)]
        wq, wk, wv2 = (part(KC * E).rearrange("p (k n) -> p k n", k=KC) for _ in range(3))
        at[0] = 0
        prod_d = [part(JU * HP * D) for _ in range(2)]
        prod_p = [part(JU * HP * D) for _ in range(2)]
        v1_diag = part(HW * D * 2 * D)
        v1_diag_hd = v1_diag.rearrange("p (h c) -> p h c", h=HW)
        probs = part(2 * R * N)
        a_sb = [part(BANK) for _ in range(2)]
        v1_sb = [part(HP * D) for _ in range(2)]
        x_pair = [part(E) for _ in range(2)]
        x_res = [part(E) for _ in range(2)]
        x_pairT, oT, hn, hT, on = (part(E) for _ in range(5))
        o_sb = part(HP * D)
        h0 = hn
        reluT = part(F)
        o_out = [part(E) for _ in range(2)]
        small = sb("small", [P, 80])
        neg_max = [small[:, 8 * k:8 * k + 8] for k in range(2)]
        sums = [small[:, 16 + 8 * k:24 + 8 * k] for k in range(2)]
        row_max, inv = small[:, 32:40], small[:, 40:48]
        stats1, stats2, mv1, mv2 = small[:, 48:54], small[:, 54:60], small[:, 60:62], small[:, 62:64]
        both_vars = small[:, 60:64].rearrange("p (a b) -> p a b", a=2)[:, :, 1]
        variance, root, rstd, tmp = (small[:, 64 + 2 * k:66 + 2 * k] for k in range(4))

        x_toks = x.rearrange("b (s i) j c -> b s (i j) c", i=2)
        x_cols = x.rearrange("b r (s j) c -> b s j r c", j=2)
        x_grid = x.rearrange("b (s i) (t g) c -> b s g t i c", i=2, g=4)
        out_grid = out.rearrange("b (s i) (t g) c -> b s g t i c", i=2, g=4)

        weights_in = sem("weights_in")
        with nc.Block() as block:
            @block.sync
            def _(sp):
                n = 0
                for dst, src in ((wv1, w["Wv1"]), (wo, w["Wo"]), (w1, w["W1"]), (w2, w["W2"])):
                    sp.dma_start(dst[:, :, :], src.rearrange("(k p) n -> p k n", p=P)).then_inc(weights_in, 16)
                    n += 1
                for dst, src in ((agg_g, w["ln_agg_g"]), (agg_b, w["ln_agg_b"]), (b1, w["b1"])):
                    sp.dma_start(dst[:, :], src.rearrange("(k p) -> p k", p=P), allow_slow_non_contiguous=True).then_inc(weights_in, 16)
                    n += 1
                for dst, src in ((out_g, w["ln_out_g"]), (out_b, w["ln_out_b"])):
                    sp.dma_start(dst[:, :], src.rearrange("(a n) -> a n", a=1).to_broadcast([P, E])).then_inc(weights_in, 16)
                    n += 1
                sp.dma_start(b2[:, :], w["b2"].rearrange("(a n) -> a n", a=1)).then_inc(weights_in, 16)
                sp.wait_ge(weights_in, 16 * (n + 1))

        names = ("qkv_in", "rows_in0", "rows_in1", "cols_in0", "cols_in1", "diag_zero", "xT_mm", "rowT_copy",
                 "colT_copy", "v2_mm", "v2_copy", "qk_mm", "kT_copy", "q0_copy", "q1_copy",
                 "scores_mm", "scores_copy",
                 "pair_in0", "pair_in1", "res_in0", "res_in1", "v1_diag_zero", "small_set", "pairT_mm",
                 "pairT_copy", "v1_mm", "v1_copy", "max_raw", "max_ready", "exp_ready", "inv_ready",
                 "probs_ready", "a_mm", "a_copy", "d_first", "d_ready", "p_first", "p_ready", "unit_mm",
                 "o_copy", "ow_copy", "oT_mm", "oT_copy", "wo_mm", "h0_ready", "stats1", "mean1", "stats2",
                 "mean2", "variance", "root", "rstd", "hn_ready", "hT_mm", "hT_copy", "w1_mm",
                 "relu_ready", "w2_mm", "on_ready", "scaled", "out_ready", "out_stored0", "out_stored1",
                 "settled", "sp_settled")
        s = {k: sem(k) for k in names}
        credit(nc, s.values())
        rows_in, cols_in = (s["rows_in0"], s["rows_in1"]), (s["cols_in0"], s["cols_in1"])
        pair_in, res_in = (s["pair_in0"], s["pair_in1"]), (s["res_in0"], s["res_in1"])
        out_stored = (s["out_stored0"], s["out_stored1"])

        with nc.Fori(0, B) as b:
            def group_steps(eng, body):
                half = b * (GROUPS // 2)
                body(Step(half, -1), None)
                with eng.Fori(0, GROUPS // 2 - 1) as i:
                    for u in range(2):
                        body(Step(half + i, u), (i, u))
                for g in (GROUPS - 2, GROUPS - 1):
                    body(Step(half, g), (0, g))

            with nc.Block() as block:
                t_bank, qk_bank = (0, 1), (2, 3)
                v2_psum = psum[:, 4:6, :].rearrange("p a n -> p (a n)")
                s_psum = psum[:, 6:8, :].rearrange("p a n -> p (a n)")

                @block.sync
                def _(sp):
                    def load(g, i):
                        sp.wait_ge(s["xT_mm"], after(g - 2))
                        for t in range(2):
                            sp.dma_start(x_row[g.slot][:, t, :],
                                         x_toks[bass.ds(b, 1), bass.ds(i * 2 + t, 1)].rearrange("a s p c -> p (a s c)")
                                         ).then_inc(rows_in[g.slot], 16)
                            for j in range(2):
                                sp.dma_start(x_col[g.slot][N * j:N * j + N, t, :],
                                             x_cols[bass.ds(b, 1), bass.ds(i * 2 + t, 1), j].rearrange("a s r c -> r (a s c)")
                                             ).then_inc(cols_in[g.slot], 16)

                    for dst, src in ((wq, w["Wq"]), (wk, w["Wk"]), (wv2, w["Wv2"])):
                        sp.dma_start(dst, src.rearrange("(k p) n -> p k n", p=P)).then_inc(s["qkv_in"], 16)
                    half = b * (GROUPS // 2)
                    for g in range(2):
                        load(Step(half, g), g)
                    with sp.Fori(0, GROUPS // 2 - 1) as i:
                        for u in range(2):
                            load(Step(half + i, 2 + u), i * 2 + 2 + u)

                @block.gpsimd
                def _(pool):
                    nc.gpsimd.memset(q_diag_all, 0.0).then_inc(s["diag_zero"], 1)

                @block.tensor
                def _(pe):
                    def body(g, where):
                        nxt = g + 1
                        if where is None or g.odd < GROUPS - 1:
                            pe.wait_ge(rows_in[nxt.slot], slot_after(nxt, 2))
                            pe.wait_ge(cols_in[nxt.slot], slot_after(nxt, 4))
                            pe.wait_ge(s["rowT_copy"], after(nxt - 1))
                            pe.wait_ge(s["colT_copy"], after(nxt - 1))
                            for bank, src in ((t_bank[0], x_row[nxt.slot]), (t_bank[1], x_col[nxt.slot])):
                                for k in range(KC):
                                    for t in range(2):
                                        c = (k * 2 + t) * P
                                        mm = nc.tensor.transpose(psum[:, bank, c:c + P], src[:, t, k * P:k * P + P], eye)
                            mm.then_inc(s["xT_mm"], 1)
                        if where is not None:
                            pe.wait_ge(s["v2_copy"], after(g - 1))
                            for j in range(4):
                                for k in range(KC):
                                    mm = nc.tensor.matmul(v2_psum[:, j * E:j * E + E], colT[g.slot][:, k, j, :],
                                                          wv2[:, k, :], start=(k == 0), stop=(k == KC - 1))
                            mm.then_inc(s["v2_mm"], 1)
                        if where is None or g.odd < GROUPS - 1:
                            if where is None:
                                pe.wait_ge(s["qkv_in"], (b + 1) * 48 + CREDIT)
                            pe.wait_ge(s["rowT_copy"], after(nxt))
                            pe.wait_ge(s["colT_copy"], after(nxt))
                            pe.wait_ge(s["kT_copy"], after(nxt - 1))
                            pe.wait_ge(s["q0_copy"], after(nxt - 1))
                            pe.wait_ge(s["q1_copy"], after(nxt - 1))
                            for bank, wt, src in ((qk_bank[0], wq, colT[nxt.slot][:, :, :, 0:N]),
                                                  (qk_bank[1], wk, rowT[:, :, :])):
                                for t in range(2):
                                    for k in range(KC):
                                        mm = nc.tensor.matmul(psum[:, bank, t * 2 * P:(t + 1) * 2 * P],
                                                              wt[:, k, t * P:t * P + P], src[:, k],
                                                              start=(k == 0), stop=(k == KC - 1))
                            mm.then_inc(s["qk_mm"], 1)
                        if where is not None:
                            pe.wait_ge(s["kT_copy"], after(g))
                            pe.wait_ge(s["q0_copy"], after(g))
                            pe.wait_ge(s["q1_copy"], after(g))
                            pe.wait_ge(s["scores_copy"], after(g - 1))
                            for l in range(4):
                                for t in range(2):
                                    mm = nc.tensor.matmul(s_psum[N * t:N * t + N, l * R * N:(l + 1) * R * N],
                                                          kT[g.slot][:, t, l * N:l * N + N],
                                                          q_diag[g.slot][:, t, l].rearrange("p r i -> p (r i)"),
                                                          start=True, stop=True)
                            mm.then_inc(s["scores_mm"], 1)

                    group_steps(pe, body)

                @block.scalar
                def _(act):
                    def body(g, where):
                        nxt = g + 1
                        if where is None or g.odd < GROUPS - 1:
                            act.wait_ge(s["xT_mm"], after(nxt))
                            act.wait_ge(s["qk_mm"], after(nxt - 1))
                            nc.scalar.activation(rowT[:, :, :], psum[:, t_bank[0], :].rearrange("p (k n) -> p k n", k=KC),
                                                 ACT.Copy).then_inc(s["rowT_copy"], 1)
                        if where is not None:
                            i, u = where
                            act.wait_ge(s["v2_mm"], after(g))
                            v2_jn = v2_psum.rearrange("p (j n) -> p j n", j=4)
                            nc.scalar.activation(v2[:, bass.ds((i * 2 + u) * 4, 4), :], v2_jn[:, :, 0:HP * D], ACT.Copy)
                            nc.scalar.activation(v2_w[:, :, bass.ds((i * 2 + u) * 4, 4)],
                                                 v2_jn[:, :, HP * D:E].rearrange("p j n -> p n j"), ACT.Copy
                                                 ).then_inc(s["v2_copy"], 1)
                        if where is None or g.odd < GROUPS - 1:
                            act.wait_ge(s["qk_mm"], after(nxt))
                            act.wait_ge(s["scores_mm"], after(nxt - 2))
                            nc.scalar.activation(kT[nxt.slot][:, :, :],
                                                 psum[:, qk_bank[1], :].rearrange("p (t n) -> p t n", t=2),
                                                 ACT.Copy).then_inc(s["kT_copy"], 1)
                            if where is None:
                                act.wait_ge(s["diag_zero"], b + 1 + CREDIT)
                            for r in range(2):
                                ins = q_copy(nc.scalar, nxt, r)
                            ins.then_inc(s["q0_copy"], 1)

                    def q_copy(eng, g, r):
                        rows = slice(D * r, D * r + D)
                        return eng.activation(q_diag[g.slot][rows, :, :, r, :],
                                              psum[rows, qk_bank[0], :].rearrange("p (t l i) -> p t l i", t=2, l=4),
                                              ACT.Copy)

                    group_steps(act, body)

                @block.vector
                def _(dve):
                    def body(g, where):
                        nxt = g + 1
                        if where is None or g.odd < GROUPS - 1:
                            dve.wait_ge(s["xT_mm"], after(nxt))
                            dve.wait_ge(s["v2_mm"], after(nxt - 2))
                            for k in range(KC):
                                src = psum[:, t_bank[1], k * 4 * N:(k + 1) * 4 * N].rearrange("p (j n) -> p j n", j=4)
                                ins = nc.vector.tensor_copy(colT[nxt.slot][:, k].rearrange("p j (a n) -> p j a n", a=2),
                                                            src.unsqueeze(2).to_broadcast([P, 4, 2, N]))
                            ins.then_inc(s["colT_copy"], 1)
                            dve.wait_ge(s["qk_mm"], after(nxt))
                            dve.wait_ge(s["kT_copy"], after(nxt))
                            if where is None:
                                dve.wait_ge(s["diag_zero"], b + 1 + CREDIT)
                            dve.wait_ge(s["q0_copy"], after(nxt))
                            for r in range(2, R):
                                rows = slice(D * r, D * r + D)
                                ins = nc.vector.tensor_copy(q_diag[nxt.slot][rows, :, :, r, :],
                                                            psum[rows, qk_bank[0], :].rearrange("p (t l i) -> p t l i", t=2, l=4))
                            ins.then_inc(s["q1_copy"], 1)
                        if where is not None:
                            i, u = where
                            dve.wait_ge(s["scores_mm"], after(g))
                            nc.vector.tensor_copy(scores[:, :, bass.ds((i * 2 + u) * 4, 4)],
                                                  s_psum.rearrange("p (l n) -> p n l", l=4)
                                                  ).then_inc(s["scores_copy"], 1)

                    group_steps(dve, body)

            UNITS = "DW PW DB DW PB DB PW DB PB DB PB DB".split()
            NU = len(UNITS)
            ORDINAL = {e: [u for u, what in enumerate(UNITS) if what[0] == e] for e in "DP"}
            B_UNITS = [u for u, what in enumerate(UNITS) if what[1] == "B"]
            W_UNITS = [u for u, what in enumerate(UNITS) if what[1] == "W"]
            LAST_W = W_UNITS[-1]
            ND, NPL = len(ORDINAL["D"]), len(ORDINAL["P"])
            NDB, NPB = UNITS.count("DB"), UNITS.count("PB")
            A, V1, O, OW, X, Z = (0, 1), (2, 3), 4, 5, 6, 7
            HALF = PAIRS // 2

            def pair_steps(eng, body):
                half = b * HALF

                def straight(n):
                    body(Step(half, n), n + 2 < PAIRS, 0 <= n + 1 < PAIRS, 0 <= n < PAIRS, 0 <= n - 1 < PAIRS,
                         0 <= n - 2, n)

                for n in range(-2, 2):
                    straight(n)
                with eng.Fori(0, HALF - 2) as i:
                    for u in range(2):
                        body(Step(half + i, 2 + u), True, True, True, True, True, i * 2 + 2 + u)
                for n in range(PAIRS - 2, PAIRS + 2):
                    straight(n)

            def after_root(n, nth=5, per=5):
                return (n.number + b - 1) * per + nth + CREDIT

            with nc.Block() as block:
                @block.sync
                def _(sp):
                    def load_pair(m, i):
                        sp.wait_ge(s["pairT_mm"], after(m - 2))
                        sp.dma_start(x_pair[m.slot], x_toks[bass.ds(b, 1), bass.ds(i, 1)].rearrange("a s p c -> p (a s c)")
                                     ).then_inc(pair_in[m.slot], 16)

                    def load_res(m, i):
                        sp.wait_ge(s["h0_ready"], after(m - 2))
                        for g in range(4):
                            sp.dma_start(x_res[m.slot][32 * g:32 * g + 32],
                                         x_grid[bass.ds(b, 1), bass.ds(i, 1), g].rearrange("a s t i c -> t i (a s c)")
                                         ).then_inc(res_in[m.slot], 16)

                    def store(m, i):
                        sp.wait_ge(s["out_ready"], after(m))
                        for g in range(4):
                            sp.dma_start(out_grid[bass.ds(b, 1), bass.ds(i, 1), g].rearrange("a s t i c -> t i (a s c)"),
                                         o_out[m.slot][32 * g:32 * g + 32]).then_inc(out_stored[m.slot], 16)

                    half = b * HALF
                    for m in range(2):
                        load_pair(Step(half, m), m)
                    for m in range(2):
                        load_res(Step(half, m), m)
                    for m in range(2, 4):
                        load_pair(Step(half, m), m)
                    with sp.Fori(0, HALF - 2) as i:
                        for u in range(2):
                            load_pair(Step(half + i, 4 + u), i * 2 + 4 + u)
                            load_res(Step(half + i, 2 + u), i * 2 + 2 + u)
                            store(Step(half + i, u), i * 2 + u)
                    for m in range(PAIRS - 4, PAIRS):
                        if m + 2 < PAIRS:
                            load_res(Step(half, m + 2), m + 2)
                        store(Step(half, m), m)
                    for m in (PAIRS - 2, PAIRS - 1):
                        sp.wait_ge(out_stored[m % 2], slot_after(Step(half, m), 4))
                    settle(sp, s["sp_settled"])

                @block.tensor
                def _(pe):
                    def unit(n, u):
                        if UNITS[u][0] == "D":
                            k = ORDINAL["D"].index(u)
                            pe.wait_ge(s["d_ready"], after(n, ND, k + 1))
                            src = prod_d[(n.odd * ND + k) % 2]
                        else:
                            k = ORDINAL["P"].index(u)
                            pe.wait_ge(s["p_ready"], after(n, NPL, k + 1))
                            src = prod_p[(n.odd * NPL + k) % 2]
                        if UNITS[u][1] == "W":
                            if u == W_UNITS[0]:
                                pe.wait_ge(s["v1_copy"], after(n))
                                pe.wait_ge(s["ow_copy"], after(n - 1))
                            h, part_ = divmod(W_UNITS.index(u), D // DU)
                            for dd in range(DU):
                                d = part_ * DU + dd
                                c = (h * D + d) * 2 * D
                                mm = nc.tensor.matmul(psum[2 * D * h:2 * D * (h + 1), OW, 0:N], v1_diag[:, c:c + 2 * D],
                                                      src[:, dd * N:dd * N + N], start=(d == 0), stop=(d == D - 1))
                        else:
                            if u == B_UNITS[0]:
                                pe.wait_ge(s["o_copy"], after(n - 1))
                            for jj in range(JU):
                                t, g = divmod(B_UNITS.index(u) * JU + jj, 4)
                                mm = nc.tensor.matmul(psum[32 * g:32 * g + 32, O, 0:HP * D],
                                                      pick[:, 30 - 2 * t:62 - 2 * t],
                                                      src[:, jj * HP * D:(jj + 1) * HP * D],
                                                      start=(t == 0), stop=(t == N // 4 - 1))
                        mm.then_inc(s["unit_mm"], 1)

                    def body(n, maxima, prep, units, dense, last, i):
                        nxt, prv, old = n + 1, n - 1, n - 2
                        if units:
                            unit(n, 0)
                            unit(n, 1)
                        if dense:
                            pe.wait_ge(s["o_copy"], after(prv))
                            pe.wait_ge(s["hT_copy"], after(prv - 1))
                            nc.tensor.transpose(psum[:, X, 0:P], o_sb[:, 0:P], eye)
                            nc.tensor.transpose(psum[0:HP * D - P, X, P:2 * P], o_sb[:, P:HP * D], eye).then_inc(s["oT_mm"], 1)
                        if units:
                            unit(n, 2)
                        if dense:
                            pe.wait_ge(s["oT_copy"], after(prv))
                            pe.wait_ge(s["ow_copy"], after(prv))
                            pe.wait_ge(s["relu_ready"], after(prv - 1))
                            for k in range(KC):
                                mm = nc.tensor.matmul(psum[:, Z, 0:E], oT[:, k * P:k * P + P], wo[:, k, :],
                                                      start=(k == 0), stop=(k == KC - 1))
                            mm.then_inc(s["wo_mm"], 1)
                        if units:
                            unit(n, 3)
                            unit(n, 4)
                            unit(n, 5)
                        if last:
                            pe.wait_ge(s["relu_ready"], after(old))
                            pe.wait_ge(s["oT_copy"], after(old + 1) if dense else after(old))
                            for f in range(FC):
                                nc.tensor.matmul(psum[:, X, 0:E], reluT[:, f * P:f * P + P], w2[:, f, :],
                                                 start=(f == 0), stop=False)
                            for k in range(KC):
                                nc.tensor.matmul(psum[:, X, 0:E], hT[:, k * P:k * P + P],
                                                 ident[:, P - k * P:P - k * P + E], start=False, stop=False)
                            nc.tensor.matmul(psum[:, X, 0:E], ones_row[:, :], b2[:, :], start=False, stop=True
                                             ).then_inc(s["w2_mm"], 1)
                        if units:
                            unit(n, 6)
                        if prep:
                            pe.wait_ge(pair_in[nxt.slot], slot_after(nxt))
                            pe.wait_ge(s["h0_ready"], after(prv))
                            for k in range(KC):
                                mm = nc.tensor.transpose(psum[:, Z, k * P:k * P + P], x_pair[nxt.slot][:, k * P:k * P + P], eye)
                            mm.then_inc(s["pairT_mm"], 1)
                        if units:
                            unit(n, 7)
                        if prep:
                            pe.wait_ge(s["probs_ready"], after(nxt))
                            pe.wait_ge(s["d_ready"], after(nxt - 2, ND))
                            pe.wait_ge(s["a_copy"], after(nxt - 2))
                            a_bank = psum[:, A[nxt.slot], :].rearrange("p (t r j) -> p t r j", t=2, r=R)
                            for r in range(R):
                                mm = nc.tensor.transpose(a_bank[:, :, r, :], probs[:, r * P:r * P + P], eye)
                            mm.then_inc(s["a_mm"], 1)
                        if units:
                            unit(n, 8)
                        if prep:
                            pe.wait_ge(s["pairT_copy"], after(nxt))
                            pe.wait_ge(s["d_first"], after(nxt - 2, NDB))
                            pe.wait_ge(s["v1_copy"], after(nxt - 2))
                            for k in range(KC):
                                mm = nc.tensor.matmul(psum[:, V1[nxt.slot], 0:E], x_pairT[:, k * P:k * P + P], wv1[:, k, :],
                                                      start=(k == 0), stop=(k == KC - 1))
                            mm.then_inc(s["v1_mm"], 1)
                        if units:
                            unit(n, 9)
                        if dense:
                            pe.wait_ge(s["hn_ready"], after(prv))
                            if last:
                                pe.wait_ge(s["on_ready"], after(old))
                            for k in range(KC):
                                mm = nc.tensor.transpose(psum[:, X, k * P:k * P + P], hn[:, k * P:k * P + P], eye)
                            mm.then_inc(s["hT_mm"], 1)
                        if units:
                            unit(n, 10)
                        if dense:
                            pe.wait_ge(s["hT_copy"], after(prv))
                            if prep:
                                pe.wait_ge(s["pairT_copy"], after(nxt))
                            for f in range(FC):
                                for k in range(KC):
                                    mm = nc.tensor.matmul(psum[:, Z, f * P:f * P + P], w1[:, k, f * P:f * P + P],
                                                          hT[:, k * P:k * P + P], start=(k == 0), stop=(k == KC - 1))
                            mm.then_inc(s["w1_mm"], 1)
                        if units:
                            unit(n, 11)

                    pair_steps(pe, body)

                @block.scalar
                def _(act):
                    def body(n, maxima, prep, units, dense, last, i):
                        nxt, prv, old = n + 1, n - 1, n - 2
                        if dense:
                            act.wait_ge(s["unit_mm"], after(prv, NU))
                            act.wait_ge(s["oT_mm"], after(prv - 1))
                            nc.scalar.activation(o_sb, psum[:, O, 0:HP * D], ACT.Copy).then_inc(s["o_copy"], 1)
                        if dense:
                            act.wait_ge(s["oT_mm"], after(prv))
                            act.wait_ge(s["wo_mm"], after(prv - 1))
                            nc.scalar.activation(oT[:, 0:P], psum[:, X, 0:P], ACT.Copy)
                            nc.scalar.activation(oT[0:HP * D - P, P:2 * P], psum[0:HP * D - P, X, P:2 * P], ACT.Copy
                                                 ).then_inc(s["oT_copy"], 1)
                        if prep:
                            act.wait_ge(s["max_ready"], after(nxt))
                            act.wait_ge(s["a_mm"], after(nxt - 1))
                            for c in range(2 * R):
                                r, ii = divmod(c, 2)
                                ins = nc.scalar.activation(
                                    probs[:, c * N:c * N + N],
                                    scores_i[:, r, bass.ds((i + 1) * 2 + ii, 1), :].rearrange("p a l -> p (a l)"),
                                    ACT.Exp, bias=neg_max[nxt.slot][:, c:c + 1], scale=1.0 / float(np.sqrt(D)),
                                    accum_out=sums[nxt.slot][:, c:c + 1])
                            ins.then_inc(s["exp_ready"], 1)
                        if units:
                            act.wait_ge(s["unit_mm"], after(n, NU, LAST_W + 1))
                            act.wait_ge(s["wo_mm"], after(n - 1))
                            for h in range(HW):
                                for ii in range(2):
                                    to = oT[HP * D - P + h * D:HP * D - P + (h + 1) * D, P:2 * P].rearrange(
                                        "p (g t i) -> p i g t", g=4, i=2)[:, ii]
                                    of = psum[(2 * h + ii) * D:(2 * h + ii + 1) * D, OW, 0:N].rearrange("p (t g) -> p g t", g=4)
                                    ins = nc.scalar.activation(to, of, ACT.Copy)
                            ins.then_inc(s["ow_copy"], 1)
                        if dense or last:
                            act.wait_ge(s["variance"], after_root(n, 1, 1))
                            nc.scalar.activation(root, variance, ACT.Sqrt).then_inc(s["root"], 1)
                        if prep:
                            act.wait_ge(s["pairT_mm"], after(nxt))
                            act.wait_ge(s["v1_mm"], after(nxt - 1))
                            nc.scalar.activation(x_pairT, psum[:, Z, 0:E], ACT.Copy).then_inc(s["pairT_copy"], 1)
                        if prep:
                            act.wait_ge(s["a_mm"], after(nxt))
                            act.wait_ge(s["p_ready"], after(nxt - 2, NPL))
                            nc.scalar.activation(a_sb[nxt.slot], psum[:, A[nxt.slot], :], ACT.Copy).then_inc(s["a_copy"], 1)
                        if prep:
                            act.wait_ge(s["v1_mm"], after(nxt))
                            act.wait_ge(s["p_ready"], after(nxt - 2, NPL))
                            act.wait_ge(s["unit_mm"], after(nxt - 1, NU, LAST_W + 1))
                            act.wait_ge(s["v1_diag_zero"], b + 1 + CREDIT)
                            nc.scalar.activation(v1_sb[nxt.slot], psum[:, V1[nxt.slot], 0:HP * D], ACT.Copy)
                            for ii in range(2):
                                rows = slice(N * ii, N * ii + N)
                                ins = nc.scalar.activation(v1_diag_hd[rows, :, ii * D::2 * D + 1][:, :, 0:D],
                                                           psum[rows, V1[nxt.slot], HP * D:E].rearrange("p (h d) -> p h d", h=HW), ACT.Copy)
                            ins.then_inc(s["v1_copy"], 1)
                        if dense:
                            act.wait_ge(s["hT_mm"], after(prv))
                            act.wait_ge(s["w2_mm"], after(prv - 1))
                            for k in range(KC):
                                ins = nc.scalar.activation(hT[:, k * P:k * P + P], psum[:, X, k * P:k * P + P], ACT.Identity,
                                                           bias=agg_b[:, k:k + 1], scale=agg_g[:, k:k + 1])
                            ins.then_inc(s["hT_copy"], 1)
                        if dense:
                            act.wait_ge(s["w1_mm"], after(prv))
                            for f in range(FC):
                                ins = nc.scalar.activation(reluT[:, f * P:f * P + P], psum[:, Z, f * P:f * P + P],
                                                           ACT.Relu, bias=b1[:, f:f + 1])
                            ins.then_inc(s["relu_ready"], 1)

                    pair_steps(act, body)

                def of_products(n, k, engine):
                    units = ORDINAL[engine]
                    buf = (prod_d if engine == "D" else prod_p)[(n.odd * len(units) + k) % 2]
                    if k >= 2:
                        return buf, after(n, NU, units[k - 2] + 1)
                    return buf, after(n - 1, NU, units[len(units) + k - 2] + 1)

                def w_factors(u, a):
                    h, part_ = divmod(W_UNITS.index(u), D // DU)
                    v2_u = v2_w[:, h * D + part_ * DU:h * D + (part_ + 1) * DU, :]
                    return v2_u, a[:, (HP + h) * N:(HP + h + 1) * N].unsqueeze(1).to_broadcast([P, DU, N])

                @block.vector
                def _(dve):
                    def unit(n, k):
                        u = ORDINAL["D"][k]
                        a = psum[:, A[n.slot], :]
                        buf, free = of_products(n, k, "D")
                        if k == 0:
                            dve.wait_ge(s["a_copy"], after(n))
                        dve.wait_ge(s["unit_mm"], free)
                        if UNITS[u] == "DW":
                            v2_u, a_u = w_factors(u, a)
                            nc.vector.tensor_tensor(buf[:, 0:DU * N].rearrange("p (d j) -> p d j", d=DU), v2_u, a_u,
                                                    ALU.mult).then_inc(s["d_ready"], 1)
                            return
                        c = B_UNITS.index(u)
                        kb = [x_ for x_ in ORDINAL["D"] if UNITS[x_] == "DB"].index(u)
                        if kb == 0:
                            dve.wait_ge(s["v1_copy"], after(n))
                        nc.vector.tensor_tensor(buf.rearrange("p (j n) -> p j n", j=JU), v2[:, c * JU:(c + 1) * JU, :],
                                                psum[:, V1[n.slot], 0:HP * D].unsqueeze(1).to_broadcast([P, JU, HP * D]),
                                                ALU.mult).then_inc(s["d_first"], 1)
                        dve.wait_ge(s["d_first"], after(n, NDB, kb + 1))
                        buf4 = buf.rearrange("p (j h d) -> p j h d", j=JU, h=HP)
                        a4 = a.rearrange("p (h j) -> p j h", h=H)[:, c * JU:(c + 1) * JU, 0:HP]
                        nc.vector.tensor_tensor(buf4, buf4, a4.unsqueeze(3).to_broadcast([P, JU, HP, D]), ALU.mult
                                                ).then_inc(s["d_ready"], 1)

                    def body(n, maxima, prep, units, dense, last, i):
                        nxt, prv, old = n + 1, n - 1, n - 2
                        if maxima and isinstance(i, int) and i == -2:
                            nc.vector.memset(small[:, 60:72], 1.0).then_inc(s["small_set"], 1)
                            dve.wait_ge(s["small_set"], b + 1 + CREDIT)
                        if units:
                            unit(n, 0)
                            unit(n, 1)
                            unit(n, 2)
                            unit(n, 3)
                        if dense:
                            dve.wait_ge(s["wo_mm"], after(prv))
                            dve.wait_ge(res_in[prv.slot], slot_after(prv, 4))
                            dve.wait_ge(s["hT_mm"], after(prv - 1))
                            nc.vector.tensor_tensor(h0, psum[:, Z, 0:E], x_res[prv.slot], ALU.add).then_inc(s["h0_ready"], 1)
                        if units:
                            unit(n, 4)
                        if last:
                            dve.wait_ge(s["w2_mm"], after(old))
                            nc.vector.bn_stats(stats2, psum[:, X, 0:E]).then_inc(s["stats2"], 1)
                        if dense:
                            dve.wait_ge(s["h0_ready"], after(prv))
                            nc.vector.bn_stats(stats1, h0).then_inc(s["stats1"], 1)
                        if last:
                            dve.wait_ge(s["stats2"], after(old))
                            settle(dve, s["settled"])
                            nc.vector.bn_aggr(mv2, stats2).then_inc(s["mean2"], 1)
                        if dense:
                            dve.wait_ge(s["stats1"], after(prv))
                            settle(dve, s["settled"])
                            nc.vector.bn_aggr(mv1, stats1).then_inc(s["mean1"], 1)
                        if dense or last:
                            if dense:
                                dve.wait_ge(s["mean1"], after(prv))
                            if last:
                                dve.wait_ge(s["mean2"], after(old))
                            nc.vector.tensor_scalar(variance, both_vars, EPS_TRI, None, ALU.add).then_inc(s["variance"], 1)
                        if prep:
                            dve.wait_ge(s["exp_ready"], after(nxt))
                            dve.wait_ge(s["probs_ready"], after(nxt - 1))
                            nc.vector.reciprocal(inv, sums[nxt.slot]).then_inc(s["inv_ready"], 1)
                            dve.wait_ge(s["inv_ready"], after(nxt))
                            nc.vector.tensor_tensor(probs.rearrange("p (c l) -> p c l", c=2 * R),
                                                    probs.rearrange("p (c l) -> p c l", c=2 * R),
                                                    inv.unsqueeze(2).to_broadcast([P, 2 * R, N]), ALU.mult
                                                    ).then_inc(s["probs_ready"], 1)
                        if units:
                            unit(n, 5)
                        if dense or last:
                            dve.wait_ge(s["root"], after_root(n, 1, 1))
                            nc.vector.reciprocal(rstd, root).then_inc(s["rstd"], 1)
                            dve.wait_ge(s["rstd"], after_root(n, 1))
                            nc.vector.tensor_tensor(tmp, rstd, rstd, ALU.mult).then_inc(s["rstd"], 1)
                            dve.wait_ge(s["rstd"], after_root(n, 2))
                            nc.vector.tensor_tensor(tmp, tmp, variance, ALU.mult).then_inc(s["rstd"], 1)
                            dve.wait_ge(s["rstd"], after_root(n, 3))
                            nc.vector.tensor_scalar(tmp, tmp, -0.5, 1.5, ALU.mult, ALU.add).then_inc(s["rstd"], 1)
                            dve.wait_ge(s["rstd"], after_root(n, 4))
                            nc.vector.tensor_tensor(rstd, rstd, tmp, ALU.mult).then_inc(s["rstd"], 1)
                            dve.wait_ge(s["rstd"], after_root(n, 5))
                        if dense:
                            nc.vector.tensor_scalar(hn, h0, mv1[:, 0:1], rstd[:, 0:1], ALU.subtract, ALU.mult
                                                    ).then_inc(s["hn_ready"], 1)
                        if last:
                            dve.wait_ge(s["scaled"], after(old - 1))
                            nc.vector.tensor_scalar(on, psum[:, X, 0:E], mv2[:, 0:1], rstd[:, 1:2], ALU.subtract, ALU.mult
                                                    ).then_inc(s["on_ready"], 1)
                        if units:
                            unit(n, 6)
                        if maxima:
                            m = n + 2
                            dve.wait_ge(s["max_ready"], after(m - 1))
                            nc.vector.tensor_reduce(row_max.rearrange("p (r i) -> p r i", r=R),
                                                    scores_i[:, :, bass.ds((i + 2) * 2, 2), :], AX_X, ALU.max
                                                    ).then_inc(s["max_raw"], 1)
                            dve.wait_ge(s["max_raw"], after(m))
                            nc.vector.tensor_scalar(neg_max[m.slot], row_max, -1.0 / float(np.sqrt(D)), None,
                                                    ALU.mult).then_inc(s["max_ready"], 1)

                    pair_steps(dve, body)

                @block.gpsimd
                def _(pool):
                    def unit(n, k):
                        u = ORDINAL["P"][k]
                        a, v1 = a_sb[n.slot], v1_sb[n.slot]
                        buf, free = of_products(n, k, "P")
                        if k == 0:
                            pool.wait_ge(s["a_copy"], after(n))
                        pool.wait_ge(s["unit_mm"], free)
                        if UNITS[u] == "PW":
                            v2_u, a_u = w_factors(u, a)
                            nc.gpsimd.tensor_tensor(buf[:, 0:DU * N].rearrange("p (d j) -> p d j", d=DU), v2_u, a_u,
                                                    ALU.mult).then_inc(s["p_ready"], 1)
                            return
                        c = B_UNITS.index(u)
                        kb = [x_ for x_ in ORDINAL["P"] if UNITS[x_] == "PB"].index(u)
                        if kb == 0:
                            pool.wait_ge(s["v1_copy"], after(n))
                        nc.gpsimd.tensor_tensor(buf.rearrange("p (j n) -> p j n", j=JU), v2[:, c * JU:(c + 1) * JU, :],
                                                v1.unsqueeze(1).to_broadcast([P, JU, HP * D]),
                                                ALU.mult).then_inc(s["p_first"], 1)
                        pool.wait_ge(s["p_first"], after(n, NPB, kb + 1))
                        buf4 = buf.rearrange("p (j h d) -> p j h d", j=JU, h=HP)
                        a4 = a.rearrange("p (h j) -> p j h", h=H)[:, c * JU:(c + 1) * JU, 0:HP]
                        nc.gpsimd.tensor_tensor(buf4, buf4, a4.unsqueeze(3).to_broadcast([P, JU, HP, D]), ALU.mult
                                                ).then_inc(s["p_ready"], 1)

                    def body(n, maxima, prep, units, dense, last, i):
                        old = n - 2
                        if maxima and isinstance(i, int) and i == -2:
                            nc.gpsimd.memset(v1_diag, 0.0).then_inc(s["v1_diag_zero"], 1)
                        if units:
                            for k in range(NPL):
                                unit(n, k)
                        if last:
                            pool.wait_ge(s["on_ready"], after(old))
                            pool.wait_ge(out_stored[old.slot], slot_after(old - 2, 4))
                            nc.gpsimd.tensor_tensor(o_out[old.slot], on, out_g[:, :], ALU.mult).then_inc(s["scaled"], 1)
                            pool.wait_ge(s["scaled"], after(old))
                            nc.gpsimd.tensor_tensor(o_out[old.slot], o_out[old.slot], out_b[:, :], ALU.add
                                                    ).then_inc(s["out_ready"], 1)

                    pair_steps(pool, body)

        clear(nc, [weights_in, *s.values()])


def global_layer(nc, consts, x, w, xn_dram, q_dram, out):
    G = TOK // BANK
    T4 = BANK // P
    scale = float(np.float32(E) ** np.float32(-0.5))
    with ExitStack() as ctx:
        def sb(what, shape):
            return ctx.enter_context(nc.sbuf_tensor(f"global_{what}", shape, F32))

        def sem(what):
            return ctx.enter_context(nc.semaphore(f"global_{what}"))

        psum = ctx.enter_context(nc.psum_tensor("global_psum", [P, 8, BANK], F32))
        eye = consts["ident"][:, P:2 * P]
        wq, wk, wv, wp = (sb(k, [P, KC, E]) for k in ("wq", "wk", "wv", "wp"))
        bq, bk = sb("bq", [P, KC]), sb("bk", [P, KC])
        gamma, beta, bv, bp = (sb(k, [P, E]) for k in ("gamma", "beta", "bv", "bp"))
        kT, v = sb("kT", [P, KC, TOK]), sb("v", [P, KT, E])
        work = sb("work", [P, 26112])
        at = [0]

        def part(n):
            at[0] += n
            return work[:, at[0] - n:at[0]]

        x_in = [part(T4 * E).rearrange("p (t c) -> p t c", t=T4) for _ in range(2)]
        centred = part(T4 * E).rearrange("p (t c) -> p t c", t=T4)
        xn = [part(T4 * E).rearrange("p (t c) -> p t c", t=T4) for _ in range(2)]
        xnT = part(KC * BANK).rearrange("p (k n) -> p k n", k=KC)
        qT_out = [part(KC * BANK).rearrange("p (k n) -> p k n", k=KC) for _ in range(2)]
        stats, mv = part(T4 * 6), part(T4 * 2)
        rstd, root, tmp, variance = (part(T4) for _ in range(4))
        at[0] = 0
        rows = [part(TOK) for _ in range(2)]
        probsT = part(TOK)
        qT = [part(KC * P).rearrange("p (k n) -> p k n", k=KC) for _ in range(2)]
        xn_in = [part(E) for _ in range(2)]
        xn_bp = [part(E) for _ in range(2)]
        o_sb, oT = part(E), part(E)
        y = [part(E) for _ in range(2)]
        maxima, row_max = part(CHUNK), part(1)
        neg_max = [part(1) for _ in range(2)]
        EXPS = 4
        sums, total = [part(EXPS) for _ in range(2)], part(1)
        inv = [part(1) for _ in range(2)]

        toks = x.rearrange("b (g i) j c -> b g (i j) c", g=G)
        xn_toks = xn_dram.rearrange("b (g i) j c -> b g (i j) c", g=G)
        xn_tiles = xn_dram.rearrange("b (s i) j c -> b s (i j) c", i=2)
        out_tiles = out.rearrange("b (s i) j c -> b s (i j) c", i=2)

        weights_in = sem("weights_in")
        with nc.Block() as block:
            @block.sync
            def _(sp):
                n = 0
                for dst, src in ((wq, w["w_q"]), (wk, w["w_k"]), (wv, w["w_v"]), (wp, w["w_p"])):
                    sp.dma_start(dst[:, :, :], src.rearrange("(k p) n -> p k n", p=P)).then_inc(weights_in, 16)
                    n += 1
                for dst, src in ((bq, w["b_q"]), (bk, w["b_k"])):
                    sp.dma_start(dst[:, :], src.rearrange("(k p) -> p k", p=P), allow_slow_non_contiguous=True).then_inc(weights_in, 16)
                    n += 1
                for dst, src in ((gamma, w["ln_gamma"]), (beta, w["ln_beta"]), (bv, w["b_v"]), (bp, w["b_p"])):
                    sp.dma_start(dst[:, :], src.rearrange("(a n) -> a n", a=1).to_broadcast([P, E])).then_inc(weights_in, 16)
                    n += 1
                sp.wait_ge(weights_in, 16 * n)

        names = ("x_in0", "x_in1", "xn_out0", "xn_out1", "q_out0", "q_out1", "stats", "mean", "variance", "root", "rstd",
                 "centred", "scaled", "xn_ready", "xT_mm", "xT_copy", "qk_mm", "v_mm", "q_copy", "k_copy", "v_copy",
                 "qT_in0", "qT_in1", "res_in0", "res_in1", "res_ready", "scores_mm", "scores_copy",
                 "chunk_max", "row_max", "neg_max", "exp_ready", "total", "inv_ready", "pT_mm", "pT_copy",
                 "pv_mm", "o_ready", "oT_mm", "oT_copy", "proj_mm", "y_ready", "y_out0", "y_out1",
                 "settled", "sp_settled")
        s = {k: sem(k) for k in names}
        credit(nc, s.values())
        x_loaded, xn_stored, q_stored = ((s[k + "0"], s[k + "1"]) for k in ("x_in", "xn_out", "q_out"))
        qT_loaded, res_loaded, y_stored = ((s[k + "0"], s[k + "1"]) for k in ("qT_in", "res_in", "y_out"))

        with nc.Fori(0, B) as b:
            def group_steps(eng, body):
                with eng.Fori(0, G // 2) as i:
                    for u in range(2):
                        body(Step(b * (G // 2) + i, u), i * 2 + u)

            with nc.Block() as block:
                @block.sync
                def _(sp):
                    def load(g, i):
                        sp.wait_ge(s["centred"], after(g - 2, T4))
                        sp.dma_start(x_in[g.slot], toks[bass.ds(b, 1), bass.ds(i, 1)].rearrange("a g (t p) c -> p (a g t) c", p=P)
                                     ).then_inc(x_loaded[g.slot], 16)

                    def store(g, i):
                        sp.wait_ge(s["xn_ready"], after(g))
                        sp.dma_start(xn_toks[bass.ds(b, 1), bass.ds(i, 1)].rearrange("a g (t p) c -> p (a g t) c", p=P),
                                     xn[g.slot]).then_inc(xn_stored[g.slot], 16)
                        sp.wait_ge(s["q_copy"], after(g, KC))
                        for k in range(KC):
                            sp.dma_start(q_dram[bass.ds(b, 1), k, :, bass.ds(i * BANK, BANK)].rearrange("a p n -> p (a n)"),
                                         qT_out[g.slot][:, k, :]).then_inc(q_stored[g.slot], 16)

                    half = b * (G // 2)
                    load(Step(half, 0), 0)
                    load(Step(half, 1), 1)
                    with sp.Fori(0, G // 2 - 1) as i:
                        for u in range(2):
                            store(Step(half + i, u), i * 2 + u)
                            load(Step(half + i, 2 + u), i * 2 + 2 + u)
                    for g in (G - 2, G - 1):
                        store(Step(half, g), g)
                    for g in (G - 2, G - 1):
                        sp.wait_ge(xn_stored[g % 2], slot_after(Step(half, g)))
                        settle(sp, s["sp_settled"])
                        sp.wait_ge(q_stored[g % 2], slot_after(Step(half, g), KC))
                    settle(sp, s["sp_settled"])

                @block.vector
                def _(dve):
                    def body(g, i):
                        dve.wait_ge(x_loaded[g.slot], slot_after(g))
                        dve.wait_ge(s["centred"], after(g - 1, T4))
                        for t in range(T4):
                            ins = nc.vector.bn_stats(stats[:, 6 * t:6 * t + 6], x_in[g.slot][:, t, :])
                        ins.then_inc(s["stats"], 1)
                        dve.wait_ge(s["stats"], after(g))
                        settle(dve, s["settled"])
                        for t in range(T4):
                            ins = nc.vector.bn_aggr(mv[:, 2 * t:2 * t + 2], stats[:, 6 * t:6 * t + 6])
                        ins.then_inc(s["mean"], 1)
                        dve.wait_ge(s["mean"], after(g))
                        nc.vector.tensor_scalar(variance, mv.rearrange("p (t a) -> p t a", a=2)[:, :, 1], EPS_GLOBAL, None,
                                                ALU.add).then_inc(s["variance"], 1)
                        dve.wait_ge(s["root"], after(g))
                        inverse_root(dve, nc.vector, variance, root, rstd, tmp, s["rstd"], g)
                        dve.wait_ge(s["scaled"], after(g - 1))
                        for t in range(T4):
                            nc.vector.tensor_scalar(centred[:, t, :], x_in[g.slot][:, t, :], mv[:, 2 * t:2 * t + 1],
                                                    rstd[:, t:t + 1], ALU.subtract, ALU.mult).then_inc(s["centred"], 1)
                        dve.wait_ge(s["qk_mm"], after(g))
                        for k in range(KC):
                            nc.vector.tensor_scalar(kT[:, k, bass.ds(i * BANK, BANK)], psum[:, 4 + k, :], bk[:, k:k + 1],
                                                    None, ALU.add).then_inc(s["k_copy"], 1)
                        dve.wait_ge(s["v_mm"], after(g))
                        nc.vector.tensor_tensor(v[:, bass.ds(i * T4, T4), :],
                                                psum[:, 6:8, :].rearrange("p a (t c) -> p (a t) c", c=E),
                                                bv[:, :].unsqueeze(1).to_broadcast([P, T4, E]), ALU.add
                                                ).then_inc(s["v_copy"], 1)

                    group_steps(dve, body)

                @block.gpsimd
                def _(pool):
                    def body(g, i):
                        pool.wait_ge(s["centred"], after(g, T4))
                        pool.wait_ge(xn_stored[(g - 2).slot], slot_after(g - 2))
                        pool.wait_ge(s["xT_mm"], after(g - 1))
                        nc.gpsimd.tensor_tensor(xn[g.slot], centred, gamma[:, :].unsqueeze(1).to_broadcast([P, T4, E]),
                                                ALU.mult).then_inc(s["scaled"], 1)
                        pool.wait_ge(s["scaled"], after(g))
                        nc.gpsimd.tensor_tensor(xn[g.slot], xn[g.slot], beta[:, :].unsqueeze(1).to_broadcast([P, T4, E]),
                                                ALU.add).then_inc(s["xn_ready"], 1)

                    group_steps(pool, body)

                @block.tensor
                def _(pe):
                    def body(g, i):
                        pe.wait_ge(s["xn_ready"], after(g))
                        pe.wait_ge(s["xT_copy"], after(g - 1, KC))
                        for k in range(KC):
                            for t in range(T4):
                                mm = nc.tensor.transpose(psum[:, k, t * P:t * P + P], xn[g.slot][:, t, k * P:k * P + P], eye)
                        mm.then_inc(s["xT_mm"], 1)
                        pe.wait_ge(s["xT_copy"], after(g, KC))
                        pe.wait_ge(s["q_copy"], after(g - 1, KC))
                        pe.wait_ge(s["k_copy"], after(g - 1, KC))
                        for wt, bank in ((wq, 2), (wk, 4)):
                            for m in range(KC):
                                for k in range(KC):
                                    mm = nc.tensor.matmul(psum[:, bank + m, :], wt[:, k, m * P:m * P + P], xnT[:, k, :],
                                                          start=(k == 0), stop=(k == KC - 1))
                        mm.then_inc(s["qk_mm"], 1)
                        pe.wait_ge(s["v_copy"], after(g - 1))
                        for t in range(T4):
                            for k in range(KC):
                                mm = nc.tensor.matmul(psum[:, 6 + t // 2, (t % 2) * E:(t % 2 + 1) * E],
                                                      xnT[:, k, t * P:t * P + P], wv[:, k, :],
                                                      start=(k == 0), stop=(k == KC - 1))
                        mm.then_inc(s["v_mm"], 1)

                    group_steps(pe, body)

                @block.scalar
                def _(act):
                    def body(g, i):
                        act.wait_ge(s["variance"], after(g))
                        nc.scalar.activation(root, variance, ACT.Sqrt).then_inc(s["root"], 1)
                        act.wait_ge(s["xT_mm"], after(g))
                        act.wait_ge(s["v_mm"], after(g - 1))
                        for k in range(KC):
                            nc.scalar.activation(xnT[:, k, :], psum[:, k, :], ACT.Copy).then_inc(s["xT_copy"], 1)
                        act.wait_ge(s["qk_mm"], after(g))
                        act.wait_ge(q_stored[(g - 2).slot], slot_after(g - 2, KC))
                        for k in range(KC):
                            nc.scalar.activation(qT_out[g.slot][:, k, :], psum[:, 2 + k, :], ACT.Identity,
                                                 bias=bq[:, k:k + 1]).then_inc(s["q_copy"], 1)

                    group_steps(act, body)

            SB, TB, O, X, Y = (0, 1), (2, 3), (4, 5), 6, 7
            ORDER = "S0 S1 T0 S2 T1 V0 S3 T2 V1 S4 T3 V2 S5 S6 T4 V3 S7 T5 V4 T6 V5 T7 V6 V7".split()
            HALF = KT // 2

            def tile_steps(eng, body):
                half = b * HALF
                body(Step(half, -1), True, False, False, -1)
                body(Step(half, 0), True, True, False, 0)
                with eng.Fori(0, HALF - 1) as i:
                    for u in range(2):
                        body(Step(half + i, 1 + u), True, True, True, i * 2 + 1 + u)
                body(Step(half, KT - 1), False, True, True, KT - 1)
                body(Step(half, KT), False, False, True, KT)

            with nc.Block() as block:
                @block.sync
                def _(sp):
                    def load(m, i):
                        sp.wait_ge(s["scores_mm"], after(m - 2, CHUNK))
                        sp.dma_start(qT[m.slot], q_dram[bass.ds(b, 1), :, :, bass.ds(i * P, P)].rearrange("a k p n -> p (a k) n")
                                     ).then_inc(qT_loaded[m.slot], 16)

                    def load_res(m, i):
                        sp.wait_ge(s["res_ready"], after(m - 2))
                        sp.dma_start(xn_in[m.slot], xn_tiles[bass.ds(b, 1), bass.ds(i, 1)].rearrange("a s p c -> p (a s c)")
                                     ).then_inc(res_loaded[m.slot], 16)

                    def store(m, i):
                        sp.wait_ge(s["y_ready"], after(m))
                        sp.dma_start(out_tiles[bass.ds(b, 1), bass.ds(i, 1)].rearrange("a s p c -> p (a s c)"),
                                     y[m.slot]).then_inc(y_stored[m.slot], 16)

                    half = b * HALF
                    for m in range(2):
                        load(Step(half, m), m)
                        load_res(Step(half, m), m)
                    with sp.Fori(0, HALF - 1) as i:
                        for u in range(2):
                            load(Step(half + i, 2 + u), i * 2 + 2 + u)
                            load_res(Step(half + i, 2 + u), i * 2 + 2 + u)
                            store(Step(half + i, u), i * 2 + u)
                    for m in (KT - 2, KT - 1):
                        store(Step(half, m), m)
                    for m in (KT - 2, KT - 1):
                        sp.wait_ge(y_stored[m % 2], slot_after(Step(half, m)))
                    settle(sp, s["sp_settled"])

                @block.tensor
                def _(pe):
                    def body(n, scores, probs, dense, i):
                        nxt, prv = n + 1, n - 1

                        def run(what, c):
                            if what == "S" and scores:
                                if c == 0:
                                    pe.wait_ge(qT_loaded[nxt.slot], slot_after(nxt))
                                if c >= 2:
                                    pe.wait_ge(s["scores_copy"], after(nxt, CHUNK, c - 1))
                                else:
                                    pe.wait_ge(s["scores_copy"], after(nxt - 1, CHUNK, CHUNK + c - 1))
                                for k in range(KC):
                                    mm = nc.tensor.matmul(psum[:, SB[c % 2], :], qT[nxt.slot][:, k, :],
                                                          kT[:, k, c * BANK:(c + 1) * BANK], start=(k == 0), stop=(k == KC - 1))
                                mm.then_inc(s["scores_mm"], 1)
                            if what == "T" and probs:
                                pe.wait_ge(s["exp_ready"], after(n, EXPS, c * EXPS // CHUNK + 1))
                                if c >= 2:
                                    pe.wait_ge(s["pT_copy"], after(n, CHUNK, c - 1))
                                else:
                                    pe.wait_ge(s["pT_copy"], after(n - 1, CHUNK, CHUNK + c - 1))
                                for t in range(T4):
                                    mm = nc.tensor.transpose(psum[:, TB[c % 2], t * P:t * P + P],
                                                             rows[n.slot][:, c * BANK + t * P:c * BANK + (t + 1) * P], eye)
                                mm.then_inc(s["pT_mm"], 1)
                            if what == "V" and probs:
                                if c == 0:
                                    pe.wait_ge(s["o_ready"], after(n - 2))
                                pe.wait_ge(s["pT_copy"], after(n, CHUNK, c + 1))
                                for t in range(T4):
                                    kt = c * T4 + t
                                    mm = nc.tensor.matmul(psum[:, O[n.slot], 0:E], probsT[:, kt * P:kt * P + P], v[:, kt, :],
                                                          start=(kt == 0), stop=(kt == KT - 1))
                                mm.then_inc(s["pv_mm"], 1)

                        for at_, op in enumerate(ORDER):
                            run(op[0], int(op[1:]))
                            if dense and op == "T1":
                                pe.wait_ge(s["o_ready"], after(prv))
                                pe.wait_ge(s["oT_copy"], after(prv - 1))
                                for k in range(KC):
                                    mm = nc.tensor.transpose(psum[:, X, k * P:k * P + P], o_sb[:, k * P:k * P + P], eye)
                                mm.then_inc(s["oT_mm"], 1)
                            if dense and op == "T3":
                                pe.wait_ge(s["oT_copy"], after(prv))
                                pe.wait_ge(s["y_ready"], after(prv - 1))
                                for k in range(KC):
                                    mm = nc.tensor.matmul(psum[:, Y, 0:E], oT[:, k * P:k * P + P], wp[:, k, :],
                                                          start=(k == 0), stop=(k == KC - 1))
                                mm.then_inc(s["proj_mm"], 1)

                    tile_steps(pe, body)

                @block.scalar
                def _(act):
                    def body(n, scores, probs, dense, i):
                        nxt, prv = n + 1, n - 1
                        for c in range(CHUNK):
                            if scores:
                                act.wait_ge(s["scores_mm"], after(nxt, CHUNK, c + 1))
                                if c == 0:
                                    act.wait_ge(s["pT_mm"], after(nxt - 2, CHUNK))
                                nc.scalar.activation(rows[nxt.slot][:, c * BANK:(c + 1) * BANK], psum[:, SB[c % 2], :],
                                                     ACT.Copy).then_inc(s["scores_copy"], 1)
                            if dense and c == 3:
                                act.wait_ge(s["oT_mm"], after(prv))
                                act.wait_ge(s["proj_mm"], after(prv - 1))
                                nc.scalar.activation(oT, psum[:, X, 0:E], ACT.Copy).then_inc(s["oT_copy"], 1)
                        if scores:
                            act.wait_ge(s["neg_max"], after(nxt))
                            for e in range(EXPS):
                                part_ = rows[nxt.slot][:, e * (TOK // EXPS):(e + 1) * (TOK // EXPS)]
                                nc.scalar.activation(part_, part_, ACT.Exp, bias=neg_max[nxt.slot], scale=scale,
                                                     accum_out=sums[nxt.slot][:, e:e + 1]).then_inc(s["exp_ready"], 1)

                    tile_steps(act, body)

                @block.vector
                def _(dve):
                    def body(n, scores, probs, dense, i):
                        nxt, prv = n + 1, n - 1
                        if dense:
                            dve.wait_ge(s["total"], after(prv))
                            dve.wait_ge(s["pv_mm"], after(prv, CHUNK))
                            dve.wait_ge(s["oT_mm"], after(prv - 1))
                            nc.vector.tensor_scalar(o_sb, psum[:, O[prv.slot], 0:E], inv[prv.slot], None, ALU.mult
                                                    ).then_inc(s["o_ready"], 1)
                        for at_, op in enumerate(ORDER):
                            what, c = op[0], int(op[1:])
                            if what == "S" and scores:
                                dve.wait_ge(s["scores_copy"], after(nxt, CHUNK, c + 1))
                                nc.vector.tensor_reduce(maxima[:, c:c + 1], rows[nxt.slot][:, c * BANK:(c + 1) * BANK],
                                                        AX_X, ALU.max).then_inc(s["chunk_max"], 1)
                                if c == CHUNK - 1:
                                    dve.wait_ge(s["chunk_max"], after(nxt, CHUNK))
                                    nc.vector.tensor_reduce(row_max, maxima, AX_X, ALU.max).then_inc(s["row_max"], 1)
                                    dve.wait_ge(s["row_max"], after(nxt))
                                    nc.vector.tensor_scalar(neg_max[nxt.slot], row_max, -scale, None, ALU.mult
                                                            ).then_inc(s["neg_max"], 1)
                            if what == "T" and probs:
                                dve.wait_ge(s["pT_mm"], after(n, CHUNK, c + 1))
                                dve.wait_ge(s["pv_mm"], after(n - 1, CHUNK, c + 1))
                                nc.vector.tensor_copy(probsT[:, c * BANK:(c + 1) * BANK], psum[:, TB[c % 2], :]
                                                      ).then_inc(s["pT_copy"], 1)
                            if dense and op == "T4":
                                dve.wait_ge(s["proj_mm"], after(prv))
                                dve.wait_ge(s["res_ready"], after(prv))
                                dve.wait_ge(y_stored[(prv - 2).slot], slot_after(prv - 2))
                                nc.vector.tensor_tensor(y[prv.slot], psum[:, Y, 0:E], xn_bp[prv.slot], ALU.add
                                                        ).then_inc(s["y_ready"], 1)
                        if probs:
                            dve.wait_ge(s["exp_ready"], after(n, EXPS))
                            nc.vector.tensor_reduce(total, sums[n.slot], AX_X, ALU.add).then_inc(s["inv_ready"], 1)
                            dve.wait_ge(s["inv_ready"], after(n))
                            nc.vector.reciprocal(inv[n.slot], total).then_inc(s["total"], 1)

                    tile_steps(dve, body)

                @block.gpsimd
                def _(pool):
                    with pool.Fori(0, HALF) as i:
                        for u in range(2):
                            m = Step(b * HALF + i, u)
                            pool.wait_ge(res_loaded[m.slot], slot_after(m))
                            pool.wait_ge(s["y_ready"], after(m - 1 - u))
                            nc.gpsimd.tensor_tensor(xn_bp[m.slot], xn_in[m.slot], bp[:, :], ALU.add
                                                    ).then_inc(s["res_ready"], 1)

        clear(nc, [weights_in, *s.values()])


def conv_layer(nc, consts, x, taps, out):
    G = N // 8
    NP = N + 2
    with ExitStack() as ctx:
        def sb(what, shape):
            return ctx.enter_context(nc.sbuf_tensor(f"conv_{what}", shape, F32))

        def sem(what):
            return ctx.enter_context(nc.semaphore(f"conv_{what}"))

        psum = ctx.enter_context(nc.psum_tensor("conv_psum", [P, 8, BANK], F32))
        eye = consts["ident"][:, P:2 * P]
        tap = sb("tap", [P, KC, 9])
        image = sb("image", [P, KC, NP * NP])
        x_in = [sb(f"x_in{k}", [P, 4, E]) for k in range(2)]
        acc = [sb(f"acc{k}", [P, KC, BANK]) for k in range(2)]
        tile = [sb(f"tile{k}", [P, 4, E]) for k in range(2)]
        img = image[:, :, :].rearrange("p k (r c) -> p k r c", c=NP)
        names = ("taps_in", "cleared", "x_in0", "x_in1", "xT_mm", "image_copy", "summed", "back_mm", "back_copy", "out0", "out1", "sp_settled")
        s = {k: sem(k) for k in names}
        credit(nc, s.values())
        x_loaded, stored = (s["x_in0"], s["x_in1"]), (s["out0"], s["out1"])
        toks = x.rearrange("b (g i) j c -> b g (i j) c", g=G)
        out_toks = out.rearrange("b (g i) j c -> b g (i j) c", g=G)
        with nc.Block() as block:
            @block.sync
            def _(sp):
                for k in range(KC):
                    sp.dma_start(tap[:, k, :], taps.rearrange("a b (k p) -> k p (a b)", p=P)[k], allow_slow_non_contiguous=True).then_inc(s["taps_in"], 16)
                sp.wait_ge(s["taps_in"], 16 * KC + CREDIT)

            @block.gpsimd
            def _(pool):
                nc.gpsimd.memset(image[:, :, :], 0.0).then_inc(s["cleared"], 1)
                pool.wait_ge(s["cleared"], 1 + CREDIT)

        with nc.Fori(0, B) as b:
            half = b * (G // 2)
            with nc.Block() as block:
                def steps(eng, body):
                    with eng.Fori(0, G // 2) as i:
                        for u in range(2):
                            body(Step(half + i, u), i * 2 + u)

                @block.sync
                def _(sp):
                    def body(g, i):
                        sp.wait_ge(s["xT_mm"], after(g - 1))
                        sp.dma_start(x_in[g.slot][:, :, :], toks[bass.ds(b, 1), bass.ds(i, 1)].rearrange("a g (t p) c -> p (a g t) c", p=P)
                                     ).then_inc(x_loaded[g.slot], 16)
                    steps(sp, body)

                @block.tensor
                def _(pe):
                    def body(g, i):
                        pe.wait_ge(x_loaded[g.slot], slot_after(g))
                        pe.wait_ge(s["image_copy"], after(g - 1, KC))
                        for k in range(KC):
                            for t in range(4):
                                mm = nc.tensor.transpose(psum[:, 2 * g.slot + k, t * P:t * P + P], x_in[g.slot][:, t, k * P:k * P + P], eye)
                        mm.then_inc(s["xT_mm"], 1)
                    steps(pe, body)

                @block.scalar
                def _(act):
                    def body(g, i):
                        act.wait_ge(s["xT_mm"], after(g))
                        for k in range(KC):
                            nc.scalar.activation(img[:, k, bass.ds(i * 8 + 1, 8), 1:N + 1],
                                                 psum[:, 2 * g.slot + k, :].rearrange("p (r c) -> p r c", c=N), ACT.Copy
                                                 ).then_inc(s["image_copy"], 1)
                    steps(act, body)

            with nc.Block() as block:
                def steps(eng, body):
                    with eng.Fori(0, G // 2) as i:
                        for u in range(2):
                            body(Step(half + i, u), i * 2 + u)

                TAPS = [(dy, dx) for dy in range(3) for dx in range(3) if (dy, dx) != (1, 1)]

                @block.vector
                def _(dve):
                    def body(g, i):
                        dve.wait_ge(s["back_mm"], after(g - 1))
                        for a, (dy, dx) in enumerate(TAPS):
                            for k in range(KC):
                                to = acc[g.slot][:, k, :].rearrange("p (r c) -> p r c", c=N)
                                plus = img[:, k, bass.ds(i * 8 + 1, 8), 1:N + 1] if a == 0 else to
                                if a:
                                    dve.wait_ge(s["summed"], after(g, 16, (a - 1) * KC + k + 1))
                                nc.vector.scalar_tensor_tensor(
                                    out=to, in0=img[:, k, bass.ds(i * 8 + dy, 8), dx:dx + N],
                                    scalar=tap[:, k, dy * 3 + dx:dy * 3 + dx + 1], in1=plus,
                                    op0=ALU.mult, op1=ALU.add).then_inc(s["summed"], 1)
                    steps(dve, body)

                @block.tensor
                def _(pe):
                    def body(g, i):
                        pe.wait_ge(s["summed"], after(g, 16))
                        pe.wait_ge(s["back_copy"], after(g - 1))
                        for t in range(4):
                            for k in range(KC):
                                mm = nc.tensor.transpose(psum[:, 4 + 2 * g.slot + t // 2, (t % 2) * E + k * P:(t % 2) * E + k * P + P],
                                                         acc[g.slot][:, k, t * P:t * P + P], eye)
                        mm.then_inc(s["back_mm"], 1)
                    steps(pe, body)

                @block.scalar
                def _(act):
                    def body(g, i):
                        act.wait_ge(s["back_mm"], after(g))
                        act.wait_ge(stored[(g - 2).slot], slot_after(g - 2))
                        nc.scalar.activation(tile[g.slot][:, :, :].rearrange("p t c -> p (t c)"),
                                             psum[:, 4 + 2 * g.slot:6 + 2 * g.slot, :].rearrange("p a n -> p (a n)"), ACT.Copy
                                             ).then_inc(s["back_copy"], 1)
                    steps(act, body)

                @block.sync
                def _(sp):
                    def body(g, i):
                        sp.wait_ge(s["back_copy"], after(g))
                        sp.dma_start(out_toks[bass.ds(b, 1), bass.ds(i, 1)].rearrange("a g (t p) c -> p (a g t) c", p=P),
                                     tile[g.slot][:, :, :]).then_inc(stored[g.slot], 16)
                    steps(sp, body)
                    for g in (G - 2, G - 1):
                        sp.wait_ge(stored[g % 2], slot_after(Step(half, g)))
                    settle(sp, s["sp_settled"])


def conv_seq_kernel(nc, x, l0, l1, l2, taps, ident, pick, out):
    x1, x2, x3, xn = (nc.dram_tensor(k, (B, N, N, E), F32).ap() for k in ("x1", "x2", "x3", "xn"))
    q_dram = nc.dram_tensor("qT", (B, KC, P, TOK), F32).ap()
    with ExitStack() as ctx:
        consts = {k: ctx.enter_context(nc.sbuf_tensor(k, shape, F32))
                  for k, shape in (("ident", [P, 3 * P]), ("pick", [P, 62]), ("ones_row", [1, P]))}
        consts_in = ctx.enter_context(nc.semaphore("consts_in"))
        with nc.Block() as block:
            @block.sync
            def _(sp):
                sp.dma_start(consts["ident"][:, :], ident).then_inc(consts_in, 16)
                sp.dma_start(consts["pick"][:, :], pick).then_inc(consts_in, 16)
                sp.wait_ge(consts_in, 32)

            @block.vector
            def _(dve):
                nc.vector.memset(consts["ones_row"][:, :], 1.0)

        triangle_layer(nc, consts, x, l0, x1, "tri0")
        global_layer(nc, consts, x1, l1, xn, q_dram, x2)
        triangle_layer(nc, consts, x2, l2, x3, "tri2")
        conv_layer(nc, consts, x3, taps, out)


_TRI = ("Wq", "Wk", "Wv1", "Wv2", "Wo", "ln_agg_g", "ln_agg_b", "W1", "b1", "W2", "b2", "ln_out_g", "ln_out_b")
_GLOBAL = ("ln_gamma", "ln_beta", "w_q", "b_q", "w_k", "b_k", "w_v", "b_v", "w_p", "b_p")


def kernel(**inputs):
    import concourse.bacc as bacc
    from concourse.bass_utils import run_bass_kernel_spmd

    nc = bacc.Bacc("TRN2", target_bir_lowering=False, num_devices=1)
    arrays = {f"in_{k}": np.ascontiguousarray(v) for k, v in inputs.items()}
    ident = np.zeros((P, 3 * P), np.float32)
    ident[:, P:2 * P] = np.eye(P, dtype=np.float32)
    pick = np.zeros((P, 62), np.float32)
    pick[:N, 30] = 1.0
    pick[N:, 31] = 1.0
    arrays["in_ident"], arrays["in_pick"] = ident, pick
    ap = {k: nc.dram_tensor(k, a.shape, mybir.dt.from_np(a.dtype), kind="ExternalInput").ap() for k, a in arrays.items()}
    out = nc.dram_tensor("out", (B, N, N, E), F32, kind="ExternalOutput").ap()
    conv_seq_kernel(nc, ap["in_x"], {k: ap[f"in_L0_conv_{k}"] for k in _TRI}, {k: ap[f"in_L1_conv_{k}"] for k in _GLOBAL},
                    {k: ap[f"in_L2_conv_{k}"] for k in _TRI}, ap["in_L3_conv_kernel"], ap["in_ident"], ap["in_pick"], out)
    return run_bass_kernel_spmd(nc, [arrays], core_ids=[0]).results[0]["out"]
```

```python
from contextlib import ExitStack

import numpy as np

import concourse.bass as bass
from concourse import mybir

F32 = mybir.dt.float32
F32R = mybir.dt.float32r
ALU = mybir.AluOpType
ACT = mybir.ActivationFunctionType
AX_X = mybir.AxisListType.X

P = 128
B, N, E, H = 2, 64, 256, 8
D = E // H
KC = E // P
F = 2 * E
FC = F // P
R = P // D
BANK = 512
PAIRS = N // 2
GROUPS = N // 4
HW = 2
HP = H - HW
JU = 8
DU = 16
EPS_TRI = 1e-5
EPS_GLOBAL = 1e-3
TOK = N * N
KT = TOK // P
CHUNK = TOK // BANK


class Step:

    def __init__(self, half, odd):
        self.half, self.odd = half, odd

    def __add__(self, k):
        return Step(self.half, self.odd + k)

    def __sub__(self, k):
        return self + -k

    @property
    def slot(self):
        return self.odd % 2

    @property
    def pair(self):
        return self.half + self.odd // 2

    @property
    def number(self):
        return self.half * 2 + self.odd


CREDIT = 32


def after(step, per=1, nth=None):
    return step.number * per + (per if nth is None else nth) + CREDIT


def slot_after(step, dmas=1):
    return (step.pair + 1) * (16 * dmas) + CREDIT


def credit(nc, sems):
    with nc.Block() as block:
        @block.gpsimd
        def _(pool):
            for sem in sems:
                pool.sem_inc(sem, CREDIT)


def clear(nc, sems):
    with nc.Block() as block:
        @block.gpsimd
        def _(pool):
            for sem in sems:
                pool.sem_clear(sem)


def settle(eng, sem):
    eng.sem_inc(sem, 1)


def inverse_root(eng, lib, variance, root, to, tmp, sem, step):
    lib.reciprocal(to, root).then_inc(sem, 1)
    eng.wait_ge(sem, after(step, 5, 1))
    lib.tensor_tensor(tmp, to, to, ALU.mult).then_inc(sem, 1)
    eng.wait_ge(sem, after(step, 5, 2))
    lib.tensor_tensor(tmp, tmp, variance, ALU.mult).then_inc(sem, 1)
    eng.wait_ge(sem, after(step, 5, 3))
    lib.tensor_scalar(tmp, tmp, -0.5, 1.5, ALU.mult, ALU.add).then_inc(sem, 1)
    eng.wait_ge(sem, after(step, 5, 4))
    lib.tensor_tensor(to, to, tmp, ALU.mult).then_inc(sem, 1)
    eng.wait_ge(sem, after(step, 5))


def high_part(lib, to, of):
    return lib.tensor_copy(to, of)


def triangle_layer(nc, consts, x, w, out, name):
    with ExitStack() as ctx:
        def sb(what, shape):
            return ctx.enter_context(nc.sbuf_tensor(f"{name}_{what}", shape, F32))

        def sem(what):
            return ctx.enter_context(nc.semaphore(f"{name}_{what}"))

        psum = ctx.enter_context(nc.psum_tensor(f"{name}_psum", [P, 8, BANK], F32))
        ident, pick, ones_row = consts["ident"], consts["pick"], consts["ones_row"]
        eye = ident[:, P:2 * P]

        wv1, wo = (sb(k, [P, KC, E]) for k in ("wv1", "wo"))
        w1, w2 = sb("w1", [P, KC, F]), sb("w2", [P, FC, E])
        agg_g, agg_b, b1 = sb("agg_g", [P, KC]), sb("agg_b", [P, KC]), sb("b1", [P, FC])
        out_g, out_b, b2 = sb("out_g", [P, E]), sb("out_b", [P, E]), sb("b2", [1, E])
        v2 = sb("v2", [P, N, HP * D])
        v2_w = sb("v2_w", [P, HW * D, N])
        scores = sb("scores", [P, R * N, N])
        scores_i = scores[:, :, :].rearrange("p (r i) l -> p r i l", r=R)

        work = sb("work", [P, 15872])
        at = [0]

        def part(n):
            at[0] += n
            return work[:, at[0] - n:at[0]]

        x_row = [part(2 * E).rearrange("p (t c) -> p t c", t=2) for _ in range(2)]
        x_col = [part(2 * E).rearrange("p (t c) -> p t c", t=2) for _ in range(2)]
        rowT = part(KC * 2 * P).rearrange("p (k n) -> p k n", k=KC)
        colT = [part(KC * 4 * N).rearrange("p (k n) -> p k n", k=KC) for _ in range(2)]
        kT = [part(2 * 2 * P).rearrange("p (t n) -> p t n", t=2) for _ in range(2)]
        q_diag_all = part(2 * 2 * 4 * R * N)
        q_diag = [q_diag_all[:, k * 8 * R * N:(k + 1) * 8 * R * N].rearrange("p (t l r i) -> p t l r i", t=2, l=4, r=R)
                  for k in range(2)]
        wq, wk, wv2 = (part(KC * E).rearrange("p (k n) -> p k n", k=KC) for _ in range(3))
        group_max = part(R * N)
        at[0] = 0
        prod_d = [part(JU * HP * D) for _ in range(2)]
        prod_p = [part(JU * HP * D) for _ in range(2)]
        v1_diag = part(HW * D * 2 * D)
        v1_diag_hd = v1_diag.rearrange("p (h c) -> p h c", h=HW)
        probs = part(2 * R * N)
        a_sb = [part(BANK) for _ in range(2)]
        v1_sb = [part(HP * D) for _ in range(2)]
        x_pair = [part(E) for _ in range(2)]
        x_res = [part(E) for _ in range(2)]
        x_pairT, oT, hn, hT, on = (part(E) for _ in range(5))
        o_sb = part(HP * D)
        h0 = hn
        reluT = part(F)
        o_out = part(E)
        neg_max = part(R * N)
        neg_max_i = neg_max.rearrange("p (r i) -> p r i", r=R)
        small = sb("small", [P, 80])
        sums = [small[:, 16 + 8 * k:24 + 8 * k] for k in range(2)]
        inv = small[:, 40:48]
        stats1, stats2, mv1, mv2 = small[:, 48:54], small[:, 54:60], small[:, 60:62], small[:, 62:64]
        both_vars = small[:, 60:64].rearrange("p (a b) -> p a b", a=2)[:, :, 1]
        variance, root, rstd, tmp = (small[:, 64 + 2 * k:66 + 2 * k] for k in range(4))

        x_toks = x.rearrange("b (s i) j c -> b s (i j) c", i=2)
        x_cols = x.rearrange("b r (s j) c -> b s j r c", j=2)
        x_grid = x.rearrange("b (s i) (t g) c -> b s g t i c", i=2, g=4)
        out_grid = out.rearrange("b (s i) (t g) c -> b s g t i c", i=2, g=4)

        weights_in = sem("weights_in")
        WEIGHTS = 10
        with nc.Block() as block:
            @block.sync
            def _(sp):
                for dst, src in ((wv1, w["Wv1"]), (wo, w["Wo"]), (w1, w["W1"]), (w2, w["W2"])):
                    sp.dma_start(dst[:, :, :], src.rearrange("(k p) n -> p k n", p=P)).then_inc(weights_in, 16)
                for dst, src in ((agg_g, w["ln_agg_g"]), (agg_b, w["ln_agg_b"]), (b1, w["b1"])):
                    sp.dma_start(dst[:, :], src.rearrange("(k p) -> p k", p=P), allow_slow_non_contiguous=True).then_inc(weights_in, 16)
                for dst, src in ((out_g, w["ln_out_g"]), (out_b, w["ln_out_b"])):
                    sp.dma_start(dst[:, :], src.rearrange("(a n) -> a n", a=1).to_broadcast([P, E])).then_inc(weights_in, 16)
                sp.dma_start(b2[:, :], w["b2"].rearrange("(a n) -> a n", a=1)).then_inc(weights_in, 16)

        names = ("qkv_in", "rows_in0", "rows_in1", "cols_in0", "cols_in1", "diag_zero", "xT_mm", "rowT_copy",
                 "colT_copy", "v2_mm", "v2_copy", "qk_mm", "kT_copy", "q0_copy", "q1_copy",
                 "scores_mm", "scores_copy", "group_max", "maxima",
                 "pair_in0", "pair_in1", "res_in0", "res_in1", "v1_diag_zero", "small_set", "pairT_mm",
                 "pairT_copy", "v1_mm", "v1_copy", "exp_ready", "inv_ready",
                 "probs_ready", "a_mm", "a_copy", "d_first", "d_ready", "p_first", "p_ready", "unit_mm",
                 "o_copy", "ow_copy", "oT_mm", "oT_copy", "wo_mm", "h0_ready", "stats1", "mean1", "stats2",
                 "mean2", "variance", "root", "rstd", "hn_ready", "hT_mm", "hT_copy", "w1_mm",
                 "relu_ready", "w2_mm", "on_ready", "scaled", "out_ready", "out_stored",
                 "settled", "sp_settled")
        s = {k: sem(k) for k in names}
        credit(nc, s.values())
        rows_in, cols_in = (s["rows_in0"], s["rows_in1"]), (s["cols_in0"], s["cols_in1"])
        pair_in, res_in = (s["pair_in0"], s["pair_in1"]), (s["res_in0"], s["res_in1"])

        with nc.Fori(0, B) as b:
            def group_steps(eng, body):
                half = b * (GROUPS // 2)
                body(Step(half, -1), None)
                for g in range(2):
                    body(Step(half, g), (0, g))
                with eng.Fori(0, GROUPS // 2 - 2) as i:
                    for u in range(2):
                        body(Step(half + i, 2 + u), (i, 2 + u))
                for g in (GROUPS - 2, GROUPS - 1):
                    body(Step(half, g), (0, g))

            with nc.Block() as block:
                t_bank, qk_bank = (0, 1), (2, 3)
                v2_psum = psum[:, 4, :].rearrange("p (a n) -> p a n", a=2)
                s_psum = psum[:, 6:8, :].rearrange("p a n -> p (a n)")

                @block.sync
                def _(sp):
                    def load(g, i):
                        sp.wait_ge(s["xT_mm"], after(g - 2))
                        for t in range(2):
                            sp.dma_start(x_row[g.slot][:, t, :],
                                         x_toks[bass.ds(b, 1), bass.ds(i * 2 + t, 1)].rearrange("a s p c -> p (a s c)")
                                         ).then_inc(rows_in[g.slot], 16)
                            for j in range(2):
                                sp.dma_start(x_col[g.slot][N * j:N * j + N, t, :],
                                             x_cols[bass.ds(b, 1), bass.ds(i * 2 + t, 1), j].rearrange("a s r c -> r (a s c)")
                                             ).then_inc(cols_in[g.slot], 16)

                    half = b * (GROUPS // 2)
                    load(Step(half, 0), 0)
                    for dst, src in ((wq, w["Wq"]), (wk, w["Wk"]), (wv2, w["Wv2"])):
                        sp.dma_start(dst, src.rearrange("(k p) n -> p k n", p=P)).then_inc(s["qkv_in"], 16)
                    load(Step(half, 1), 1)
                    with sp.Fori(0, GROUPS // 2 - 1) as i:
                        for u in range(2):
                            load(Step(half + i, 2 + u), i * 2 + 2 + u)
                    sp.wait_ge(weights_in, 16 * WEIGHTS)
                    settle(sp, s["sp_settled"])

                @block.gpsimd
                def _(pool):
                    nc.gpsimd.memset(q_diag_all, 0.0).then_inc(s["diag_zero"], 1)

                @block.tensor
                def _(pe):
                    def body(g, where):
                        nxt = g + 1
                        if where is None or g.odd < GROUPS - 1:
                            pe.wait_ge(rows_in[nxt.slot], slot_after(nxt, 2))
                            pe.wait_ge(cols_in[nxt.slot], slot_after(nxt, 4))
                            pe.wait_ge(s["rowT_copy"], after(nxt - 1))
                            pe.wait_ge(s["colT_copy"], after(nxt - 1))
                            for bank, src in ((t_bank[0], x_row[nxt.slot]), (t_bank[1], x_col[nxt.slot])):
                                for k in range(KC):
                                    for t in range(2):
                                        c = (k * 2 + t) * P
                                        mm = nc.tensor.transpose(psum[:, bank, c:c + P], src[:, t, k * P:k * P + P], eye)
                            mm.then_inc(s["xT_mm"], 1)
                        if where is not None:
                            pe.wait_ge(s["v2_copy"], after(g - 1))
                            for a in range(2):
                                for k in range(KC):
                                    mm = nc.tensor.matmul(v2_psum[:, a, :], colT[g.slot][:, k, a * P:(a + 1) * P],
                                                          wv2[:, k, :], start=(k == 0), stop=(k == KC - 1))
                            mm.then_inc(s["v2_mm"], 1)
                        if where is None or g.odd < GROUPS - 1:
                            if where is None:
                                pe.wait_ge(s["qkv_in"], (b + 1) * 48 + CREDIT)
                            pe.wait_ge(s["rowT_copy"], after(nxt))
                            pe.wait_ge(s["colT_copy"], after(nxt))
                            pe.wait_ge(s["kT_copy"], after(nxt - 1))
                            pe.wait_ge(s["q0_copy"], after(nxt - 1))
                            pe.wait_ge(s["q1_copy"], after(nxt - 1))
                            for bank, wt, src in ((qk_bank[0], wq, colT[nxt.slot]),
                                                  (qk_bank[1], wk, rowT[:, :, :])):
                                for t in range(2):
                                    for k in range(KC):
                                        mm = nc.tensor.matmul(psum[:, bank, t * 2 * P:(t + 1) * 2 * P],
                                                              wt[:, k, t * P:t * P + P], src[:, k],
                                                              start=(k == 0), stop=(k == KC - 1))
                            mm.then_inc(s["qk_mm"], 1)
                        if where is not None:
                            pe.wait_ge(s["kT_copy"], after(g))
                            pe.wait_ge(s["q0_copy"], after(g))
                            pe.wait_ge(s["q1_copy"], after(g))
                            pe.wait_ge(s["scores_copy"], after(g - 1))
                            for l in range(4):
                                for t in range(2):
                                    mm = nc.tensor.matmul(s_psum[N * t:N * t + N, l * R * N:(l + 1) * R * N],
                                                          kT[g.slot][:, t, l * N:l * N + N],
                                                          q_diag[g.slot][:, t, l].rearrange("p r i -> p (r i)"),
                                                          start=True, stop=True)
                            mm.then_inc(s["scores_mm"], 1)

                    group_steps(pe, body)

                @block.scalar
                def _(act):
                    def body(g, where):
                        nxt = g + 1
                        if where is None or g.odd < GROUPS - 1:
                            act.wait_ge(s["xT_mm"], after(nxt))
                            act.wait_ge(s["qk_mm"], after(nxt - 1))
                            nc.scalar.activation(rowT[:, :, :], psum[:, t_bank[0], :].rearrange("p (k n) -> p k n", k=KC),
                                                 ACT.Copy).then_inc(s["rowT_copy"], 1)
                        if where is not None:
                            i, u = where
                            act.wait_ge(s["v2_mm"], after(g))
                            for odd in range(2):
                                of = v2_psum[N * odd:N * odd + N, :, :]
                                for twice in range(2):
                                    rows = slice(N * twice, N * twice + N)
                                    to = v2[rows, bass.ds((i * 2 + u) * 4, 4), :].rearrange("p (a b) n -> p b a n", b=2)[:, odd]
                                    to_w = v2_w[rows, :, bass.ds((i * 2 + u) * 4, 4)].rearrange("p n (a b) -> p b n a", b=2)[:, odd]
                                    nc.scalar.activation(to, of[:, :, 0:HP * D], ACT.Copy)
                                    ins = nc.scalar.activation(to_w, of[:, :, HP * D:E].rearrange("p a n -> p n a"), ACT.Copy)
                            ins.then_inc(s["v2_copy"], 1)
                        if where is None or g.odd < GROUPS - 1:
                            act.wait_ge(s["qk_mm"], after(nxt))
                            act.wait_ge(s["scores_mm"], after(nxt - 2))
                            nc.scalar.activation(kT[nxt.slot][:, :, :],
                                                 psum[:, qk_bank[1], :].rearrange("p (t n) -> p t n", t=2),
                                                 ACT.Copy).then_inc(s["kT_copy"], 1)
                            if where is None:
                                act.wait_ge(s["diag_zero"], b + 1 + CREDIT)
                            for r in range(2):
                                ins = q_copy(nc.scalar, nxt, r)
                            ins.then_inc(s["q0_copy"], 1)
                        if where is not None:
                            act.wait_ge(s["scores_mm"], after(g))
                            nc.scalar.activation(scores[:, :, bass.ds((i * 2 + u) * 4, 4)],
                                                 s_psum.rearrange("p (l n) -> p n l", l=4), ACT.Copy
                                                 ).then_inc(s["scores_copy"], 1)

                    def q_copy(eng, g, r):
                        rows = slice(D * r, D * r + D)
                        return eng.activation(q_diag[g.slot][rows, :, :, r, :],
                                              psum[rows, qk_bank[0], :].rearrange("p (t l i) -> p t l i", t=2, l=4),
                                              ACT.Copy)

                    group_steps(act, body)

                @block.vector
                def _(dve):
                    def body(g, where):
                        nxt = g + 1
                        if where is None or g.odd < GROUPS - 1:
                            dve.wait_ge(s["xT_mm"], after(nxt))
                            dve.wait_ge(s["v2_mm"], after(nxt - 2))
                            nc.vector.tensor_copy(colT[nxt.slot], psum[:, t_bank[1], :].rearrange("p (k n) -> p k n", k=KC)
                                                  ).then_inc(s["colT_copy"], 1)
                        if where is not None and where[1] > 0:
                            max_over_l(g - 1, where[0], where[1] - 1)
                        if where is None or g.odd < GROUPS - 1:
                            dve.wait_ge(s["qk_mm"], after(nxt))
                            dve.wait_ge(s["kT_copy"], after(nxt))
                            if where is None:
                                dve.wait_ge(s["diag_zero"], b + 1 + CREDIT)
                            dve.wait_ge(s["q0_copy"], after(nxt))
                            for r in range(2, R):
                                rows = slice(D * r, D * r + D)
                                ins = nc.vector.tensor_copy(q_diag[nxt.slot][rows, :, :, r, :],
                                                            psum[rows, qk_bank[0], :].rearrange("p (t l i) -> p t l i", t=2, l=4))
                            ins.then_inc(s["q1_copy"], 1)

                    def max_over_l(g, i, u):
                        dve.wait_ge(s["scores_copy"], after(g))
                        dve.wait_ge(s["maxima"], after_maxima(g - 1))
                        nc.vector.tensor_reduce(group_max, scores[:, :, bass.ds((i * 2 + u) * 4, 4)], AX_X, ALU.max
                                                ).then_inc(s["group_max"], 1)
                        dve.wait_ge(s["group_max"], after(g))
                        nc.vector.tensor_tensor(neg_max, neg_max, group_max, ALU.max).then_inc(s["maxima"], 1)

                    def after_maxima(g):
                        return g.number + 2 * b + 2 + CREDIT

                    nc.vector.memset(neg_max, float(np.finfo(np.float32).min)).then_inc(s["maxima"], 1)
                    group_steps(dve, body)
                    last = Step(b * (GROUPS // 2), GROUPS - 1)
                    max_over_l(last, 0, GROUPS - 1)
                    dve.wait_ge(s["maxima"], after_maxima(last))
                    nc.vector.tensor_scalar(neg_max, neg_max, -1.0 / float(np.sqrt(D)), None, ALU.mult
                                            ).then_inc(s["maxima"], 1)

            UNITS = "DW PW DB DW PB DB PW DB PB DB PB DB".split()
            NU = len(UNITS)
            ORDINAL = {e: [u for u, what in enumerate(UNITS) if what[0] == e] for e in "DP"}
            B_UNITS = [u for u, what in enumerate(UNITS) if what[1] == "B"]
            W_UNITS = [u for u, what in enumerate(UNITS) if what[1] == "W"]
            LAST_W = W_UNITS[-1]
            ND, NPL = len(ORDINAL["D"]), len(ORDINAL["P"])
            NDB, NPB = UNITS.count("DB"), UNITS.count("PB")
            A, V1, O, OW, X, Z = (0, 1), (2, 3), 4, 5, 6, 7
            HALF = PAIRS // 2

            def pair_steps(eng, body):
                half = b * HALF

                def straight(n):
                    body(Step(half, n), n + 1 < PAIRS, 0 <= n < PAIRS, 0 <= n - 1 < PAIRS,
                         0 <= n - 2, n)

                for n in range(-1, 2):
                    straight(n)
                with eng.Fori(0, HALF - 2) as i:
                    for u in range(2):
                        body(Step(half + i, 2 + u), True, True, True, True, i * 2 + 2 + u)
                for n in range(PAIRS - 2, PAIRS + 2):
                    straight(n)

            def after_root(n, nth=5, per=5):
                return (n.number + b - 1) * per + nth + CREDIT

            with nc.Block() as block:
                @block.sync
                def _(sp):
                    def load_pair(m, i):
                        sp.wait_ge(s["pairT_mm"], after(m - 2))
                        sp.dma_start(x_pair[m.slot], x_toks[bass.ds(b, 1), bass.ds(i, 1)].rearrange("a s p c -> p (a s c)")
                                     ).then_inc(pair_in[m.slot], 16)

                    def load_res(m, i):
                        sp.wait_ge(s["h0_ready"], after(m - 2))
                        for g in range(4):
                            sp.dma_start(x_res[m.slot][32 * g:32 * g + 32],
                                         x_grid[bass.ds(b, 1), bass.ds(i, 1), g].rearrange("a s t i c -> t i (a s c)")
                                         ).then_inc(res_in[m.slot], 16)

                    def store(m, i):
                        sp.wait_ge(s["out_ready"], after(m))
                        for g in range(4):
                            sp.dma_start(out_grid[bass.ds(b, 1), bass.ds(i, 1), g].rearrange("a s t i c -> t i (a s c)"),
                                         o_out[32 * g:32 * g + 32]).then_inc(s["out_stored"], 16)

                    half = b * HALF
                    for m in range(2):
                        load_pair(Step(half, m), m)
                    for m in range(2):
                        load_res(Step(half, m), m)
                    for m in range(2, 4):
                        load_pair(Step(half, m), m)
                    with sp.Fori(0, HALF - 2) as i:
                        for u in range(2):
                            load_pair(Step(half + i, 4 + u), i * 2 + 4 + u)
                            load_res(Step(half + i, 2 + u), i * 2 + 2 + u)
                            store(Step(half + i, u), i * 2 + u)
                    for m in range(PAIRS - 4, PAIRS):
                        if m + 2 < PAIRS:
                            load_res(Step(half, m + 2), m + 2)
                        store(Step(half, m), m)
                    sp.wait_ge(s["out_stored"], after(Step(half, PAIRS - 1), 64))
                    settle(sp, s["sp_settled"])

                @block.tensor
                def _(pe):
                    def unit(n, u):
                        if UNITS[u][0] == "D":
                            k = ORDINAL["D"].index(u)
                            pe.wait_ge(s["d_ready"], after(n, ND, k + 1))
                            src = prod_d[(n.odd * ND + k) % 2]
                        else:
                            k = ORDINAL["P"].index(u)
                            pe.wait_ge(s["p_ready"], after(n, NPL, k + 1))
                            src = prod_p[(n.odd * NPL + k) % 2]
                        if UNITS[u][1] == "W":
                            if u == W_UNITS[0]:
                                pe.wait_ge(s["v1_copy"], after(n))
                                pe.wait_ge(s["ow_copy"], after(n - 1))
                            h, part_ = divmod(W_UNITS.index(u), D // DU)
                            for dd in range(DU):
                                d = part_ * DU + dd
                                c = (h * D + d) * 2 * D
                                mm = nc.tensor.matmul(psum[2 * D * h:2 * D * (h + 1), OW, 0:N], v1_diag[:, c:c + 2 * D],
                                                      src[:, dd * N:dd * N + N], start=(d == 0), stop=(d == D - 1))
                        else:
                            if u == B_UNITS[0]:
                                pe.wait_ge(s["o_copy"], after(n - 1))
                            for jj in range(JU):
                                t, g = divmod(B_UNITS.index(u) * JU + jj, 4)
                                mm = nc.tensor.matmul(psum[32 * g:32 * g + 32, O, 0:HP * D],
                                                      pick[:, 30 - 2 * t:62 - 2 * t],
                                                      src[:, jj * HP * D:(jj + 1) * HP * D],
                                                      start=(t == 0), stop=(t == N // 4 - 1))
                        mm.then_inc(s["unit_mm"], 1)

                    def body(n, prep, units, dense, last, i):
                        nxt, prv, old = n + 1, n - 1, n - 2
                        if units:
                            unit(n, 0)
                            unit(n, 1)
                        if dense:
                            pe.wait_ge(s["o_copy"], after(prv))
                            pe.wait_ge(s["hT_copy"], after(prv - 1))
                            nc.tensor.transpose(psum[:, X, 0:P], o_sb[:, 0:P], eye)
                            nc.tensor.transpose(psum[0:HP * D - P, X, P:2 * P], o_sb[:, P:HP * D], eye).then_inc(s["oT_mm"], 1)
                        if units:
                            unit(n, 2)
                        if dense:
                            pe.wait_ge(s["oT_copy"], after(prv))
                            pe.wait_ge(s["ow_copy"], after(prv))
                            pe.wait_ge(s["relu_ready"], after(prv - 1))
                            for k in range(KC):
                                mm = nc.tensor.matmul(psum[:, Z, 0:E], oT[:, k * P:k * P + P], wo[:, k, :],
                                                      start=(k == 0), stop=(k == KC - 1))
                            mm.then_inc(s["wo_mm"], 1)
                        if units:
                            unit(n, 3)
                            unit(n, 4)
                        if last:
                            pe.wait_ge(s["relu_ready"], after(old))
                            pe.wait_ge(s["oT_copy"], after(old + 1) if dense else after(old))
                            for f in range(FC):
                                nc.tensor.matmul(psum[:, X, 0:E], reluT[:, f * P:f * P + P], w2[:, f, :],
                                                 start=(f == 0), stop=False)
                            for k in range(KC):
                                nc.tensor.matmul(psum[:, X, 0:E], hT[:, k * P:k * P + P],
                                                 ident[:, P - k * P:P - k * P + E], start=False, stop=False)
                            nc.tensor.matmul(psum[:, X, 0:E], ones_row[:, :], b2[:, :], start=False, stop=True
                                             ).then_inc(s["w2_mm"], 1)
                        if units:
                            unit(n, 5)
                        if units:
                            unit(n, 6)
                        if prep:
                            pe.wait_ge(pair_in[nxt.slot], slot_after(nxt))
                            pe.wait_ge(s["h0_ready"], after(prv))
                            for k in range(KC):
                                mm = nc.tensor.transpose(psum[:, Z, k * P:k * P + P], x_pair[nxt.slot][:, k * P:k * P + P], eye)
                            mm.then_inc(s["pairT_mm"], 1)
                        if units:
                            unit(n, 7)
                        if prep:
                            pe.wait_ge(s["probs_ready"], after(nxt))
                            pe.wait_ge(s["d_ready"], after(nxt - 2, ND))
                            pe.wait_ge(s["a_copy"], after(nxt - 2))
                            a_bank = psum[:, A[nxt.slot], :].rearrange("p (t r j) -> p t r j", t=2, r=R)
                            for r in range(R):
                                mm = nc.tensor.transpose(a_bank[:, :, r, :], probs[:, r * P:r * P + P], eye)
                            mm.then_inc(s["a_mm"], 1)
                        if units:
                            unit(n, 8)
                        if prep:
                            pe.wait_ge(s["pairT_copy"], after(nxt))
                            pe.wait_ge(s["d_first"], after(nxt - 2, NDB))
                            pe.wait_ge(s["v1_copy"], after(nxt - 2))
                            for k in range(KC):
                                mm = nc.tensor.matmul(psum[:, V1[nxt.slot], 0:E], x_pairT[:, k * P:k * P + P], wv1[:, k, :],
                                                      start=(k == 0), stop=(k == KC - 1))
                            mm.then_inc(s["v1_mm"], 1)
                        if units:
                            unit(n, 9)
                        if dense:
                            pe.wait_ge(s["hn_ready"], after(prv))
                            if last:
                                pe.wait_ge(s["on_ready"], after(old))
                            for k in range(KC):
                                mm = nc.tensor.transpose(psum[:, X, k * P:k * P + P], hn[:, k * P:k * P + P], eye)
                            mm.then_inc(s["hT_mm"], 1)
                        if units:
                            unit(n, 10)
                        if dense:
                            pe.wait_ge(s["hT_copy"], after(prv))
                            if prep:
                                pe.wait_ge(s["pairT_copy"], after(nxt))
                            for f in range(FC):
                                for k in range(KC):
                                    mm = nc.tensor.matmul(psum[:, Z, f * P:f * P + P], w1[:, k, f * P:f * P + P],
                                                          hT[:, k * P:k * P + P], start=(k == 0), stop=(k == KC - 1))
                            mm.then_inc(s["w1_mm"], 1)
                        if units:
                            unit(n, 11)

                    pair_steps(pe, body)

                @block.scalar
                def _(act):
                    def body(n, prep, units, dense, last, i):
                        nxt, prv, old = n + 1, n - 1, n - 2
                        if dense:
                            act.wait_ge(s["unit_mm"], after(prv, NU))
                            act.wait_ge(s["oT_mm"], after(prv - 1))
                            nc.scalar.activation(o_sb, psum[:, O, 0:HP * D], ACT.Copy).then_inc(s["o_copy"], 1)
                        if dense:
                            act.wait_ge(s["oT_mm"], after(prv))
                            act.wait_ge(s["wo_mm"], after(prv - 1))
                            nc.scalar.activation(oT[:, 0:P], psum[:, X, 0:P], ACT.Copy)
                            nc.scalar.activation(oT[0:HP * D - P, P:2 * P], psum[0:HP * D - P, X, P:2 * P], ACT.Copy
                                                 ).then_inc(s["oT_copy"], 1)
                        if prep:
                            act.wait_ge(s["a_mm"], after(nxt - 1))
                            for c in range(2 * R):
                                r, ii = divmod(c, 2)
                                ins = nc.scalar.activation(
                                    probs[:, c * N:c * N + N],
                                    scores_i[:, r, bass.ds((i + 1) * 2 + ii, 1), :].rearrange("p a l -> p (a l)"),
                                    ACT.Exp, bias=neg_max_i[:, r, bass.ds((i + 1) * 2 + ii, 1)], scale=1.0 / float(np.sqrt(D)),
                                    accum_out=sums[nxt.slot][:, c:c + 1])
                            ins.then_inc(s["exp_ready"], 1)
                        if units:
                            act.wait_ge(s["unit_mm"], after(n, NU, LAST_W + 1))
                            act.wait_ge(s["wo_mm"], after(n - 1))
                            for h in range(HW):
                                for ii in range(2):
                                    to = oT[HP * D - P + h * D:HP * D - P + (h + 1) * D, P:2 * P].rearrange(
                                        "p (g t i) -> p i g t", g=4, i=2)[:, ii]
                                    of = psum[(2 * h + ii) * D:(2 * h + ii + 1) * D, OW, 0:N].rearrange("p (t g) -> p g t", g=4)
                                    ins = nc.scalar.activation(to, of, ACT.Copy)
                            ins.then_inc(s["ow_copy"], 1)
                        if dense or last:
                            act.wait_ge(s["variance"], after_root(n, 1, 1))
                            nc.scalar.activation(root, variance, ACT.Sqrt).then_inc(s["root"], 1)
                        if prep:
                            act.wait_ge(s["pairT_mm"], after(nxt))
                            act.wait_ge(s["v1_mm"], after(nxt - 1))
                            nc.scalar.activation(x_pairT, psum[:, Z, 0:E], ACT.Copy).then_inc(s["pairT_copy"], 1)
                        if prep:
                            act.wait_ge(s["a_mm"], after(nxt))
                            act.wait_ge(s["p_ready"], after(nxt - 2, NPL))
                            nc.scalar.activation(a_sb[nxt.slot], psum[:, A[nxt.slot], :], ACT.Copy).then_inc(s["a_copy"], 1)
                        if prep:
                            act.wait_ge(s["v1_mm"], after(nxt))
                            act.wait_ge(s["p_ready"], after(nxt - 2, NPL))
                            act.wait_ge(s["unit_mm"], after(nxt - 1, NU, LAST_W + 1))
                            act.wait_ge(s["v1_diag_zero"], b + 1 + CREDIT)
                            nc.scalar.activation(v1_sb[nxt.slot], psum[:, V1[nxt.slot], 0:HP * D], ACT.Copy)
                            for ii in range(2):
                                rows = slice(N * ii, N * ii + N)
                                ins = nc.scalar.activation(v1_diag_hd[rows, :, ii * D::2 * D + 1][:, :, 0:D],
                                                           psum[rows, V1[nxt.slot], HP * D:E].rearrange("p (h d) -> p h d", h=HW), ACT.Copy)
                            ins.then_inc(s["v1_copy"], 1)
                        if dense:
                            act.wait_ge(s["hT_mm"], after(prv))
                            act.wait_ge(s["w2_mm"], after(prv - 1))
                            for k in range(KC):
                                ins = nc.scalar.activation(hT[:, k * P:k * P + P], psum[:, X, k * P:k * P + P], ACT.Identity,
                                                           bias=agg_b[:, k:k + 1], scale=agg_g[:, k:k + 1])
                            ins.then_inc(s["hT_copy"], 1)
                        if dense:
                            act.wait_ge(s["w1_mm"], after(prv))
                            for f in range(FC):
                                ins = nc.scalar.activation(reluT[:, f * P:f * P + P], psum[:, Z, f * P:f * P + P],
                                                           ACT.Relu, bias=b1[:, f:f + 1])
                            ins.then_inc(s["relu_ready"], 1)

                    pair_steps(act, body)

                def of_products(n, k, engine):
                    units = ORDINAL[engine]
                    buf = (prod_d if engine == "D" else prod_p)[(n.odd * len(units) + k) % 2]
                    if k >= 2:
                        return buf, after(n, NU, units[k - 2] + 1)
                    return buf, after(n - 1, NU, units[len(units) + k - 2] + 1)

                def w_factors(u, a):
                    h, part_ = divmod(W_UNITS.index(u), D // DU)
                    v2_u = v2_w[:, h * D + part_ * DU:h * D + (part_ + 1) * DU, :]
                    return v2_u, a[:, (HP + h) * N:(HP + h + 1) * N].unsqueeze(1).to_broadcast([P, DU, N])

                @block.vector
                def _(dve):
                    def unit(n, k):
                        u = ORDINAL["D"][k]
                        a = psum[:, A[n.slot], :]
                        buf, free = of_products(n, k, "D")
                        if k == 0:
                            dve.wait_ge(s["a_copy"], after(n))
                        dve.wait_ge(s["unit_mm"], free)
                        if UNITS[u] == "DW":
                            v2_u, a_u = w_factors(u, a)
                            nc.vector.tensor_tensor(buf[:, 0:DU * N].rearrange("p (d j) -> p d j", d=DU), v2_u, a_u,
                                                    ALU.mult).then_inc(s["d_ready"], 1)
                            return
                        c = B_UNITS.index(u)
                        kb = [x_ for x_ in ORDINAL["D"] if UNITS[x_] == "DB"].index(u)
                        if kb == 0:
                            dve.wait_ge(s["v1_copy"], after(n))
                        nc.vector.tensor_tensor(buf.rearrange("p (j n) -> p j n", j=JU), v2[:, c * JU:(c + 1) * JU, :],
                                                psum[:, V1[n.slot], 0:HP * D].unsqueeze(1).to_broadcast([P, JU, HP * D]),
                                                ALU.mult).then_inc(s["d_first"], 1)
                        dve.wait_ge(s["d_first"], after(n, NDB, kb + 1))
                        buf4 = buf.rearrange("p (j h d) -> p j h d", j=JU, h=HP)
                        a4 = a.rearrange("p (h j) -> p j h", h=H)[:, c * JU:(c + 1) * JU, 0:HP]
                        nc.vector.tensor_tensor(buf4, buf4, a4.unsqueeze(3).to_broadcast([P, JU, HP, D]), ALU.mult
                                                ).then_inc(s["d_ready"], 1)

                    def body(n, prep, units, dense, last, i):
                        nxt, prv, old = n + 1, n - 1, n - 2
                        if isinstance(i, int) and i == -1:
                            nc.vector.memset(small[:, 60:72], 1.0).then_inc(s["small_set"], 1)
                            dve.wait_ge(s["small_set"], b + 1 + CREDIT)
                        if units:
                            unit(n, 0)
                            unit(n, 1)
                            unit(n, 2)
                            unit(n, 3)
                        if dense:
                            dve.wait_ge(s["wo_mm"], after(prv))
                            dve.wait_ge(res_in[prv.slot], slot_after(prv, 4))
                            dve.wait_ge(s["hT_mm"], after(prv - 1))
                            nc.vector.tensor_tensor(h0, psum[:, Z, 0:E], x_res[prv.slot], ALU.add).then_inc(s["h0_ready"], 1)
                        if units:
                            unit(n, 4)
                        if last:
                            dve.wait_ge(s["w2_mm"], after(old))
                            nc.vector.bn_stats(stats2, psum[:, X, 0:E]).then_inc(s["stats2"], 1)
                        if dense:
                            dve.wait_ge(s["h0_ready"], after(prv))
                            nc.vector.bn_stats(stats1, h0).then_inc(s["stats1"], 1)
                        if last:
                            dve.wait_ge(s["stats2"], after(old))
                            settle(dve, s["settled"])
                            nc.vector.bn_aggr(mv2, stats2).then_inc(s["mean2"], 1)
                        if dense:
                            dve.wait_ge(s["stats1"], after(prv))
                            settle(dve, s["settled"])
                            nc.vector.bn_aggr(mv1, stats1).then_inc(s["mean1"], 1)
                        if dense or last:
                            if dense:
                                dve.wait_ge(s["mean1"], after(prv))
                            if last:
                                dve.wait_ge(s["mean2"], after(old))
                            nc.vector.tensor_scalar(variance, both_vars, EPS_TRI, None, ALU.add).then_inc(s["variance"], 1)
                        if prep:
                            dve.wait_ge(s["exp_ready"], after(nxt))
                            dve.wait_ge(s["probs_ready"], after(nxt - 1))
                            nc.vector.reciprocal(inv, sums[nxt.slot]).then_inc(s["inv_ready"], 1)
                            dve.wait_ge(s["inv_ready"], after(nxt))
                            nc.vector.tensor_tensor(probs.rearrange("p (c l) -> p c l", c=2 * R),
                                                    probs.rearrange("p (c l) -> p c l", c=2 * R),
                                                    inv.unsqueeze(2).to_broadcast([P, 2 * R, N]), ALU.mult
                                                    ).then_inc(s["probs_ready"], 1)
                        if units:
                            unit(n, 5)
                        if dense or last:
                            dve.wait_ge(s["root"], after_root(n, 1, 1))
                            nc.vector.reciprocal(rstd, root).then_inc(s["rstd"], 1)
                            dve.wait_ge(s["rstd"], after_root(n, 1))
                            nc.vector.tensor_tensor(tmp, rstd, rstd, ALU.mult).then_inc(s["rstd"], 1)
                            dve.wait_ge(s["rstd"], after_root(n, 2))
                            nc.vector.tensor_tensor(tmp, tmp, variance, ALU.mult).then_inc(s["rstd"], 1)
                            dve.wait_ge(s["rstd"], after_root(n, 3))
                            nc.vector.tensor_scalar(tmp, tmp, -0.5, 1.5, ALU.mult, ALU.add).then_inc(s["rstd"], 1)
                            dve.wait_ge(s["rstd"], after_root(n, 4))
                            nc.vector.tensor_tensor(rstd, rstd, tmp, ALU.mult).then_inc(s["rstd"], 1)
                            dve.wait_ge(s["rstd"], after_root(n, 5))
                        if dense:
                            nc.vector.tensor_scalar(hn, h0, mv1[:, 0:1], rstd[:, 0:1], ALU.subtract, ALU.mult
                                                    ).then_inc(s["hn_ready"], 1)
                        if last:
                            dve.wait_ge(s["scaled"], after(old - 1))
                            nc.vector.tensor_scalar(on, psum[:, X, 0:E], mv2[:, 0:1], rstd[:, 1:2], ALU.subtract, ALU.mult
                                                    ).then_inc(s["on_ready"], 1)
                        if units:
                            unit(n, 6)

                    pair_steps(dve, body)

                @block.gpsimd
                def _(pool):
                    def unit(n, k):
                        u = ORDINAL["P"][k]
                        a, v1 = a_sb[n.slot], v1_sb[n.slot]
                        buf, free = of_products(n, k, "P")
                        if k == 0:
                            pool.wait_ge(s["a_copy"], after(n))
                        pool.wait_ge(s["unit_mm"], free)
                        if UNITS[u] == "PW":
                            v2_u, a_u = w_factors(u, a)
                            nc.gpsimd.tensor_tensor(buf[:, 0:DU * N].rearrange("p (d j) -> p d j", d=DU), v2_u, a_u,
                                                    ALU.mult).then_inc(s["p_ready"], 1)
                            return
                        c = B_UNITS.index(u)
                        kb = [x_ for x_ in ORDINAL["P"] if UNITS[x_] == "PB"].index(u)
                        if kb == 0:
                            pool.wait_ge(s["v1_copy"], after(n))
                        nc.gpsimd.tensor_tensor(buf.rearrange("p (j n) -> p j n", j=JU), v2[:, c * JU:(c + 1) * JU, :],
                                                v1.unsqueeze(1).to_broadcast([P, JU, HP * D]),
                                                ALU.mult).then_inc(s["p_first"], 1)
                        pool.wait_ge(s["p_first"], after(n, NPB, kb + 1))
                        buf4 = buf.rearrange("p (j h d) -> p j h d", j=JU, h=HP)
                        a4 = a.rearrange("p (h j) -> p j h", h=H)[:, c * JU:(c + 1) * JU, 0:HP]
                        nc.gpsimd.tensor_tensor(buf4, buf4, a4.unsqueeze(3).to_broadcast([P, JU, HP, D]), ALU.mult
                                                ).then_inc(s["p_ready"], 1)

                    def body(n, prep, units, dense, last, i):
                        old = n - 2
                        if isinstance(i, int) and i == -1:
                            nc.gpsimd.memset(v1_diag, 0.0).then_inc(s["v1_diag_zero"], 1)
                        if units:
                            for k in range(NPL):
                                unit(n, k)
                        if last:
                            pool.wait_ge(s["on_ready"], after(old))
                            pool.wait_ge(s["out_stored"], after(old - 1, 64))
                            nc.gpsimd.tensor_tensor(o_out, on, out_g[:, :], ALU.mult).then_inc(s["scaled"], 1)
                            pool.wait_ge(s["scaled"], after(old))
                            nc.gpsimd.tensor_tensor(o_out, o_out, out_b[:, :], ALU.add
                                                    ).then_inc(s["out_ready"], 1)

                    pair_steps(pool, body)

        clear(nc, [weights_in, *s.values()])


def global_layer(nc, consts, x, w, xn_dram, q_dram, out):
    G = TOK // BANK
    T4 = BANK // P
    PT_SLOTS = 4
    scale = float(np.float32(E) ** np.float32(-0.5))
    with ExitStack() as ctx:
        def sb(what, shape, dtype=F32):
            return ctx.enter_context(nc.sbuf_tensor(f"global_{what}", shape, dtype))

        def sem(what):
            return ctx.enter_context(nc.semaphore(f"global_{what}"))

        psum = ctx.enter_context(nc.psum_tensor("global_psum", [P, 8, BANK], F32))
        eye = consts["ident"][:, P:2 * P]
        wq, wk, wv, wp = (sb(k, [P, KC, E]) for k in ("wq", "wk", "wv", "wp"))
        bq, bk = sb("bq", [P, KC]), sb("bk", [P, KC])
        gamma, beta, bv, bp = (sb(k, [P, E]) for k in ("gamma", "beta", "bv", "bp"))
        k_high, k_low = (sb(what, [P, KC, TOK], F32R) for what in ("k_high", "k_low"))
        v_high, v_low = (sb(what, [P, KT, E], F32R) for what in ("v_high", "v_low"))
        pT_high, pT_low = (sb(what, [P, PT_SLOTS, BANK], F32R) for what in ("pT_high", "pT_low"))
        q_high, q_low = (sb(what, [P, 2, KC, P], F32R) for what in ("q_high", "q_low"))
        work = sb("work", [P, 10816])
        at = [0]

        def part(n):
            at[0] += n
            return work[:, at[0] - n:at[0]]

        x_in = [part(T4 * E).rearrange("p (t c) -> p t c", t=T4) for _ in range(2)]
        centred = part(T4 * E).rearrange("p (t c) -> p t c", t=T4)
        xn = [part(T4 * E).rearrange("p (t c) -> p t c", t=T4) for _ in range(2)]
        xnT = part(KC * BANK).rearrange("p (k n) -> p k n", k=KC)
        qT_out = [part(KC * BANK).rearrange("p (k n) -> p k n", k=KC) for _ in range(2)]
        k_sum = part(KC * BANK).rearrange("p (k n) -> p k n", k=KC)
        v_sum = part(T4 * E).rearrange("p (t c) -> p t c", t=T4)
        stats, mv = part(T4 * 6), part(T4 * 2)
        rstd, root, tmp, variance = (part(T4) for _ in range(4))
        at[0] = 0
        rows = [part(TOK) for _ in range(2)]
        qT = [part(KC * P).rearrange("p (k n) -> p k n", k=KC) for _ in range(2)]
        xn_in = [part(E) for _ in range(2)]
        xn_bp = [part(E) for _ in range(2)]
        o_sb, oT = part(E), part(E)
        y = [part(E) for _ in range(2)]
        maxima, row_max = part(CHUNK), part(1)
        neg_max = [part(1) for _ in range(2)]
        EXPS = 4
        sums, total = [part(EXPS) for _ in range(2)], part(1)
        inv = [part(1) for _ in range(2)]

        toks = x.rearrange("b (g i) j c -> b g (i j) c", g=G)
        xn_toks = xn_dram.rearrange("b (g i) j c -> b g (i j) c", g=G)
        xn_tiles = xn_dram.rearrange("b (s i) j c -> b s (i j) c", i=2)
        out_tiles = out.rearrange("b (s i) j c -> b s (i j) c", i=2)

        weights_in = sem("weights_in")
        with nc.Block() as block:
            @block.sync
            def _(sp):
                n = 0
                for dst, src in ((wq, w["w_q"]), (wk, w["w_k"]), (wv, w["w_v"]), (wp, w["w_p"])):
                    sp.dma_start(dst[:, :, :], src.rearrange("(k p) n -> p k n", p=P)).then_inc(weights_in, 16)
                    n += 1
                for dst, src in ((bq, w["b_q"]), (bk, w["b_k"])):
                    sp.dma_start(dst[:, :], src.rearrange("(k p) -> p k", p=P), allow_slow_non_contiguous=True).then_inc(weights_in, 16)
                    n += 1
                for dst, src in ((gamma, w["ln_gamma"]), (beta, w["ln_beta"]), (bv, w["b_v"]), (bp, w["b_p"])):
                    sp.dma_start(dst[:, :], src.rearrange("(a n) -> a n", a=1).to_broadcast([P, E])).then_inc(weights_in, 16)
                    n += 1
                sp.wait_ge(weights_in, 16 * n)

        names = ("x_in0", "x_in1", "xn_out0", "xn_out1", "q_out0", "q_out1", "stats", "mean", "variance", "root", "rstd",
                 "centred", "scaled", "xn_ready", "xT_mm", "xT_copy", "qk_mm", "v_mm", "q_copy", "k_sum", "k_high", "k_low", "v_sum", "v_high", "v_low",
                 "qT_in0", "qT_in1", "res_in0", "res_in1", "res_ready", "scores_mm", "scores_copy",
                 "chunk_max", "row_max", "neg_max", "exp_ready", "total", "inv_ready", "pT_mm", "pT_high", "pT_copy", "q_high", "q_low",
                 "pv_mm", "o_ready", "oT_mm", "oT_copy", "proj_mm", "y_ready", "y_out0", "y_out1",
                 "settled", "sp_settled")
        s = {k: sem(k) for k in names}
        credit(nc, s.values())
        x_loaded, xn_stored, q_stored = ((s[k + "0"], s[k + "1"]) for k in ("x_in", "xn_out", "q_out"))
        qT_loaded, res_loaded, y_stored = ((s[k + "0"], s[k + "1"]) for k in ("qT_in", "res_in", "y_out"))

        with nc.Fori(0, B) as b:
            def group_steps(eng, body):
                half = b * (G // 2)
                body(Step(half, -1), None, True, False)
                with eng.Fori(0, G // 2 - 1) as i:
                    for u in range(2):
                        body(Step(half + i, u), i * 2 + u, True, True)
                body(Step(half, G - 2), G - 2, True, True)
                body(Step(half, G - 1), G - 1, False, True)

            with nc.Block() as block:
                @block.sync
                def _(sp):
                    def load(g, i):
                        sp.wait_ge(s["centred"], after(g - 2, T4))
                        sp.dma_start(x_in[g.slot], toks[bass.ds(b, 1), bass.ds(i, 1)].rearrange("a g (t p) c -> p (a g t) c", p=P)
                                     ).then_inc(x_loaded[g.slot], 16)

                    def store(g, i):
                        sp.wait_ge(s["xn_ready"], after(g))
                        sp.dma_start(xn_toks[bass.ds(b, 1), bass.ds(i, 1)].rearrange("a g (t p) c -> p (a g t) c", p=P),
                                     xn[g.slot]).then_inc(xn_stored[g.slot], 16)
                        sp.wait_ge(s["q_copy"], after(g, KC))
                        for k in range(KC):
                            sp.dma_start(q_dram[bass.ds(b, 1), k, :, bass.ds(i * BANK, BANK)].rearrange("a p n -> p (a n)"),
                                         qT_out[g.slot][:, k, :]).then_inc(q_stored[g.slot], 16)

                    half = b * (G // 2)
                    load(Step(half, 0), 0)
                    load(Step(half, 1), 1)
                    with sp.Fori(0, G // 2 - 1) as i:
                        for u in range(2):
                            store(Step(half + i, u), i * 2 + u)
                            load(Step(half + i, 2 + u), i * 2 + 2 + u)
                    for g in (G - 2, G - 1):
                        store(Step(half, g), g)
                    for g in (G - 2, G - 1):
                        sp.wait_ge(xn_stored[g % 2], slot_after(Step(half, g)))
                        settle(sp, s["sp_settled"])
                        sp.wait_ge(q_stored[g % 2], slot_after(Step(half, g), KC))
                    settle(sp, s["sp_settled"])

                @block.vector
                def _(dve):
                    def norm(g):
                        dve.wait_ge(x_loaded[g.slot], slot_after(g))
                        dve.wait_ge(s["centred"], after(g - 1, T4))
                        for t in range(T4):
                            ins = nc.vector.bn_stats(stats[:, 6 * t:6 * t + 6], x_in[g.slot][:, t, :])
                        ins.then_inc(s["stats"], 1)
                        dve.wait_ge(s["stats"], after(g))
                        settle(dve, s["settled"])
                        for t in range(T4):
                            ins = nc.vector.bn_aggr(mv[:, 2 * t:2 * t + 2], stats[:, 6 * t:6 * t + 6])
                        ins.then_inc(s["mean"], 1)
                        dve.wait_ge(s["mean"], after(g))
                        nc.vector.tensor_scalar(variance, mv.rearrange("p (t a) -> p t a", a=2)[:, :, 1], EPS_GLOBAL, None,
                                                ALU.add).then_inc(s["variance"], 1)
                        dve.wait_ge(s["root"], after(g))
                        inverse_root(dve, nc.vector, variance, root, rstd, tmp, s["rstd"], g)
                        dve.wait_ge(s["scaled"], after(g - 1))
                        for t in range(T4):
                            nc.vector.tensor_scalar(centred[:, t, :], x_in[g.slot][:, t, :], mv[:, 2 * t:2 * t + 1],
                                                    rstd[:, t:t + 1], ALU.subtract, ALU.mult).then_inc(s["centred"], 1)

                    def body(g, i, ahead, now):
                        if ahead:
                            norm(g + 1)
                        if now:
                            keys, tiles = bass.ds(i * BANK, BANK), bass.ds(i * T4, T4)
                            dve.wait_ge(s["v_mm"], after(g))
                            dve.wait_ge(s["v_low"], after(g - 1))
                            nc.vector.tensor_tensor(v_sum, psum[:, 6:8, :].rearrange("p a (t c) -> p (a t) c", c=E),
                                                    bv[:, :].unsqueeze(1).to_broadcast([P, T4, E]), ALU.add
                                                    ).then_inc(s["v_sum"], 1)
                            dve.wait_ge(s["k_sum"], after(g, KC))
                            high_part(nc.vector, k_high[:, :, keys], k_sum).then_inc(s["k_high"], 1)
                            dve.wait_ge(s["v_sum"], after(g))
                            high_part(nc.vector, v_high[:, tiles, :], v_sum).then_inc(s["v_high"], 1)

                    group_steps(dve, body)

                @block.gpsimd
                def _(pool):
                    def body(g, i, low):
                        pool.wait_ge(s["centred"], after(g, T4))
                        pool.wait_ge(xn_stored[(g - 2).slot], slot_after(g - 2))
                        pool.wait_ge(s["xT_mm"], after(g - 1))
                        nc.gpsimd.tensor_tensor(xn[g.slot], centred, gamma[:, :].unsqueeze(1).to_broadcast([P, T4, E]),
                                                ALU.mult).then_inc(s["scaled"], 1)
                        pool.wait_ge(s["scaled"], after(g))
                        nc.gpsimd.tensor_tensor(xn[g.slot], xn[g.slot], beta[:, :].unsqueeze(1).to_broadcast([P, T4, E]),
                                                ALU.add).then_inc(s["xn_ready"], 1)
                        if low:
                            split(g - 1, i - 1)

                    def split(g, i):
                        pool.wait_ge(s["k_high"], after(g))
                        keys, tiles = bass.ds(i * BANK, BANK), bass.ds(i * T4, T4)
                        nc.gpsimd.tensor_tensor(k_low[:, :, keys], k_sum, k_high[:, :, keys].bitcast(F32), ALU.subtract
                                                ).then_inc(s["k_low"], 1)
                        pool.wait_ge(s["v_high"], after(g))
                        nc.gpsimd.tensor_tensor(v_low[:, tiles, :], v_sum, v_high[:, tiles, :].bitcast(F32), ALU.subtract
                                                ).then_inc(s["v_low"], 1)

                    half = b * (G // 2)
                    body(Step(half, 0), 0, False)
                    body(Step(half, 1), 1, True)
                    with pool.Fori(0, G // 2 - 1) as i:
                        for u in range(2):
                            body(Step(half + i, 2 + u), i * 2 + 2 + u, True)
                    split(Step(half, G - 1), G - 1)

                @block.tensor
                def _(pe):
                    def body(g, i, ahead, now):
                        if now:
                            pe.wait_ge(s["xT_copy"], after(g, KC))
                            pe.wait_ge(s["q_copy"], after(g - 1, KC))
                            pe.wait_ge(s["k_sum"], after(g - 1, KC))
                            for wt, bank in ((wq, 2), (wk, 4)):
                                for m in range(KC):
                                    for k in range(KC):
                                        mm = nc.tensor.matmul(psum[:, bank + m, :], wt[:, k, m * P:m * P + P], xnT[:, k, :],
                                                              start=(k == 0), stop=(k == KC - 1))
                            mm.then_inc(s["qk_mm"], 1)
                        if now:
                            pe.wait_ge(s["v_sum"], after(g - 1))
                            for t in range(T4):
                                for k in range(KC):
                                    mm = nc.tensor.matmul(psum[:, 6 + t // 2, (t % 2) * E:(t % 2 + 1) * E],
                                                          xnT[:, k, t * P:t * P + P], wv[:, k, :],
                                                          start=(k == 0), stop=(k == KC - 1))
                            mm.then_inc(s["v_mm"], 1)
                        if ahead:
                            pe.wait_ge(s["xn_ready"], after(g + 1))
                            pe.wait_ge(s["xT_copy"], after(g, KC))
                            for k in range(KC):
                                for t in range(T4):
                                    mm = nc.tensor.transpose(psum[:, k, t * P:t * P + P], xn[(g + 1).slot][:, t, k * P:k * P + P], eye)
                            mm.then_inc(s["xT_mm"], 1)

                    group_steps(pe, body)

                @block.scalar
                def _(act):
                    def body(g, i, ahead, now):
                        if now:
                            act.wait_ge(s["xT_mm"], after(g))
                            act.wait_ge(s["v_mm"], after(g - 1))
                            for k in range(KC):
                                nc.scalar.activation(xnT[:, k, :], psum[:, k, :], ACT.Copy).then_inc(s["xT_copy"], 1)
                        if ahead:
                            act.wait_ge(s["variance"], after(g + 1))
                            nc.scalar.activation(root, variance, ACT.Sqrt).then_inc(s["root"], 1)
                        if now:
                            act.wait_ge(s["qk_mm"], after(g))
                            act.wait_ge(q_stored[(g - 2).slot], slot_after(g - 2, KC))
                            for k in range(KC):
                                nc.scalar.activation(qT_out[g.slot][:, k, :], psum[:, 2 + k, :], ACT.Identity,
                                                     bias=bq[:, k:k + 1]).then_inc(s["q_copy"], 1)
                            act.wait_ge(s["k_low"], after(g - 1))
                            for k in range(KC):
                                nc.scalar.activation(k_sum[:, k, :], psum[:, 4 + k, :], ACT.Identity,
                                                     bias=bk[:, k:k + 1]).then_inc(s["k_sum"], 1)

                    group_steps(act, body)

            SB, TB, O, X, Y = (0, 1), (2, 3), (4, 5), 6, 7
            ORDER = "S0 T0 S1 T1 S2 V0 T2 V1 S3 T3 V2 S4 T4 V3 S5 T5 V4 S6 T6 S7 T7 V5 V6 V7".split()
            HALF = KT // 2

            def tile_steps(eng, body):
                half = b * HALF
                body(Step(half, -1), True, False, False, -1)
                body(Step(half, 0), True, True, False, 0)
                with eng.Fori(0, HALF - 2) as i:
                    for u in range(2):
                        body(Step(half + i, 1 + u), True, True, True, i * 2 + 1 + u)
                for n in (KT - 3, KT - 2):
                    body(Step(half, n), True, True, True, n)
                body(Step(half, KT - 1), False, True, True, KT - 1)
                body(Step(half, KT), False, False, True, KT)

            with nc.Block() as block:
                @block.sync
                def _(sp):
                    def load(m, i):
                        sp.wait_ge(s["q_low"], after(m - 2))
                        sp.dma_start(qT[m.slot], q_dram[bass.ds(b, 1), :, :, bass.ds(i * P, P)].rearrange("a k p n -> p (a k) n")
                                     ).then_inc(qT_loaded[m.slot], 16)

                    def load_res(m, i):
                        sp.wait_ge(s["res_ready"], after(m - 2))
                        sp.dma_start(xn_in[m.slot], xn_tiles[bass.ds(b, 1), bass.ds(i, 1)].rearrange("a s p c -> p (a s c)")
                                     ).then_inc(res_loaded[m.slot], 16)

                    def store(m, i):
                        sp.wait_ge(s["y_ready"], after(m))
                        sp.dma_start(out_tiles[bass.ds(b, 1), bass.ds(i, 1)].rearrange("a s p c -> p (a s c)"),
                                     y[m.slot]).then_inc(y_stored[m.slot], 16)

                    half = b * HALF
                    for m in range(2):
                        load(Step(half, m), m)
                        load_res(Step(half, m), m)
                    load(Step(half, 2), 2)
                    with sp.Fori(0, HALF - 2) as i:
                        for u in range(2):
                            load(Step(half + i, 3 + u), i * 2 + 3 + u)
                            load_res(Step(half + i, 2 + u), i * 2 + 2 + u)
                            store(Step(half + i, u), i * 2 + u)
                    for m in range(KT - 4, KT):
                        if m + 3 < KT:
                            load(Step(half, m + 3), m + 3)
                        if m + 2 < KT:
                            load_res(Step(half, m + 2), m + 2)
                        store(Step(half, m), m)
                    for m in (KT - 2, KT - 1):
                        sp.wait_ge(y_stored[m % 2], slot_after(Step(half, m)))
                    settle(sp, s["sp_settled"])

                @block.tensor
                def _(pe):
                    def body(n, scores, probs, dense, i):
                        nxt, prv = n + 1, n - 1

                        def run(what, c):
                            if what == "S" and scores:
                                if c == 0:
                                    pe.wait_ge(s["q_low"], after(nxt))
                                if c >= 2:
                                    pe.wait_ge(s["scores_copy"], after(nxt, CHUNK, c - 1))
                                else:
                                    pe.wait_ge(s["scores_copy"], after(nxt - 1, CHUNK, CHUNK + c - 1))
                                keys = slice(c * BANK, (c + 1) * BANK)
                                for k in range(KC):
                                    for at_, (q_part, k_part) in enumerate(((q_high, k_high), (q_high, k_low), (q_low, k_high))):
                                        mm = nc.tensor.matmul(psum[:, SB[c % 2], :], q_part[:, nxt.slot, k, :], k_part[:, k, keys],
                                                              start=(k == 0 and at_ == 0), stop=(k == KC - 1 and at_ == 2))
                                mm.then_inc(s["scores_mm"], 1)
                            if what == "T" and probs:
                                pe.wait_ge(s["exp_ready"], after(n, EXPS, c * EXPS // CHUNK + 1))
                                if c >= 2:
                                    pe.wait_ge(s["pT_copy"], after(n, CHUNK, c - 1))
                                else:
                                    pe.wait_ge(s["pT_copy"], after(n - 1, CHUNK, CHUNK + c - 1))
                                for t in range(T4):
                                    mm = nc.tensor.transpose(psum[:, TB[c % 2], t * P:t * P + P],
                                                             rows[n.slot][:, c * BANK + t * P:c * BANK + (t + 1) * P], eye)
                                mm.then_inc(s["pT_mm"], 1)
                            if what == "V" and probs:
                                if c == 0:
                                    pe.wait_ge(s["o_ready"], after(n - 2))
                                pe.wait_ge(s["pT_copy"], after(n, CHUNK, c + 1))
                                for t in range(T4):
                                    kt = c * T4 + t
                                    for at_, (p_part, v_part) in enumerate(((pT_high, v_high), (pT_high, v_low), (pT_low, v_high))):
                                        mm = nc.tensor.matmul(psum[:, O[n.slot], 0:E],
                                                              p_part[:, c % PT_SLOTS, t * P:t * P + P], v_part[:, kt, :],
                                                              start=(kt == 0 and at_ == 0), stop=(kt == KT - 1 and at_ == 2))
                                mm.then_inc(s["pv_mm"], 1)

                        for at_, op in enumerate(ORDER):
                            run(op[0], int(op[1:]))
                            if dense and op == "T1":
                                pe.wait_ge(s["o_ready"], after(prv))
                                pe.wait_ge(s["oT_copy"], after(prv - 1))
                                for k in range(KC):
                                    mm = nc.tensor.transpose(psum[:, X, k * P:k * P + P], o_sb[:, k * P:k * P + P], eye)
                                mm.then_inc(s["oT_mm"], 1)
                            if dense and op == "T4":
                                pe.wait_ge(s["oT_copy"], after(prv))
                                pe.wait_ge(s["y_ready"], after(prv - 1))
                                for k in range(KC):
                                    mm = nc.tensor.matmul(psum[:, Y, 0:E], oT[:, k * P:k * P + P], wp[:, k, :],
                                                          start=(k == 0), stop=(k == KC - 1))
                                mm.then_inc(s["proj_mm"], 1)

                    tile_steps(pe, body)

                @block.scalar
                def _(act):
                    def body(n, scores, probs, dense, i):
                        nxt, prv = n + 1, n - 1
                        for c in range(CHUNK):
                            if scores:
                                act.wait_ge(s["scores_mm"], after(nxt, CHUNK, c + 1))
                                if c == 0:
                                    act.wait_ge(s["pT_mm"], after(nxt - 2, CHUNK))
                                nc.scalar.activation(rows[nxt.slot][:, c * BANK:(c + 1) * BANK], psum[:, SB[c % 2], :],
                                                     ACT.Copy).then_inc(s["scores_copy"], 1)
                            if dense and c == 2:
                                act.wait_ge(s["oT_mm"], after(prv))
                                act.wait_ge(s["proj_mm"], after(prv - 1))
                                nc.scalar.activation(oT, psum[:, X, 0:E], ACT.Copy).then_inc(s["oT_copy"], 1)
                        if scores:
                            act.wait_ge(s["neg_max"], after(nxt))
                            for e in range(EXPS):
                                part_ = rows[nxt.slot][:, e * (TOK // EXPS):(e + 1) * (TOK // EXPS)]
                                nc.scalar.activation(part_, part_, ACT.Exp, bias=neg_max[nxt.slot], scale=scale,
                                                     accum_out=sums[nxt.slot][:, e:e + 1]).then_inc(s["exp_ready"], 1)

                    tile_steps(act, body)

                @block.vector
                def _(dve):
                    def split_q(m):
                        dve.wait_ge(qT_loaded[m.slot], slot_after(m))
                        dve.wait_ge(s["scores_mm"], after(m - 2, CHUNK))
                        high_part(nc.vector, q_high[:, m.slot], qT[m.slot]).then_inc(s["q_high"], 1)
                        dve.wait_ge(s["q_high"], after(m))
                        nc.vector.tensor_tensor(q_low[:, m.slot], qT[m.slot], q_high[:, m.slot].bitcast(F32), ALU.subtract
                                                ).then_inc(s["q_low"], 1)

                    def body(n, scores, probs, dense, i):
                        nxt, prv = n + 1, n - 1
                        if isinstance(i, int) and i == -1:
                            split_q(n + 1)
                        if not isinstance(i, int) or i + 2 < KT:
                            split_q(n + 2)
                        if dense:
                            dve.wait_ge(s["total"], after(prv))
                            dve.wait_ge(s["pv_mm"], after(prv, CHUNK))
                            dve.wait_ge(s["oT_mm"], after(prv - 1))
                            nc.vector.tensor_scalar(o_sb, psum[:, O[prv.slot], 0:E], inv[prv.slot], None, ALU.mult
                                                    ).then_inc(s["o_ready"], 1)
                        for at_, op in enumerate(ORDER):
                            what, c = op[0], int(op[1:])
                            if what == "S" and scores:
                                dve.wait_ge(s["scores_copy"], after(nxt, CHUNK, c + 1))
                                nc.vector.tensor_reduce(maxima[:, c:c + 1], rows[nxt.slot][:, c * BANK:(c + 1) * BANK],
                                                        AX_X, ALU.max).then_inc(s["chunk_max"], 1)
                                if c == CHUNK - 1:
                                    dve.wait_ge(s["chunk_max"], after(nxt, CHUNK))
                                    nc.vector.tensor_reduce(row_max, maxima, AX_X, ALU.max).then_inc(s["row_max"], 1)
                                    dve.wait_ge(s["row_max"], after(nxt))
                                    nc.vector.tensor_scalar(neg_max[nxt.slot], row_max, -scale, None, ALU.mult
                                                            ).then_inc(s["neg_max"], 1)
                            if what == "T" and probs:
                                dve.wait_ge(s["pT_mm"], after(n, CHUNK, c + 1))
                                if c >= PT_SLOTS:
                                    dve.wait_ge(s["pv_mm"], after(n, CHUNK, c - PT_SLOTS + 1))
                                else:
                                    dve.wait_ge(s["pv_mm"], after(n - 1, CHUNK, CHUNK + c - PT_SLOTS + 1))
                                high_part(nc.vector, pT_high[:, c % PT_SLOTS, :], psum[:, TB[c % 2], :]
                                          ).then_inc(s["pT_high"], 1)
                                dve.wait_ge(s["pT_high"], after(n, CHUNK, c + 1))
                                nc.vector.tensor_tensor(pT_low[:, c % PT_SLOTS, :], psum[:, TB[c % 2], :],
                                                        pT_high[:, c % PT_SLOTS, :].bitcast(F32), ALU.subtract
                                                        ).then_inc(s["pT_copy"], 1)
                            if dense and op == "T5":
                                dve.wait_ge(s["proj_mm"], after(prv))
                                dve.wait_ge(s["res_ready"], after(prv))
                                dve.wait_ge(y_stored[(prv - 2).slot], slot_after(prv - 2))
                                nc.vector.tensor_tensor(y[prv.slot], psum[:, Y, 0:E], xn_bp[prv.slot], ALU.add
                                                        ).then_inc(s["y_ready"], 1)
                        if probs:
                            dve.wait_ge(s["exp_ready"], after(n, EXPS))
                            nc.vector.tensor_reduce(total, sums[n.slot], AX_X, ALU.add).then_inc(s["inv_ready"], 1)
                            dve.wait_ge(s["inv_ready"], after(n))
                            nc.vector.reciprocal(inv[n.slot], total).then_inc(s["total"], 1)

                    tile_steps(dve, body)

                @block.gpsimd
                def _(pool):
                    with pool.Fori(0, HALF) as i:
                        for u in range(2):
                            m = Step(b * HALF + i, u)
                            pool.wait_ge(res_loaded[m.slot], slot_after(m))
                            pool.wait_ge(s["y_ready"], after(m - 1 - u))
                            nc.gpsimd.tensor_tensor(xn_bp[m.slot], xn_in[m.slot], bp[:, :], ALU.add
                                                    ).then_inc(s["res_ready"], 1)

        clear(nc, [weights_in, *s.values()])


def conv_layer(nc, consts, x, taps, out):
    G = N // 8
    NP = N + 2
    with ExitStack() as ctx:
        def sb(what, shape):
            return ctx.enter_context(nc.sbuf_tensor(f"conv_{what}", shape, F32))

        def sem(what):
            return ctx.enter_context(nc.semaphore(f"conv_{what}"))

        psum = ctx.enter_context(nc.psum_tensor("conv_psum", [P, 8, BANK], F32))
        eye = consts["ident"][:, P:2 * P]
        tap = sb("tap", [P, KC, 9])
        image = sb("image", [P, KC, NP * NP])
        x_in = [sb(f"x_in{k}", [P, 4, E]) for k in range(2)]
        acc = [sb(f"acc{k}", [P, KC, BANK]) for k in range(2)]
        prod = [sb(f"prod{k}", [P, 2, KC, BANK]) for k in range(2)]
        tile = [sb(f"tile{k}", [P, 4, E]) for k in range(2)]
        img = image[:, :, :].rearrange("p k (r c) -> p k r c", c=NP)
        names = ("taps_in", "cleared", "x_in0", "x_in1", "xT_mm", "image_copy", "summed", "products", "back_mm", "back_copy", "out0", "out1", "sp_settled")
        s = {k: sem(k) for k in names}
        credit(nc, s.values())
        x_loaded, stored = (s["x_in0"], s["x_in1"]), (s["out0"], s["out1"])
        toks = x.rearrange("b (g i) j c -> b g (i j) c", g=G)
        out_toks = out.rearrange("b (g i) j c -> b g (i j) c", g=G)
        with nc.Block() as block:
            @block.sync
            def _(sp):
                for k in range(KC):
                    sp.dma_start(tap[:, k, :], taps.rearrange("a b (k p) -> k p (a b)", p=P)[k], allow_slow_non_contiguous=True).then_inc(s["taps_in"], 16)
                sp.wait_ge(s["taps_in"], 16 * KC + CREDIT)

            @block.gpsimd
            def _(pool):
                nc.gpsimd.memset(image[:, 0, :], 0.0).then_inc(s["cleared"], 1)

            @block.vector
            def _(dve):
                nc.vector.memset(image[:, 1, :], 0.0).then_inc(s["cleared"], 1)
                dve.wait_ge(s["cleared"], 2 + CREDIT)

        TAPS = [(dy, dx) for dy in range(3) for dx in range(3) if (dy, dx) != (1, 1)]
        PROD = TAPS[-2:]
        SUMS = TAPS[:-2]
        NS, NPR = len(SUMS) * KC, len(PROD) * KC

        with nc.Fori(0, B) as b:
            half = b * (G // 2)

            def steps(eng, body):
                for g in range(-2, 2):
                    body(Step(half, g), g, True, g >= 0)
                with eng.Fori(0, G // 2 - 2) as i:
                    for u in range(2):
                        body(Step(half + i, 2 + u), i * 2 + 2 + u, True, True)
                for g in (G - 2, G - 1):
                    body(Step(half, g), g, False, True)

            with nc.Block() as block:
                @block.sync
                def _(sp):
                    def load(g, i):
                        sp.wait_ge(s["xT_mm"], after(g - 2))
                        sp.dma_start(x_in[g.slot][:, :, :], toks[bass.ds(b, 1), bass.ds(i, 1)].rearrange("a g (t p) c -> p (a g t) c", p=P)
                                     ).then_inc(x_loaded[g.slot], 16)

                    def store(g, i):
                        sp.wait_ge(s["back_copy"], after(g))
                        sp.dma_start(out_toks[bass.ds(b, 1), bass.ds(i, 1)].rearrange("a g (t p) c -> p (a g t) c", p=P),
                                     tile[g.slot][:, :, :]).then_inc(stored[g.slot], 16)

                    for g in range(4):
                        load(Step(half, g), g)
                    with sp.Fori(0, G // 2 - 2) as i:
                        for u in range(2):
                            load(Step(half + i, 4 + u), i * 2 + 4 + u)
                            store(Step(half + i, u), i * 2 + u)
                    for g in range(G - 4, G):
                        store(Step(half, g), g)
                    for g in (G - 2, G - 1):
                        sp.wait_ge(stored[g % 2], slot_after(Step(half, g)))
                    settle(sp, s["sp_settled"])

                @block.tensor
                def _(pe):
                    def body(g, i, ahead, now):
                        nxt = g + 2
                        if ahead:
                            pe.wait_ge(x_loaded[nxt.slot], slot_after(nxt))
                            pe.wait_ge(s["image_copy"], after(nxt - 2, KC))
                            for k in range(KC):
                                for t in range(4):
                                    mm = nc.tensor.transpose(psum[:, 2 * nxt.slot + k, t * P:t * P + P],
                                                             x_in[nxt.slot][:, t, k * P:k * P + P], eye)
                            mm.then_inc(s["xT_mm"], 1)
                        if now:
                            pe.wait_ge(s["back_copy"], after(g - 2))
                            pe.wait_ge(s["products"], after(g, NPR))
                            pe.wait_ge(s["summed"], after(g, NS))
                            for t in range(4):
                                for k in range(KC):
                                    to = psum[:, 4 + 2 * g.slot + t // 2, (t % 2) * E + k * P:(t % 2) * E + k * P + P]
                                    for q in range(len(PROD)):
                                        nc.tensor.matmul(to, prod[g.slot][:, q, k, t * P:t * P + P], eye, start=(q == 0), stop=False)
                                    mm = nc.tensor.matmul(to, acc[g.slot][:, k, t * P:t * P + P], eye, start=False, stop=True)
                            mm.then_inc(s["back_mm"], 1)
                    steps(pe, body)

                def rows_in(g, i):
                    return after(g, KC) if isinstance(i, int) and i == G - 1 else after(g + 1, KC)

                @block.scalar
                def _(act):
                    def body(g, i, ahead, now):
                        if now:
                            act.wait_ge(s["image_copy"], rows_in(g, i))
                            act.wait_ge(s["back_mm"], after(g - 2))
                            for q, (dy, dx) in enumerate(PROD):
                                for k in range(KC):
                                    nc.scalar.activation(prod[g.slot][:, q, k, :].rearrange("p (r c) -> p r c", c=N),
                                                         img[:, k, bass.ds(i * 8 + dy, 8), dx:dx + N], ACT.Copy,
                                                         scale=tap[:, k, dy * 3 + dx:dy * 3 + dx + 1]).then_inc(s["products"], 1)
                        if ahead:
                            nxt = g + 2
                            act.wait_ge(s["xT_mm"], after(nxt))
                            for k in range(KC):
                                nc.scalar.activation(img[:, k, bass.ds((i + 2) * 8 + 1, 8), 1:N + 1],
                                                     psum[:, 2 * nxt.slot + k, :].rearrange("p (r c) -> p r c", c=N), ACT.Copy
                                                     ).then_inc(s["image_copy"], 1)
                        if now and (not isinstance(i, int) or i > 0):
                            send(g - 1)

                    def send(g):
                        act.wait_ge(s["back_mm"], after(g))
                        act.wait_ge(stored[g.slot], slot_after(g - 2))
                        nc.scalar.activation(tile[g.slot][:, :, :].rearrange("p t c -> p (t c)"),
                                             psum[:, 4 + 2 * g.slot:6 + 2 * g.slot, :].rearrange("p a n -> p (a n)"), ACT.Copy
                                             ).then_inc(s["back_copy"], 1)

                    steps(act, body)
                    send(Step(half, G - 1))

                @block.vector
                def _(dve):
                    def body(g, i, ahead, now):
                        if now:
                            dve.wait_ge(s["image_copy"], rows_in(g, i))
                            dve.wait_ge(s["back_mm"], after(g - 2))
                            for a, (dy, dx) in enumerate(SUMS):
                                for k in range(KC):
                                    to = acc[g.slot][:, k, :].rearrange("p (r c) -> p r c", c=N)
                                    plus = img[:, k, bass.ds(i * 8 + 1, 8), 1:N + 1] if a == 0 else to
                                    if a:
                                        dve.wait_ge(s["summed"], after(g, NS, (a - 1) * KC + k + 1))
                                    nc.vector.scalar_tensor_tensor(
                                        out=to, in0=img[:, k, bass.ds(i * 8 + dy, 8), dx:dx + N],
                                        scalar=tap[:, k, dy * 3 + dx:dy * 3 + dx + 1], in1=plus,
                                        op0=ALU.mult, op1=ALU.add).then_inc(s["summed"], 1)
                    steps(dve, body)


def conv_seq_kernel(nc, x, l0, l1, l2, taps, ident, pick, out):
    x1, x2, x3, xn = (nc.dram_tensor(k, (B, N, N, E), F32).ap() for k in ("x1", "x2", "x3", "xn"))
    q_dram = nc.dram_tensor("qT", (B, KC, P, TOK), F32).ap()
    with ExitStack() as ctx:
        consts = {k: ctx.enter_context(nc.sbuf_tensor(k, shape, F32))
                  for k, shape in (("ident", [P, 3 * P]), ("pick", [P, 62]), ("ones_row", [1, P]))}
        consts_in = ctx.enter_context(nc.semaphore("consts_in"))
        with nc.Block() as block:
            @block.sync
            def _(sp):
                sp.dma_start(consts["ident"][:, :], ident).then_inc(consts_in, 16)
                sp.dma_start(consts["pick"][:, :], pick).then_inc(consts_in, 16)
                sp.wait_ge(consts_in, 32)

            @block.vector
            def _(dve):
                nc.vector.memset(consts["ones_row"][:, :], 1.0)

        triangle_layer(nc, consts, x, l0, x1, "tri0")
        global_layer(nc, consts, x1, l1, xn, q_dram, x2)
        triangle_layer(nc, consts, x2, l2, x3, "tri2")
        conv_layer(nc, consts, x3, taps, out)


_TRI = ("Wq", "Wk", "Wv1", "Wv2", "Wo", "ln_agg_g", "ln_agg_b", "W1", "b1", "W2", "b2", "ln_out_g", "ln_out_b")
_GLOBAL = ("ln_gamma", "ln_beta", "w_q", "b_q", "w_k", "b_k", "w_v", "b_v", "w_p", "b_p")


def kernel(**inputs):
    import concourse.bacc as bacc
    from concourse.bass_utils import run_bass_kernel_spmd

    nc = bacc.Bacc("TRN2", target_bir_lowering=False, num_devices=1)
    arrays = {f"in_{k}": np.ascontiguousarray(v) for k, v in inputs.items()}
    ident = np.zeros((P, 3 * P), np.float32)
    ident[:, P:2 * P] = np.eye(P, dtype=np.float32)
    pick = np.zeros((P, 62), np.float32)
    pick[:N, 30] = 1.0
    pick[N:, 31] = 1.0
    arrays["in_ident"], arrays["in_pick"] = ident, pick
    ap = {k: nc.dram_tensor(k, a.shape, mybir.dt.from_np(a.dtype), kind="ExternalInput").ap() for k, a in arrays.items()}
    out = nc.dram_tensor("out", (B, N, N, E), F32, kind="ExternalOutput").ap()
    conv_seq_kernel(nc, ap["in_x"], {k: ap[f"in_L0_conv_{k}"] for k in _TRI}, {k: ap[f"in_L1_conv_{k}"] for k in _GLOBAL},
                    {k: ap[f"in_L2_conv_{k}"] for k in _TRI}, ap["in_L3_conv_kernel"], ap["in_ident"], ap["in_pick"], out)
    return run_bass_kernel_spmd(nc, [arrays], core_ids=[0]).results[0]["out"]
```
